# Optimizing a Trainium2 kernel written in Bass

```python
import numpy as np
import jax
import jax.numpy as jnp

def _softmax(x, axis=-1):
    return jax.nn.softmax(x, axis=axis)

def _gelu(x):
    return jax.nn.gelu(x, approximate=True)

def _silu(x):
    return jax.nn.silu(x)

def _sigmoid(x):
    return jax.nn.sigmoid(x)

def _layernorm(x, axis=-1, eps=1e-05):
    m = jnp.mean(x, axis=axis, keepdims=True)
    v = jnp.var(x, axis=axis, keepdims=True)
    return (x - m) / jnp.sqrt(v + eps)

def _scatter_add(tgt, idx, src, axis=0):
    return tgt.at[idx].add(src)

def _segment_sum(src, seg, n):
    return jax.ops.segment_sum(src, seg, n)
kernel_name = 'mk_xattn_ffn_d1_seqx_r2_eda8ad'

def setup_inputs(seed: int=0):
    np.random.seed(seed)
    _w = jnp.asarray

    def _rec_inputs():
        import jax
        import jax.numpy as jnp
        _rk = jax.random.key(seed)
        x = -0.0002928 + 1 * jax.random.normal(jax.random.fold_in(_rk, 1), (2, 2048, 512), jnp.float32)
        _lenS = 2048 - jax.random.randint(jax.random.fold_in(_rk, 7), (2,), 0, max(1, 2048 // 4) + 1, jnp.int32)
        _lenS2 = 77 - jax.random.randint(jax.random.fold_in(_rk, 8), (2,), 0, max(1, 77 // 4) + 1, jnp.int32)
        _ctx_1024P = jax.random.normal(jax.random.fold_in(_rk, 11), (2, 16, 512), jnp.float32)
        _ctx_1024c = jax.random.dirichlet(jax.random.fold_in(_rk, 511), 0.3 * jnp.ones((16,), jnp.float32), (2, 77))
        _ctx_1024t = jnp.einsum('bsk,bkd->bsd', _ctx_1024c, _ctx_1024P)
        _ctx_1024t = _ctx_1024t * jax.lax.rsqrt(jnp.mean(jnp.square(_ctx_1024t)) + 1e-12) * 0.953939
        ctx_1024 = -1.39393e-06 + 0.999914 * (_ctx_1024t + 0.3 * jax.random.normal(jax.random.fold_in(_rk, 611), (2, 77, 512), jnp.float32))
        return (x, ctx_1024)
    x, ctx_1024 = _rec_inputs()

    def _L0_xattn_setup():
        import jax, jax.numpy as jnp
        import numpy as np
        import math
        DIM = 512
        H = 16
        HD = DIM // H // 2
        DEPTH = 4
        LAMBDA_INIT = 0.8 - 0.6 * math.exp(-0.3 * DEPTH)
        SCALE = HD ** (-0.5)
        EPS = 1e-05

        def _sdpa(q, k, v):
            scores = jnp.einsum('bhqd,bhkd->bhqk', q * SCALE, k)
            p = jax.nn.softmax(scores, axis=-1)
            return jnp.einsum('bhqk,bhkd->bhqd', p, v)
        key = jax.random.key(seed)
        ks = jax.random.split(key, 12)
        B, Nq, Nk = (2, 1024, 1024)
        s = DIM ** (-0.5)
        return {'query': jax.random.normal(ks[0], (B, Nq, DIM), jnp.float32), 'key_': jax.random.normal(ks[1], (B, Nk, DIM), jnp.float32), 'value': jax.random.normal(ks[2], (B, Nk, DIM), jnp.float32), 'Wq': jax.random.normal(ks[3], (DIM, DIM), jnp.float32) * s, 'Wk': jax.random.normal(ks[4], (DIM, DIM), jnp.float32) * s, 'Wv': jax.random.normal(ks[5], (DIM, DIM), jnp.float32) * s, 'Wp': jax.random.normal(ks[6], (DIM, DIM), jnp.float32) * s, 'bp': jnp.zeros((DIM,), jnp.float32), 'lq1': jax.random.normal(ks[7], (HD,), jnp.float32) * 0.1, 'lk1': jax.random.normal(ks[8], (HD,), jnp.float32) * 0.1, 'lq2': jax.random.normal(ks[9], (HD,), jnp.float32) * 0.1, 'lk2': jax.random.normal(ks[10], (HD,), jnp.float32) * 0.1, 'subln_w': jnp.ones((2 * HD,), jnp.float32)}
    _L0_xattn_all = _L0_xattn_setup()
    _L0_xattn_in = {k: v for k, v in _L0_xattn_all.items() if k in ('Wq', 'Wk', 'Wv', 'Wp', 'bp', 'lq1', 'lk1', 'lq2', 'lk2', 'subln_w')}
    del _L0_xattn_all

    def _L0_ffn_setup():
        import jax, jax.numpy as jnp
        import numpy as np
        CAPACITY = 2
        B, S, D, E, I = (4, 2048, 512, 8, 2048)
        key = jax.random.key(seed)
        k0, k1, k2, k3, k4 = jax.random.split(key, 5)
        x = jax.random.normal(k0, (B, S, D), dtype=jnp.float32)
        gate_w = jax.random.normal(k1, (E, D), dtype=jnp.float32) * 0.006
        w_gate = jax.random.normal(k2, (E, I, D), dtype=jnp.float32) * (1.0 / np.sqrt(D))
        w_up = jax.random.normal(k3, (E, I, D), dtype=jnp.float32) * (1.0 / np.sqrt(D))
        w_down = jax.random.normal(k4, (E, D, I), dtype=jnp.float32) * (1.0 / np.sqrt(I))
        return {'x': x, 'gate_w': gate_w, 'w_gate': w_gate, 'w_up': w_up, 'w_down': w_down}
    _L0_ffn_all = _L0_ffn_setup()
    _L0_ffn_in = {k: v for k, v in _L0_ffn_all.items() if k in ('gate_w', 'w_gate', 'w_up', 'w_down')}
    del _L0_ffn_all
    return {'x': x, 'ctx_1024': ctx_1024, 'L0_xattn_Wq': _L0_xattn_in['Wq'], 'L0_xattn_Wk': _L0_xattn_in['Wk'], 'L0_xattn_Wv': _L0_xattn_in['Wv'], 'L0_xattn_Wp': _L0_xattn_in['Wp'], 'L0_xattn_bp': _L0_xattn_in['bp'], 'L0_xattn_lq1': _L0_xattn_in['lq1'], 'L0_xattn_lk1': _L0_xattn_in['lk1'], 'L0_xattn_lq2': _L0_xattn_in['lq2'], 'L0_xattn_lk2': _L0_xattn_in['lk2'], 'L0_xattn_subln_w': _L0_xattn_in['subln_w'], 'L0_ffn_gate_w': _L0_ffn_in['gate_w'], 'L0_ffn_w_gate': _L0_ffn_in['w_gate'], 'L0_ffn_w_up': _L0_ffn_in['w_up'], 'L0_ffn_w_down': _L0_ffn_in['w_down']}

def reference(x, ctx_1024, L0_xattn_Wq, L0_xattn_Wk, L0_xattn_Wv, L0_xattn_Wp, L0_xattn_bp, L0_xattn_lq1, L0_xattn_lk1, L0_xattn_lq2, L0_xattn_lk2, L0_xattn_subln_w, L0_ffn_gate_w, L0_ffn_w_gate, L0_ffn_w_up, L0_ffn_w_down):
    import jax
    import jax.numpy as jnp

    def _L0_xattn_ref(query, key_, value, Wq, Wk, Wv, Wp, bp, lq1, lk1, lq2, lk2, subln_w):
        import jax, jax.numpy as jnp
        import numpy as np
        import math
        DIM = 512
        H = 16
        HD = DIM // H // 2
        DEPTH = 4
        LAMBDA_INIT = 0.8 - 0.6 * math.exp(-0.3 * DEPTH)
        SCALE = HD ** (-0.5)
        EPS = 1e-05

        def _sdpa(q, k, v):
            scores = jnp.einsum('bhqd,bhkd->bhqk', q * SCALE, k)
            p = jax.nn.softmax(scores, axis=-1)
            return jnp.einsum('bhqk,bhkd->bhqd', p, v)
        B, Nq, C = query.shape
        Nk = key_.shape[1]
        q = (query @ Wq.T).reshape(B, Nq, 2 * H, HD).transpose(0, 2, 1, 3)
        k = (key_ @ Wk.T).reshape(B, Nk, 2 * H, HD).transpose(0, 2, 1, 3)
        v = (value @ Wv.T).reshape(B, Nk, H, 2 * HD).transpose(0, 2, 1, 3)
        q1, q2 = (q[:, :H], q[:, H:])
        k1, k2 = (k[:, :H], k[:, H:])
        a1 = _sdpa(q1, k1, v)
        a2 = _sdpa(q2, k2, v)
        lam1 = jnp.exp(jnp.sum(lq1 * lk1))
        lam2 = jnp.exp(jnp.sum(lq2 * lk2))
        lam = lam1 - lam2 + LAMBDA_INIT
        attn = a1 - lam * a2
        attn = attn.transpose(0, 2, 1, 3)
        attn = attn * jax.lax.rsqrt(jnp.mean(attn * attn, axis=-1, keepdims=True) + EPS)
        attn = attn * subln_w
        attn = attn * (1.0 - LAMBDA_INIT)
        attn = attn.reshape(B, Nq, C)
        return attn @ Wp.T + bp

    def _L0_ffn_ref(x, gate_w, w_gate, w_up, w_down):
        import jax, jax.numpy as jnp
        import numpy as np
        CAPACITY = 2
        B, S, D = x.shape
        E = gate_w.shape[0]
        k = S // E * CAPACITY
        logits = jnp.einsum('bsd,ed->bse', x, gate_w)
        affinity = jax.nn.softmax(logits, axis=-1)
        affinity = jnp.transpose(affinity, (0, 2, 1))
        gating, idx = jax.lax.top_k(affinity, k)
        bidx = jnp.arange(B)[:, None, None]
        x_in = x[bidx, idx]
        h = jax.nn.silu(jnp.einsum('bekd,eid->beki', x_in, w_gate)) * jnp.einsum('bekd,eid->beki', x_in, w_up)
        x_e = jnp.einsum('beki,edi->bekd', h, w_down)
        out = jnp.zeros_like(x).at[bidx, idx].add(gating[..., None] * x_e)
        return out
    x = x + _L0_xattn_ref(_layernorm(x, axis=-1), ctx_1024, ctx_1024, L0_xattn_Wq, L0_xattn_Wk, L0_xattn_Wv, L0_xattn_Wp, L0_xattn_bp, L0_xattn_lq1, L0_xattn_lk1, L0_xattn_lq2, L0_xattn_lk2, L0_xattn_subln_w)
    x = x + _L0_ffn_ref(_layernorm(x, axis=-1), L0_ffn_gate_w, L0_ffn_w_gate, L0_ffn_w_up, L0_ffn_w_down)
    return x

_drawn_inputs = setup_inputs


def setup_inputs(seed=0):
    import zlib

    import numpy as np

    out = dict(_drawn_inputs(seed))
    spreads = {'L0_xattn_bp': (0.0, 0.1), 'L0_xattn_subln_w': (1.0, 0.2)}
    factors = {'L0_xattn_lq1': 4.449, 'L0_xattn_lk1': 2.942, 'L0_xattn_lq2': 8.0, 'L0_xattn_lk2': 4.512}
    for name, (base, spread) in spreads.items():
        noise = np.random.default_rng([zlib.crc32(name.encode()), seed]).standard_normal(out[name].shape)
        drawn = base * np.exp(spread * noise) if base else spread * noise
        out[name] = jnp.asarray(drawn.astype(out[name].dtype))
    for name, factor in factors.items():
        out[name] = (out[name] * factor).astype(out[name].dtype)
    return out
```

```python
from contextlib import ExitStack
import math

import numpy as np

import concourse.bass as bass
from concourse import mybir
from concourse.alu_op_type import AluOpType as ALU

F32 = mybir.dt.float32
F32R = mybir.dt.float32r
F16 = mybir.dt.float16
U32 = mybir.dt.uint32
ACT = mybir.ActivationFunctionType
X = mybir.AxisListType.X

P = 128
BATCH, SEQ, DIM = 2, 2048, 512
TOKENS = BATCH * SEQ
KEYS = 77
HEADS = 16
QK_HEADS = 2 * HEADS
QK_DIM = DIM // QK_HEADS
V_DIM = DIM // HEADS
KD = DIM // P
HEADS_PER_BLOCK = P // QK_DIM
BLOCKS = QK_HEADS // HEADS_PER_BLOCK
HALF = HEADS_PER_BLOCK // 2 * KEYS
CHUNKS = -(-HEADS * KEYS // P)
WINDOW = 3
WIN = WINDOW * V_DIM
CTX_COLS = 3 * KEYS
EPS = 1e-5
LAMBDA_INIT = 0.8 - 0.6 * math.exp(-0.3 * 4)
Q_SCALE = QK_DIM ** -0.5
TILES = TOKENS // P
SUB = 4
MACROS = TILES // SUB

EXPERTS, INNER = 8, 2048
CAP = SEQ // EXPERTS * 2
SLOT_TILES = CAP // P
XT = BATCH * SLOT_TILES
GJ = 4
GROUPS = INNER // P // GJ
GU = 2 * DIM
WCOLS = 3 * DIM
ROW = DIM + EXPERTS
SET_E = 4
SETS = EXPERTS // SET_E
GROUP_P = SEQ // P
TOP_BIT = 29

BLOCK_ORDER = [0, 2, 1, 3]


def after(eng, sem, count):
    if not isinstance(count, int) or count > 0:
        eng.wait_ge(sem, count)


def hold(eng, sem, count, passed):
    eng.wait_ge(sem, count)
    eng.sem_inc(passed, 1)


def first_head(c):
    return min(P * c // KEYS, HEADS - WINDOW)


def shape_constants():
    p = np.arange(P)
    flat = P * np.arange(CHUNKS)[None, :] + p[:, None]
    h0 = np.array([first_head(c) for c in range(CHUNKS)])
    vmask = (flat[:, :, None] // KEYS == h0[None, :, None] + np.arange(WINDOW)[None, None, :])
    same = p[:, None] // GROUP_P == p[None, :] // GROUP_P
    return {
        "ident": np.eye(P, dtype=np.float32),
        "headmask": (p[:, None] // QK_DIM == np.arange(HEADS_PER_BLOCK)[None, :]).astype(np.float32),
        "vmask": vmask.astype(np.float32),
        "same_group": same.astype(np.float32),
        "before_in_group": (same & (p[:, None] < p[None, :])).astype(np.float32),
        "slot_number": (p[:, None] + P * np.arange(SLOT_TILES)[None, :]).astype(np.float32),
        "top_bit": np.full((P, SETS), 1 << TOP_BIT, np.uint32),
    }


def build(nc, io):
    with ExitStack() as whole:
        ps = whole.enter_context(nc.psum_tensor("ps", [P, 8, 512], F32))
        keep = {}
        for name, shape, dt in [("ident", [P, P], F32), ("logits", [P, EXPERTS, TILES], F32),
                                ("slot_number", [P, SLOT_TILES], F32)]:
            keep[name] = whole.enter_context(nc.sbuf_tensor(name, shape, dt))
        with ExitStack() as ctx:
            att = {}
            for name, shape, dt in [
                ("wq_hi", [P, KD, DIM], F32R), ("wq_lo", [P, KD, DIM], F32R),
                ("wp_hi", [P, KD, DIM], F32R), ("wp_lo", [P, KD, DIM], F32R),
                ("k_hi", [P, BATCH, BLOCKS, HEADS_PER_BLOCK * KEYS], F32R),
                ("k_lo", [P, BATCH, BLOCKS, HEADS_PER_BLOCK * KEYS], F32R),
                ("v_hi", [P, BATCH, CHUNKS, WIN], F32R), ("v_lo", [P, BATCH, CHUNKS, WIN], F32R),
                ("gate_w", [P, KD, EXPERTS], F32), ("bias", [P, DIM], F32),
                ("neg_lambda", [P, 1], F32),
            ]:
                att[name] = ctx.enter_context(nc.sbuf_tensor(name, shape, dt))
            prepare(nc, io, ps, keep, att)
            attend(nc, io, ps, keep, att)
        route(nc, io, ps, keep)
        experts(nc, io, ps, keep)


def prepare(nc, io, ps, keep, att):
    with ExitStack() as ctx:
        def sb(name, shape, dt=F32):
            return ctx.enter_context(nc.sbuf_tensor(name, shape, dt))

        def sem(name):
            return ctx.enter_context(nc.semaphore(name))

        wq_raw, wp_raw = sb("wq_raw", [P, KD, DIM]), sb("wp_raw", [P, KD, DIM])
        wk, wv = sb("wk", [P, KD, DIM]), sb("wv", [P, KD, DIM])
        ctx_t = sb("ctx_t", [P, KD, BATCH, CTX_COLS])
        headmask = sb("headmask", [P, HEADS_PER_BLOCK])
        vmask = sb("vmask", [P, CHUNKS, WINDOW])
        k_f32 = sb("k_f32", [P, BATCH, BLOCKS, HEADS_PER_BLOCK, KEYS])
        v_f32 = sb("v_f32", [P, BATCH, CHUNKS, WIN])
        subln = sb("subln", [P, 1])
        lam_in = sb("lam_in", [P, 4, QK_DIM])
        lam_prod = sb("lam_prod", [P, 2, QK_DIM])
        lam_dot, lam_exp, lam_diff = sb("lam_dot", [P, 2]), sb("lam_exp", [P, 2]), sb("lam_diff", [P, 1])

        small_loaded, kv_loaded, q_loaded = sem("small_loaded"), sem("kv_loaded"), sem("q_loaded")
        wp_loaded = sem("wp_loaded")
        wp_scaled, hi_done, lam_dots, lam_exps = (sem("wp_scaled"), sem("hi_done"), sem("lam_dots"),
                                                  sem("lam_exps"))
        k_done, v_done, k_masked, v_masked = sem("k_done"), sem("v_done"), sem("k_masked"), sem("v_masked")

        def chunked(a):
            return a.rearrange("(k p) n -> p k n", p=P)

        small = [(keep["ident"], io["ident"]), (headmask, io["headmask"]), (vmask, io["vmask"]),
                 (keep["slot_number"], io["slot_number"]), (subln, io["subln"]), (lam_in, io["lam_in"]),
                 (att["gate_w"], chunked(io["gate_wT"])), (att["bias"], io["bias"])]

        with nc.Block() as block:
            @block.sync
            def _(sp):
                sp.dma_start(ctx_t[:], io["ctxT"].rearrange("(k p) b n -> p k b n", p=P)).then_inc(kv_loaded, 16)
                sp.dma_start(wk[:], chunked(io["WkT"])).then_inc(kv_loaded, 16)
                sp.dma_start(wv[:], chunked(io["WvT"])).then_inc(kv_loaded, 16)
                for dst, src in small:
                    sp.dma_start(dst[:], src).then_inc(small_loaded, 16)
                sp.dma_start(wq_raw[:], chunked(io["WqT"])).then_inc(q_loaded, 16)
                sp.dma_start(wp_raw[:], chunked(io["WpT"])).then_inc(wp_loaded, 16)

            @block.tensor
            def _(pe):
                pe.wait_ge(kv_loaded, 48)
                for b in range(BATCH):
                    for hb in range(BLOCKS):
                        for k in range(KD):
                            mm = nc.tensor.matmul(ps[:, b, hb * P:hb * P + KEYS], wk[:, k, hb * P:(hb + 1) * P],
                                                  ctx_t[:, k, b, 0:KEYS], start=(k == 0), stop=(k == KD - 1))
                        mm.then_inc(k_done, 1)
                for g in range(BATCH * CHUNKS):
                    b, c = divmod(g, CHUNKS)
                    key0, h0 = P * c % KEYS, first_head(c)
                    for k in range(KD):
                        mm = nc.tensor.matmul(ps[:, 2 + g // 5, g % 5 * WIN:(g % 5 + 1) * WIN],
                                              ctx_t[:, k, b, key0:key0 + P],
                                              wv[:, k, h0 * V_DIM:h0 * V_DIM + WIN],
                                              start=(k == 0), stop=(k == KD - 1))
                    if g % 5 == 4:
                        mm.then_inc(v_done, 1)

            @block.scalar
            def _(act):
                act.wait_ge(lam_dots, 1)
                nc.scalar.activation(lam_exp[:], lam_dot[:], ACT.Exp).then_inc(lam_exps, 1)
                for n in range(BATCH * BLOCKS):
                    b, hb = divmod(n, BLOCKS)
                    act.wait_ge(k_masked, n + 1)
                    nc.scalar.activation(att["k_hi"][:, b, hb, :],
                                         k_f32[:, b, hb].rearrange("p h k -> p (h k)"),
                                         ACT.Copy).then_inc(hi_done, 1)
                act.wait_ge(v_masked, 4)
                nc.scalar.activation(att["v_hi"][:], v_f32[:], ACT.Copy).then_inc(hi_done, 1)
                act.wait_ge(q_loaded, 16)
                nc.scalar.activation(att["wq_hi"][:], wq_raw[:], ACT.Copy).then_inc(hi_done, 1)
                act.wait_ge(wp_scaled, 1)
                nc.scalar.activation(att["wp_hi"][:], wp_raw[:], ACT.Copy).then_inc(hi_done, 1)

            @block.vector
            def _(dve):
                dve.wait_ge(small_loaded, 16 * len(small))
                lam_v = lam_in[:].rearrange("p (a b) d -> p a b d", b=2)
                nc.vector.tensor_tensor(lam_prod[:], lam_v[:, :, 0, :], lam_v[:, :, 1, :], ALU.mult)
                dve.drain()
                nc.vector.tensor_reduce(lam_dot[:], lam_prod[:], X, ALU.add).then_inc(lam_dots, 1)
                for n in range(BATCH * BLOCKS):
                    b, hb = divmod(n, BLOCKS)
                    dve.wait_ge(k_done, BLOCKS * (b + 1))
                    kt = ps[:, b, hb * P:hb * P + KEYS].unsqueeze(1).to_broadcast([P, HEADS_PER_BLOCK, KEYS])
                    mask = headmask[:].unsqueeze(2).to_broadcast([P, HEADS_PER_BLOCK, KEYS])
                    nc.vector.tensor_tensor(k_f32[:, b, hb], kt, mask, ALU.mult).then_inc(k_masked, 1)
                for g in range(4):
                    b, half = divmod(g, 2)
                    c0 = half * 5
                    dve.wait_ge(v_done, g + 1)
                    vv = ps[:, 2 + g, 0:5 * WIN].rearrange("p (a d) -> p a d", d=V_DIM)
                    mask = vmask[:, c0:c0 + 5, :].rearrange("p c w -> p (c w)").unsqueeze(2).to_broadcast(
                        [P, 5 * WINDOW, V_DIM])
                    nc.vector.tensor_tensor(v_f32[:, b, c0:c0 + 5, :].rearrange("p c (w d) -> p (c w) d", d=V_DIM),
                                            vv, mask, ALU.mult).then_inc(v_masked, 1)
                dve.wait_ge(wp_loaded, 16)
                nc.vector.tensor_scalar(wp_raw[:], wp_raw[:], subln[:, 0:1], 1.0 - LAMBDA_INIT,
                                        ALU.mult, ALU.mult).then_inc(wp_scaled, 1)
                for n in range(BATCH * BLOCKS):
                    b, hb = divmod(n, BLOCKS)
                    dve.wait_ge(hi_done, n + 1)
                    nc.vector.tensor_tensor(att["k_lo"][:, b, hb, :],
                                            k_f32[:, b, hb].rearrange("p h k -> p (h k)"),
                                            att["k_hi"][:, b, hb, :].bitcast(F32), ALU.subtract)
                for n, (lo, raw, hi) in enumerate([("v_lo", v_f32, "v_hi"), ("wq_lo", wq_raw, "wq_hi"),
                                                   ("wp_lo", wp_raw, "wp_hi")]):
                    dve.wait_ge(hi_done, BATCH * BLOCKS + n + 1)
                    nc.vector.tensor_tensor(att[lo][:], raw[:], att[hi][:].bitcast(F32), ALU.subtract)
                dve.wait_ge(lam_exps, 1)
                nc.vector.tensor_tensor(lam_diff[:], lam_exp[:, 1:2], lam_exp[:, 0:1], ALU.subtract)
                dve.drain()
                nc.vector.tensor_scalar(att["neg_lambda"][:], lam_diff[:], LAMBDA_INIT, None, ALU.subtract)
                dve.drain()


TURN_BANK, PROJECT_BANK, VALUE_BANK = 4, 6, 7

FIRST, MIDDLE, LAST, TAIL = "first", "middle", "last", "tail"


def has(kind, u, lag):
    if kind == FIRST:
        return u >= lag
    if kind == TAIL:
        return lag > u
    return True


def turns(kind):
    uses = []
    for u in range(SUB):
        if u == 0 and kind != TAIL:
            uses.append(("query", 2))
        if u == SUB - 1 and kind in (FIRST, MIDDLE):
            uses += [("tokens", s) for s in range(SUB)]
        if u == 0 and kind != TAIL:
            uses.append(("query", 3))
        if has(kind, u, 1):
            uses += [("mix", u, g) for g in range(3)]
        if has(kind, u, 2):
            uses.append(("attn", u))
        if u == SUB - 1 and kind in (FIRST, MIDDLE):
            uses += [("query", 0), ("query", 1)]
    return uses


TURNS_AHEAD = SUB + 2


def turns_before(n, kind):
    if kind == FIRST:
        return TURNS_AHEAD
    if kind == TAIL:
        return TURNS_AHEAD + len(turns(FIRST)) + (MACROS - 2) * len(turns(MIDDLE)) + len(turns(LAST))
    return TURNS_AHEAD + len(turns(FIRST)) + (n - 1) * len(turns(MIDDLE))


class Turn:

    def __init__(self, n, kind):
        self.start, self.order = turns_before(n, kind), turns(kind)
        assert len(turns(MIDDLE)) % 2 == 0
        self.parity = turns_before(1, MIDDLE) % 2 if kind in (MIDDLE, LAST) else self.start % 2

    def at(self, *label):
        k = self.order.index(label)
        return self.start + k, TURN_BANK + (self.parity + k) % 2


def attend(nc, io, ps, keep, att):
    with ExitStack() as ctx:
        def sb(name, shape, dt=F32):
            return ctx.enter_context(nc.sbuf_tensor(name, shape, dt))

        def sem(name):
            return ctx.enter_context(nc.semaphore(name))

        x_in = sb("x_in", [P, SUB, DIM])
        xn = sb("xn", [P, SUB, DIM])
        stats, mean_var = sb("stats", [P, SUB, 6]), sb("mean_var", [P, SUB, 2])
        var_eps, rstd, minus_half = sb("var_eps", [P, SUB]), sb("rstd", [P, SUB]), sb("minus_half", [P, HEADS])
        xnT_hi, xnT_lo = sb("xnT_hi", [P, KD, SUB * P], F32R), sb("xnT_lo", [P, KD, SUB * P], F32R)
        q_hi, q_lo = sb("q_hi", [P, BLOCKS, SUB * P], F32R), sb("q_lo", [P, BLOCKS, SUB * P], F32R)
        neg_max, sums = sb("neg_max", [P, 2, QK_HEADS]), sb("sums", [P, 2, QK_HEADS])
        recips = sb("recips", [P, 2, QK_HEADS])
        probs = sb("probs", [P, 2, QK_HEADS, KEYS])
        mix = sb("mix", [P, CHUNKS * P])
        mixT_hi, mixT_lo = sb("mixT_hi", [P, CHUNKS, P], F32R), sb("mixT_lo", [P, CHUNKS, P], F32R)
        squares, head_ms = sb("squares", [P, DIM]), sb("head_ms", [P, HEADS])
        ms_eps, head_rms = sb("ms_eps", [P, HEADS]), sb("head_rms", [P, HEADS])
        attn = sb("attn", [P, DIM])
        attnT_hi, attnT_lo = sb("attnT_hi", [P, KD, P], F32R), sb("attnT_lo", [P, KD, P], F32R)
        x_res, x1 = sb("x_res", [P, 2, DIM]), sb("x1", [P, 2, DIM])
        stats2, mean_var2 = sb("stats2", [P, 6]), sb("mean_var2", [P, 2])
        var_eps2, rstd2 = sb("var_eps2", [P, 1]), sb("rstd2", [P, 1])
        xn2, xn2T = sb("xn2", [P, 2, DIM]), sb("xn2T", [P, KD, P])

        x_loaded, res_loaded = sem("x_loaded"), [sem("res_loaded0"), sem("res_loaded1")]
        x1_stored = [sem("x1_stored0"), sem("x1_stored1")]
        xn2_stored = [sem("xn2_stored0"), sem("xn2_stored1")]
        out_free = sem("out_free")
        ln1_stats, ln1_rstd, xn_done = sem("ln1_stats"), sem("ln1_rstd"), sem("xn_done")
        turn_done, turn_hi, turn_lo = sem("turn_done"), sem("turn_hi"), sem("turn_lo")
        scores_done, max_done, exp_done = sem("scores_done"), sem("max_done"), sem("exp_done")
        recip_done, second_scaled, mix_done = sem("recip_done"), sem("second_scaled"), sem("mix_done")
        values_done, squared, ms_done, rms_done = sem("values_done"), sem("squared"), sem("ms_done"), sem("rms_done")
        attn_done, projected, res_ready, x1_done = (sem("attn_done"), sem("projected"), sem("res_ready"),
                                                    sem("x1_done"))
        ln2_stats, ln2_rstd, xn2_done = sem("ln2_stats"), sem("ln2_rstd"), sem("xn2_done")
        xn2T_psum, xn2T_done = sem("xn2T_psum"), sem("xn2T_done")
        logits_psum, logits_done = sem("logits_psum"), sem("logits_done")
        pool_passed = sem("pool_passed")

        x_rows = io["x"].rearrange("(n s p) d -> n p s d", s=SUB, p=P)
        x_tiles = io["x"].rearrange("(t p) d -> t p d", p=P)
        out_tiles = io["out"].rearrange("(t p) d -> t p d", p=P)
        row_tiles = io["rows"].rearrange("(t p) d -> t p d", p=P)

        def plan(eng, body):
            body(0, FIRST)
            with eng.Fori(1, MACROS - 1) as n:
                body(n, MIDDLE)
            body(MACROS - 1, LAST)
            body(MACROS, TAIL)

        def split_view(bank, w=DIM):
            return ps[:, bank, 0:w].rearrange("p (k t) -> p k t", t=P)

        with nc.Block() as block:
            @block.sync
            def _(sp):
                sp.sem_inc(out_free, 2)
                sp.dma_start(x_in[:], x_rows[0]).then_inc(x_loaded, 16)

                def body(n, kind):
                    for u in range(SUB):
                        s = 4 * n + u
                        if u == 0 and kind in (FIRST, MIDDLE):
                            sp.wait_ge(xn_done, n + 1)
                            sp.dma_start(x_in[:], x_rows[n + 1]).then_inc(x_loaded, 16)
                        if has(kind, u, 1):
                            after(sp, x1_done, s - 2)
                            sp.dma_start(x_res[:, (u - 1) % 2], x_tiles[s - 1]).then_inc(
                                res_loaded[(u - 1) % 2], 16)
                        if has(kind, u, 3):
                            t, c = s - 3, (u - 3) % 2
                            sp.wait_ge(x1_done, t + 1)
                            sp.dma_start(out_tiles[t], x1[:, c]).then_inc(x1_stored[c], 16)
                            sp.wait_ge(xn2_done, t + 1)
                            sp.dma_start(row_tiles[t, :, 0:DIM], xn2[:, c]).then_inc(xn2_stored[c], 16)
                        if has(kind, u, 4):
                            done = 16 * (2 * (n - 1) + u // 2 + 1)
                            sp.wait_ge(x1_stored[u % 2], done)
                            sp.wait_ge(xn2_stored[u % 2], done)
                            sp.sem_inc(out_free, 1)
                plan(sp, body)

            @block.tensor
            def _(pe):
                def three(out, a_hi, a_lo, b_hi, b_lo, start=True, stop=True, **kw):
                    nc.tensor.matmul(out, a_hi, b_hi, start=start, stop=False, **kw)
                    nc.tensor.matmul(out, a_hi, b_lo, start=False, stop=False, **kw)
                    return nc.tensor.matmul(out, a_lo, b_hi, start=False, stop=stop, **kw)

                def turn(use, src, chunks=KD):
                    index, bank = use
                    after(pe, turn_lo, index - 1)
                    for k in range(chunks):
                        mm = nc.tensor.transpose(ps[:, bank, k * P:(k + 1) * P], src[:, k * P:(k + 1) * P],
                                                 keep["ident"][:])
                    mm.then_inc(turn_done, 1)

                def turn_tokens(n, uses):
                    pe.wait_ge(xn_done, n + 1)
                    for s in range(SUB):
                        turn(uses[s], xn[:, s, :])

                def query(i, use, tokens):
                    index, bank = use
                    pe.wait_ge(turn_lo, tokens + 1)
                    after(pe, turn_lo, index - 1)
                    hb = BLOCK_ORDER[i]
                    cols = slice(hb * P, (hb + 1) * P)
                    for k in range(KD):
                        mm = three(ps[:, bank, :], att["wq_hi"][:, k, cols], att["wq_lo"][:, k, cols],
                                   xnT_hi[:, k, :], xnT_lo[:, k, :], start=(k == 0), stop=(k == KD - 1))
                    mm.then_inc(turn_done, 1)

                def scores(n, b, u, i, start):
                    hb = BLOCK_ORDER[i]
                    if u == 0:
                        pe.wait_ge(turn_lo, start - 2 + i + 1)
                    after(pe, exp_done, 16 * n + 4 * u + i - 1)
                    q = slice(u * P, (u + 1) * P)
                    for half in range(2):
                        k = slice(half * HALF, (half + 1) * HALF)
                        mm = three(ps[:, 2 * (i % 2) + half, 0:HALF], q_hi[:, hb, q], q_lo[:, hb, q],
                                   att["k_hi"][:, b, hb, k], att["k_lo"][:, b, hb, k])
                    mm.then_inc(scores_done, 1)

                def turn_mix(t, uses):
                    pe.wait_ge(mix_done, 2 * t + 2)
                    for g in range(3):
                        turn(uses[g], mix[:, 4 * g * P:], min(4, CHUNKS - 4 * g))

                def values(t, b, use):
                    pe.wait_ge(turn_lo, use[0] + 1)
                    after(pe, attn_done, t)
                    after(pe, logits_done, t - 1)
                    for c in range(CHUNKS):
                        h0 = first_head(c)
                        mm = three(ps[:, VALUE_BANK, h0 * V_DIM:h0 * V_DIM + WIN], mixT_hi[:, c, :], mixT_lo[:, c, :],
                                   att["v_hi"][:, b, c, :], att["v_lo"][:, b, c, :], start=(c == 0),
                                   stop=(c == CHUNKS - 1), skip_group_check=True)
                    mm.then_inc(values_done, 1)

                def project(t, attn_use):
                    pe.wait_ge(turn_lo, attn_use + 1)
                    after(pe, x1_done, t)
                    for k in range(KD):
                        mm = three(ps[:, PROJECT_BANK, :], attnT_hi[:, k, :], attnT_lo[:, k, :],
                                   att["wp_hi"][:, k, :], att["wp_lo"][:, k, :], start=(k == 0), stop=(k == KD - 1))
                    mm.then_inc(projected, 1)

                def turn_router(t, c, more):
                    pe.wait_ge(xn2_done, t + 1)
                    if more:
                        pe.wait_ge(attn_done, t + 2)
                    else:
                        pe.wait_ge(logits_done, t)
                    for k in range(KD):
                        mm = nc.tensor.transpose(ps[:, VALUE_BANK, k * P:(k + 1) * P],
                                                 xn2[:, c, k * P:(k + 1) * P], keep["ident"][:])
                    mm.then_inc(xn2T_psum, 1)

                def router(t):
                    pe.wait_ge(xn2T_done, t + 1)
                    for k in range(KD):
                        mm = nc.tensor.matmul(ps[:, VALUE_BANK, 0:EXPERTS], xn2T[:, k, :], att["gate_w"][:, k, :],
                                              start=(k == 0), stop=(k == KD - 1))
                    mm.then_inc(logits_psum, 1)

                def body(n, kind, b, b_before):
                    use = Turn(n, kind)
                    own = kind != TAIL
                    ahead = kind in (FIRST, MIDDLE)
                    for u in range(SUB):
                        s = 4 * n + u
                        if own:
                            scores(n, b, u, 0, use.start)
                            if u == 0:
                                query(2, use.at("query", 2), use.start - 3)
                        if has(kind, u, 3):
                            project(s - 3, attn_use(n, kind, u))
                        if ahead and u == SUB - 1:
                            turn_tokens(n + 1, [use.at("tokens", k) for k in range(SUB)])
                        if own:
                            scores(n, b, u, 1, use.start)
                            if u == 0:
                                query(3, use.at("query", 3), use.start - 3)
                        if own:
                            scores(n, b, u, 2, use.start)
                        if has(kind, u, 1):
                            turn_mix(s - 1, [use.at("mix", u, g) for g in range(3)])
                        if has(kind, u, 2):
                            pe.wait_ge(attn_done, s - 2 + 1)
                            turn(use.at("attn", u), attn[:])
                        if has(kind, u, 3):
                            turn_router(s - 3, (u - 3) % 2, has(kind, u, 2))
                        if ahead and u == SUB - 1:
                            query(0, use.at("query", 0), use.at("tokens", SUB - 1)[0])
                        if own:
                            scores(n, b, u, 3, use.start)
                        if has(kind, u, 3):
                            router(s - 3)
                        if has(kind, u, 1):
                            values(s - 1, b if u else b_before, use.at("mix", u, 2))
                        if ahead and u == SUB - 1:
                            query(1, use.at("query", 1), use.at("tokens", SUB - 1)[0])

                def attn_use(n, kind, u):
                    if u:
                        return Turn(n, kind).at("attn", u - 1)[0]
                    return Turn(n, kind).start - (3 if kind in (FIRST, MIDDLE, LAST) else 1)

                mid = MACROS // BATCH
                turn_tokens(0, [(k, TURN_BANK + k % 2) for k in range(SUB)])
                query(0, (SUB, TURN_BANK + SUB % 2), SUB - 1)
                query(1, (SUB + 1, TURN_BANK + (SUB + 1) % 2), SUB - 1)
                body(0, FIRST, 0, 0)
                with pe.Fori(1, mid) as n:
                    body(n, MIDDLE, 0, 0)
                body(mid, MIDDLE, 1, 0)
                with pe.Fori(mid + 1, MACROS - 1) as n:
                    body(n, MIDDLE, 1, 1)
                body(MACROS - 1, LAST, 1, 1)
                body(MACROS, TAIL, 1, 1)

            @block.scalar
            def _(act):
                def hi_part(dst, src, use, scale=1.0):
                    act.wait_ge(turn_done, use[0] + 1)
                    nc.scalar.activation(dst, src, ACT.Copy, scale=scale).then_inc(turn_hi, 1)

                def tokens_hi(uses):
                    for s in range(SUB):
                        hi_part(xnT_hi[:, :, s * P:(s + 1) * P], split_view(uses[s][1]), uses[s])

                def query_hi(i, use):
                    hi_part(q_hi[:, BLOCK_ORDER[i], :], ps[:, use[1], :], use, Q_SCALE)

                def exponentials(s, c, i):
                    hb = BLOCK_ORDER[i]
                    act.wait_ge(max_done, 4 * s + i + 1)
                    after(act, mix_done, 2 * (s - 2) + i // 2 + 1)
                    for h in range(HEADS_PER_BLOCK):
                        head = hb * HEADS_PER_BLOCK + h
                        e = nc.scalar.activation(probs[:, c, head, :],
                                                 ps[:, 2 * (i % 2) + h // 4, h % 4 * KEYS:(h % 4 + 1) * KEYS],
                                                 ACT.Exp, bias=neg_max[:, c, head:head + 1],
                                                 accum_out=sums[:, c, head:head + 1])
                    e.then_inc(exp_done, 1)

                def mix_hi(uses):
                    for g in range(3):
                        c = slice(4 * g, min(4 * g + 4, CHUNKS))
                        hi_part(mixT_hi[:, c, :], split_view(uses[g][1], (c.stop - c.start) * P), uses[g])

                def body(n, kind):
                    use = Turn(n, kind)
                    own = kind != TAIL
                    ahead = kind in (FIRST, MIDDLE)
                    for u in range(SUB):
                        s = 4 * n + u
                        if has(kind, u, 1):
                            exponentials(s - 1, (u - 1) % 2, 3)
                        if has(kind, u, 2):
                            act.wait_ge(values_done, s - 2 + 1)
                            nc.scalar.activation(squares[:], ps[:, VALUE_BANK, :], ACT.Square).then_inc(squared, 1)
                        if own and u == 0:
                            query_hi(2, use.at("query", 2))
                        if ahead and u == SUB - 1:
                            tokens_hi([use.at("tokens", k) for k in range(SUB)])
                        if own:
                            exponentials(s, u % 2, 0)
                            if u == 0:
                                query_hi(3, use.at("query", 3))
                        if own:
                            exponentials(s, u % 2, 1)
                        if has(kind, u, 1):
                            mix_hi([use.at("mix", u, g) for g in range(3)])
                        if has(kind, u, 2):
                            hi_part(attnT_hi[:], split_view(use.at("attn", u)[1]), use.at("attn", u))
                        if has(kind, u, 3):
                            act.wait_ge(xn2T_psum, s - 3 + 1)
                            nc.scalar.activation(xn2T[:], split_view(VALUE_BANK), ACT.Copy).then_inc(xn2T_done, 1)
                        if own:
                            exponentials(s, u % 2, 2)
                        if ahead and u == SUB - 1:
                            query_hi(0, use.at("query", 0))
                        if has(kind, u, 3):
                            act.wait_ge(logits_psum, s - 3 + 1)
                            nc.scalar.activation(keep["logits"][:, :, bass.ds(s - 3, 1)].rearrange("p e t -> p (e t)"),
                                                 ps[:, VALUE_BANK, 0:EXPERTS], ACT.Copy).then_inc(logits_done, 1)
                        if ahead and u == SUB - 1:
                            query_hi(1, use.at("query", 1))

                tokens_hi([(k, TURN_BANK + k % 2) for k in range(SUB)])
                query_hi(0, (SUB, TURN_BANK + SUB % 2))
                query_hi(1, (SUB + 1, TURN_BANK + (SUB + 1) % 2))
                plan(act, body)

            @block.vector
            def _(dve):
                def lo_part(dst, src, hi, use):
                    dve.wait_ge(turn_hi, use[0] + 1)
                    nc.vector.tensor_tensor(dst, src, hi.bitcast(F32), ALU.subtract).then_inc(turn_lo, 1)

                def layer_norm(n):
                    dve.wait_ge(x_loaded, 16 * (n + 1))
                    for s in range(SUB):
                        nc.vector.bn_stats(stats[:, s, :], x_in[:, s, :])
                    dve.drain()
                    for s in range(SUB):
                        a = nc.vector.bn_aggr(mean_var[:, s, :], stats[:, s, :])
                    a.then_inc(ln1_stats, 1)

                def normalise(n):
                    dve.wait_ge(ln1_rstd, n + 1)
                    for s in range(SUB):
                        a = nc.vector.tensor_scalar(xn[:, s, :], x_in[:, s, :], mean_var[:, s, 0:1],
                                                    rstd[:, s:s + 1], ALU.subtract, ALU.mult)
                    a.then_inc(xn_done, 1)

                def tokens_lo(uses):
                    for s in range(SUB):
                        cols = slice(s * P, (s + 1) * P)
                        lo_part(xnT_lo[:, :, cols], split_view(uses[s][1]), xnT_hi[:, :, cols], uses[s])

                def query_lo(i, use):
                    hb = BLOCK_ORDER[i]
                    dve.wait_ge(turn_hi, use[0] + 1)
                    nc.vector.scalar_tensor_tensor(q_lo[:, hb, :], ps[:, use[1], :], Q_SCALE,
                                                   q_hi[:, hb, :].bitcast(F32), ALU.mult,
                                                   ALU.subtract).then_inc(turn_lo, 1)

                def maxima(s, c, i):
                    hb = BLOCK_ORDER[i]
                    dve.wait_ge(scores_done, 4 * s + i + 1)
                    heads = slice(hb * HEADS_PER_BLOCK, (hb + 1) * HEADS_PER_BLOCK)
                    nc.vector.tensor_reduce(
                        neg_max[:, c, heads].rearrange("p (a h) -> p a h", a=2),
                        ps[:, 2 * (i % 2):2 * (i % 2) + 2, 0:HALF].rearrange("p a (h k) -> p a h k", k=KEYS),
                        X, ALU.max, negate=True).then_inc(max_done, 1)

                def mix_half(s, c, half, turned):
                    dve.wait_ge(exp_done, 4 * s + 2 * half + 2)
                    first = slice(half * 8, half * 8 + 8)
                    second = slice(HEADS + half * 8, HEADS + half * 8 + 8)
                    heads = [ap[:, c, :].rearrange("p (a h) -> p a h", a=2)[:, :, half * 8:half * 8 + 8]
                             for ap in (recips, sums)]
                    nc.vector.reciprocal(*heads)
                    dve.drain()
                    nc.vector.tensor_scalar(recips[:, c, second], recips[:, c, second],
                                            att["neg_lambda"][:, 0:1], None, ALU.mult).then_inc(recip_done, 1)
                    nc.vector.tensor_tensor(probs[:, c, first, :], probs[:, c, first, :],
                                            recips[:, c, first].unsqueeze(2).to_broadcast([P, 8, KEYS]), ALU.mult)
                    dve.drain()
                    dve.wait_ge(second_scaled, 2 * s + half + 1)
                    after(dve, turn_done, turned)
                    nc.vector.tensor_tensor(
                        mix[:, half * 8 * KEYS:(half + 1) * 8 * KEYS].rearrange("p (h k) -> p h k", k=KEYS),
                        probs[:, c, first, :], probs[:, c, second, :], ALU.add).then_inc(mix_done, 1)

                def mix_lo(uses):
                    for g in range(3):
                        c = slice(4 * g, min(4 * g + 4, CHUNKS))
                        lo_part(mixT_lo[:, c, :], split_view(uses[g][1], (c.stop - c.start) * P),
                                mixT_hi[:, c, :], uses[g])

                def mean_square(t):
                    dve.wait_ge(squared, t + 1)
                    nc.vector.tensor_reduce(head_ms[:], squares[:].rearrange("p (h d) -> p h d", d=V_DIM),
                                            X, ALU.add).then_inc(ms_done, 1)

                def head_norm(t):
                    dve.wait_ge(rms_done, t + 1)
                    nc.vector.tensor_tensor(attn[:].rearrange("p (h d) -> p h d", d=V_DIM),
                                            ps[:, VALUE_BANK, :].rearrange("p (h d) -> p h d", d=V_DIM),
                                            head_rms[:].unsqueeze(2).to_broadcast([P, HEADS, V_DIM]),
                                            ALU.mult).then_inc(attn_done, 1)

                def residual(t, c):
                    dve.wait_ge(projected, t + 1)
                    dve.wait_ge(res_ready, t + 1)
                    dve.wait_ge(out_free, t + 1)
                    nc.vector.tensor_tensor(x1[:, c], ps[:, PROJECT_BANK, :], x_res[:, c], ALU.add)
                    dve.drain()
                    nc.vector.bn_stats(stats2[:], x1[:, c]).then_inc(x1_done, 1)
                    dve.drain()
                    nc.vector.bn_aggr(mean_var2[:], stats2[:]).then_inc(ln2_stats, 1)

                def normalise2(t, c):
                    dve.wait_ge(ln2_rstd, t + 1)
                    nc.vector.tensor_scalar(xn2[:, c], x1[:, c], mean_var2[:, 0:1], rstd2[:, 0:1],
                                            ALU.subtract, ALU.mult).then_inc(xn2_done, 1)

                def body(n, kind):
                    use = Turn(n, kind)
                    own = kind != TAIL
                    ahead = kind in (FIRST, MIDDLE)
                    for u in range(SUB):
                        s = 4 * n + u
                        turned = (0 if not has(kind, u, 2) else
                                  use.at("mix", u - 1, 2)[0] + 1 if u else
                                  use.start - (3 if kind != TAIL else 1))
                        if own:
                            maxima(s, u % 2, 0)
                        if has(kind, u, 2):
                            mean_square(s - 2)
                        if own and u == 0:
                            query_lo(2, use.at("query", 2))
                        if has(kind, u, 1):
                            mix_half(s - 1, (u - 1) % 2, 0, turned)
                        if ahead and u == SUB - 1:
                            tokens_lo([use.at("tokens", k) for k in range(SUB)])
                        if own:
                            maxima(s, u % 2, 1)
                            if u == 0:
                                query_lo(3, use.at("query", 3))
                        if has(kind, u, 2):
                            head_norm(s - 2)
                        if has(kind, u, 3):
                            residual(s - 3, (u - 3) % 2)
                        if has(kind, u, 1):
                            mix_half(s - 1, (u - 1) % 2, 1, turned)
                        if has(kind, u, 3):
                            normalise2(s - 3, (u - 3) % 2)
                        if own:
                            maxima(s, u % 2, 2)
                        if has(kind, u, 1):
                            mix_lo([use.at("mix", u, g) for g in range(3)])
                        if has(kind, u, 2):
                            lo_part(attnT_lo[:], split_view(use.at("attn", u)[1]), attnT_hi[:], use.at("attn", u))
                        if own:
                            maxima(s, u % 2, 3)
                        if ahead and u == 1:
                            layer_norm(n + 1)
                        if ahead and u == 2:
                            normalise(n + 1)
                        if ahead and u == SUB - 1:
                            query_lo(0, use.at("query", 0))
                            query_lo(1, use.at("query", 1))

                nc.vector.memset(mix[:, HEADS * KEYS:], 0.0)
                layer_norm(0)
                normalise(0)
                tokens_lo([(k, TURN_BANK + k % 2) for k in range(SUB)])
                query_lo(0, (SUB, TURN_BANK + SUB % 2))
                query_lo(1, (SUB + 1, TURN_BANK + (SUB + 1) % 2))
                plan(dve, body)

            @block.gpsimd
            def _(pool):
                def power(dst, src, w):
                    pool.drain()
                    return nc.gpsimd.tensor_tensor(dst, src, minus_half[:, 0:w], ALU.pow)

                def ln1(n):
                    hold(pool, ln1_stats, n + 1, pool_passed)
                    nc.gpsimd.tensor_scalar(var_eps[:], mean_var[:, :, 1], EPS, None, ALU.add)
                    power(rstd[:], var_eps[:], SUB).then_inc(ln1_rstd, 1)

                def scale_second(s, c, half):
                    second = slice(HEADS + half * 8, HEADS + half * 8 + 8)
                    pool.wait_ge(recip_done, 2 * s + half + 1)
                    nc.gpsimd.tensor_tensor(probs[:, c, second, :], probs[:, c, second, :],
                                            recips[:, c, second].unsqueeze(2).to_broadcast([P, 8, KEYS]),
                                            ALU.mult).then_inc(second_scaled, 1)

                def add_bias(n, u):
                    c = u % 2
                    loads = 2 * n + (u - 2) // 2 + 1
                    pool.wait_ge(res_loaded[c], 16 * loads)
                    nc.gpsimd.tensor_tensor(x_res[:, c], x_res[:, c], att["bias"][:], ALU.add).then_inc(res_ready, 1)

                def body(n, kind):
                    for u in range(SUB):
                        s = 4 * n + u
                        if has(kind, u, 1):
                            scale_second(s - 1, (u - 1) % 2, 0)
                        if has(kind, u, 2):
                            hold(pool, ms_done, s - 2 + 1, pool_passed)
                            nc.gpsimd.tensor_scalar(ms_eps[:], head_ms[:], 1.0 / V_DIM, EPS, ALU.mult, ALU.add)
                            power(head_rms[:], ms_eps[:], HEADS).then_inc(rms_done, 1)
                            add_bias(n, u)
                        if has(kind, u, 3):
                            hold(pool, ln2_stats, s - 3 + 1, pool_passed)
                            nc.gpsimd.tensor_scalar(var_eps2[:], mean_var2[:, 1:2], EPS, None, ALU.add)
                            power(rstd2[:], var_eps2[:], 1).then_inc(ln2_rstd, 1)
                        if has(kind, u, 1):
                            scale_second(s - 1, (u - 1) % 2, 1)
                        if kind in (FIRST, MIDDLE) and u == 1:
                            ln1(n + 1)

                nc.gpsimd.memset(minus_half[:], -0.5)
                ln1(0)
                plan(pool, body)


def route(nc, io, ps, keep):
    with ExitStack() as ctx:
        def sb(name, shape, dt=F32):
            return ctx.enter_context(nc.sbuf_tensor(name, shape, dt))

        def sem(name):
            return ctx.enter_context(nc.semaphore(name))

        same_group, before_in_group = sb("same_group", [P, P]), sb("before_in_group", [P, P])
        top = sb("top", [P, TILES])
        shifted = sb("shifted", [P, EXPERTS, TILES])
        expo = sb("expo", [P, EXPERTS, TILES])
        total, inverse = sb("total", [P, TILES]), sb("inverse", [P, TILES])
        affinity = sb("affinity", [P, EXPERTS, TILES])
        by_token = sb("by_token", [P, TILES, EXPERTS])
        aff = sb("aff", [P, SETS, P])
        bit, cut, trial = sb("bit", [P, SETS], U32), sb("cut", [P, SETS], U32), sb("trial", [P, SETS], U32)
        enough = sb("enough", [P, SETS], U32)
        flags = sb("flags", [P, SETS, P])
        count = sb("count", [P, SETS])
        above, equal = sb("above", [P, SETS, P]), sb("equal", [P, SETS, P])
        counts = sb("counts", [P, 2, SETS])
        wanted, equal_before = sb("wanted", [P, SETS]), sb("equal_before", [P, SETS])
        ones = sb("ones", [P, P])
        rank, kept, chosen = sb("rank", [P, SETS, P]), sb("kept", [P, SETS, P]), sb("chosen", [P, SETS, P])
        running = sb("running", [P, SETS, P])
        chosen_before = sb("chosen_before", [P, SETS])
        prefix = sb("prefix", [P, SETS, P], F16)

        loaded, exp_ready, exp_done = sem("consts_loaded"), sem("exp_ready"), sem("expo_done")
        aff_done, aff_turned = sem("aff_done"), sem("aff_turned")
        counted, summed, totals_ready, totals_done = (sem("counted"), sem("summed"), sem("totals_ready"),
                                                      sem("totals_done"))
        by_token_done, chosen_counted, chosen_summed = (sem("by_token_done"), sem("chosen_counted"),
                                                        sem("chosen_summed"))
        prefix_done, stored = sem("prefix_done"), sem("stored")

        with nc.Block() as block:
            @block.sync
            def _(sp):
                sp.dma_start(same_group[:], io["same_group"]).then_inc(loaded, 16)
                sp.dma_start(before_in_group[:], io["before_in_group"]).then_inc(loaded, 16)
                sp.dma_start(bit[:], io["top_bit"]).then_inc(loaded, 16)
                sp.wait_ge(by_token_done, 1)
                sp.dma_start(io["rows"].rearrange("(t p) c -> p t c", p=P)[:, :, DIM:ROW],
                             by_token[:]).then_inc(stored, 16)
                sp.wait_ge(prefix_done, 1)
                sp.dma_start(io["prefix"].rearrange("(s q) t -> q s t", s=SETS), prefix[:]).then_inc(stored, 16)
                sp.wait_ge(stored, 32)

            @block.scalar
            def _(act):
                act.wait_ge(exp_ready, 1)
                nc.scalar.activation(expo[:], shifted[:], ACT.Exp).then_inc(exp_done, 1)

            @block.tensor
            def _(pe):
                pe.wait_ge(aff_done, 1)
                for s in range(SETS):
                    mm = nc.tensor.transpose(ps[:, 0, s * P:(s + 1) * P],
                                             affinity[:, s * SET_E:(s + 1) * SET_E, :].rearrange("p e t -> p (e t)"),
                                             keep["ident"][:])
                mm.then_inc(aff_turned, 1)
                pe.wait_ge(loaded, 48)
                with pe.Fori(0, TOP_BIT + 1) as i:
                    pe.wait_ge(counted, i + 1)
                    nc.tensor.matmul(ps[:, 1, 0:SETS], same_group[:], count[:]).then_inc(summed, 1)
                pe.wait_ge(totals_ready, 1)
                nc.tensor.matmul(ps[:, 2, 0:SETS], same_group[:], counts[:, 0, :])
                nc.tensor.matmul(ps[:, 3, 0:SETS], before_in_group[:], counts[:, 1, :]).then_inc(totals_done, 1)
                pe.wait_ge(chosen_counted, 1)
                nc.tensor.matmul(ps[:, 4, 0:SETS], before_in_group[:], running[:, :, P - 1]).then_inc(
                    chosen_summed, 1)

            @block.vector
            def _(dve):
                nc.vector.memset(ones[:], 1.0)
                nc.vector.memset(cut[:], 0)
                wide = [P, EXPERTS, TILES]
                nc.vector.tensor_reduce(top[:], keep["logits"][:].rearrange("p e t -> p t e"), X, ALU.max)
                dve.drain()
                nc.vector.tensor_tensor(shifted[:], keep["logits"][:], top[:].unsqueeze(1).to_broadcast(wide),
                                        ALU.subtract).then_inc(exp_ready, 1)
                dve.wait_ge(exp_done, 1)
                nc.vector.tensor_reduce(total[:], expo[:].rearrange("p e t -> p t e"), X, ALU.add)
                dve.drain()
                nc.vector.reciprocal(inverse[:], total[:])
                dve.drain()
                nc.vector.tensor_tensor(affinity[:], expo[:], inverse[:].unsqueeze(1).to_broadcast(wide),
                                        ALU.mult).then_inc(aff_done, 1)
                dve.drain()
                nc.vector.tensor_copy(by_token[:], affinity[:].rearrange("p e t -> p t e")).then_inc(by_token_done, 1)
                dve.wait_ge(aff_turned, 1)
                nc.vector.tensor_copy(aff[:].rearrange("p s t -> p (s t)"), ps[:, 0, 0:SETS * P])
                dve.wait_ge(loaded, 48)
                dve.drain()
                with dve.Fori(0, TOP_BIT + 1) as i:
                    nc.vector.tensor_tensor(trial[:], cut[:], bit[:], ALU.bitwise_or)
                    dve.drain()
                    for s in range(SETS):
                        c = nc.vector.tensor_scalar(flags[:, s, :], aff[:, s, :], trial[:, s:s + 1].bitcast(F32),
                                                    0.0, ALU.is_ge, ALU.add, accum_out=count[:, s:s + 1])
                    c.then_inc(counted, 1)
                    nc.vector.tensor_single_scalar(bit[:], bit[:], 1, ALU.logical_shift_right)
                    dve.wait_ge(summed, i + 1)
                    nc.vector.tensor_scalar(enough[:], ps[:, 1, 0:SETS], float(CAP), None, ALU.is_ge)
                    dve.drain()
                    nc.vector.copy_predicated(cut[:], enough[:], trial[:])
                    dve.drain()
                for s in range(SETS):
                    level = cut[:, s:s + 1].bitcast(F32)
                    nc.vector.tensor_scalar(above[:, s, :], aff[:, s, :], level, 0.0, ALU.is_gt, ALU.add,
                                            accum_out=counts[:, 0, s:s + 1])
                    c = nc.vector.tensor_scalar(equal[:, s, :], aff[:, s, :], level, 0.0, ALU.is_equal, ALU.add,
                                                accum_out=counts[:, 1, s:s + 1])
                c.then_inc(totals_ready, 1)
                dve.wait_ge(totals_done, 1)
                nc.vector.tensor_scalar(wanted[:], ps[:, 2, 0:SETS], -1.0, float(CAP), ALU.mult, ALU.add)
                nc.vector.tensor_copy(equal_before[:], ps[:, 3, 0:SETS])
                dve.drain()
                for s in range(SETS):
                    nc.vector.tensor_tensor_scan(rank[:, s, :], ones[:], equal[:, s, :], equal_before[:, s:s + 1],
                                                 ALU.mult, ALU.add)
                dve.drain()
                for s in range(SETS):
                    nc.vector.scalar_tensor_tensor(kept[:, s, :], rank[:, s, :], wanted[:, s:s + 1],
                                                   equal[:, s, :], ALU.is_le, ALU.mult)
                dve.drain()
                nc.vector.tensor_tensor(chosen[:], kept[:], above[:], ALU.add)
                dve.drain()
                for s in range(SETS):
                    c = nc.vector.tensor_tensor_scan(running[:, s, :], ones[:], chosen[:, s, :], 0.0,
                                                     ALU.mult, ALU.add)
                c.then_inc(chosen_counted, 1)
                dve.wait_ge(chosen_summed, 1)
                nc.vector.tensor_copy(chosen_before[:], ps[:, 4, 0:SETS])
                dve.drain()
                for s in range(SETS):
                    c = nc.vector.tensor_scalar(prefix[:, s, :], running[:, s, :], chosen_before[:, s:s + 1],
                                                None, ALU.add)
                c.then_inc(prefix_done, 1)


DOWN_BANK = 4
DOWN_USES = XT + GROUPS * XT


def experts(nc, io, ps, keep):
    with ExitStack() as ctx:
        def sb(name, shape, dt=F32):
            return ctx.enter_context(nc.sbuf_tensor(name, shape, dt))

        def sem(name):
            return ctx.enter_context(nc.semaphore(name))

        raw = sb("raw", [P, GJ, WCOLS])
        gu_hi, gu_lo = sb("gu_hi", [P, GJ, 2, KD, P], F32R), sb("gu_lo", [P, GJ, 2, KD, P], F32R)
        down_hi, down_lo = sb("down_hi", [P, GJ, DIM], F32R), sb("down_lo", [P, GJ, DIM], F32R)
        act_out = sb("act_out", [P, 2, CAP])
        h_hi, h_lo = sb("h_hi", [P, BATCH, GJ, CAP], F32R), sb("h_lo", [P, BATCH, GJ, CAP], F32R)
        gathered = sb("gathered", [P, XT, ROW])
        xT_hi, xT_lo = sb("xT_hi", [P, KD, BATCH * CAP], F32R), sb("xT_lo", [P, KD, BATCH * CAP], F32R)
        y = sb("y", [P, XT, DIM])
        gates = sb("gates", [P, XT])
        prefix = sb("prefix_rows", [P, BATCH, SEQ], F16)
        flags = sb("slot_flags", [P, SEQ], F16)
        found = sb("found", [P, XT])
        take, put = sb("take", [P, XT], U32), sb("put", [P, XT], U32)

        raw_loaded = [sem(f"raw_loaded{j}") for j in range(GJ)]
        gu_hi_done, gu_lo_done, gu_used = sem("gu_hi_done"), sem("gu_lo_done"), sem("gu_used")
        down_hi_done, down_lo_done, down_used = sem("down_hi_done"), sem("down_lo_done"), sem("down_used")
        pair_done, silu_done, h_done, h_hi_done, h_lo_done = (sem("pair_done"), sem("silu_done"), sem("h_done"),
                                                              sem("h_hi_done"), sem("h_lo_done"))
        h_used = sem("h_used")
        bank_done, x_hi_done, bank_free = sem("bank_done"), sem("x_hi_done"), sem("bank_free")
        prefix_loaded, listed, gates_read = sem("prefix_loaded"), sem("listed"), sem("gates_read")
        tokens_gathered = [sem(f"tokens_gathered{t}") for t in range(XT)]
        y_ready, put_ready = sem("y_ready"), sem("put_ready")
        added = [sem(f"added{t}") for t in range(XT)]
        added_all = sem("added_all")
        pool_passed = sem("pool_passed")

        w = io["weights"]
        out_rows, rows = io["out"], io["rows"]

        def prefix_rows(e):
            return io["prefix"].rearrange("(e q) t -> e (q t)", e=EXPERTS)[bass.ds(e, 1), :]

        def plan(eng, body):
            body(0, True, False)
            with eng.Fori(1, EXPERTS - 1) as e:
                body(e, False, False)
            body(EXPERTS - 1, False, True)

        def groups(eng, group):
            group(0)
            with eng.Fori(1, GROUPS) as g:
                group(g)

        with nc.Block() as block:
            @block.sync
            def _(sp):
                def body(e, first, last):
                    if not last:
                        sp.wait_ge(listed, GROUPS * (e + 1))
                        sp.dma_start(prefix[:].rearrange("p b t -> p (b t)"),
                                     prefix_rows(e + 1).to_broadcast([P, BATCH * SEQ])).then_inc(prefix_loaded, 16)

                    def group(g):
                        n = GROUPS * e + g
                        for j in range(GJ):
                            after(sp, down_lo_done, GJ * (n - 1) + j + 1)
                            sp.dma_start(raw[:, j, :], w[n, j]).then_inc(raw_loaded[j], 16)
                    groups(sp, group)

                sp.dma_start(prefix[:].rearrange("p b t -> p (b t)"),
                             prefix_rows(0).to_broadcast([P, BATCH * SEQ])).then_inc(prefix_loaded, 16)
                plan(sp, body)

            @block.tensor
            def _(pe):
                def three(out, a_hi, a_lo, b_hi, b_lo, start, stop):
                    nc.tensor.matmul(out, a_hi, b_hi, start=start, stop=False)
                    nc.tensor.matmul(out, a_hi, b_lo, start=False, stop=False)
                    return nc.tensor.matmul(out, a_lo, b_hi, start=False, stop=stop)

                def body(e, first, last):
                    uses = DOWN_USES * e
                    for t in range(XT):
                        pe.wait_ge(tokens_gathered[t], 16 * (e + 1))
                        after(pe, bank_free, uses + t - 3)
                        for k in range(KD):
                            mm = nc.tensor.transpose(ps[:, DOWN_BANK + t % 4, k * P:(k + 1) * P],
                                                     gathered[:, t, k * P:(k + 1) * P], keep["ident"][:])
                        mm.then_inc(bank_done, 1)

                    def group(g):
                        n = GROUPS * e + g
                        for b in range(BATCH):
                            after_x = uses + SLOT_TILES * (b + 1)
                            if isinstance(g, int):
                                pe.wait_ge(bank_free, after_x)
                            for j in range(GJ):
                                pair = XT * n + GJ * b + j
                                if b == 0:
                                    pe.wait_ge(gu_lo_done, GJ * n + j + 1)
                                after(pe, silu_free, pair - 1)
                                for m in range(2):
                                    for k in range(KD):
                                        cols = slice(b * CAP, (b + 1) * CAP)
                                        mm = three(ps[:, 2 * (j % 2) + m, :], gu_hi[:, j, m, k, :],
                                                   gu_lo[:, j, m, k, :], xT_hi[:, k, cols], xT_lo[:, k, cols],
                                                   k == 0, k == KD - 1)
                                mm.then_inc(pair_done, 1)
                        for b in range(BATCH):
                            pe.wait_ge(h_lo_done, XT * n + GJ * (b + 1))
                            if b == 0:
                                pe.wait_ge(down_lo_done, GJ * (n + 1))
                            for t in range(SLOT_TILES):
                                use = uses + XT + XT * g + SLOT_TILES * b + t
                                pe.wait_ge(bank_free, use - 3)
                                cols = slice(t * P, (t + 1) * P)
                                for j in range(GJ):
                                    mm = three(ps[:, DOWN_BANK + t, :], h_hi[:, b, j, cols], h_lo[:, b, j, cols],
                                               down_hi[:, j, :], down_lo[:, j, :], j == 0, j == GJ - 1)
                                mm.then_inc(bank_done, 1)
                    groups(pe, group)

                silu_free = h_done
                plan(pe, body)

            @block.scalar
            def _(act):
                def body(e, first, last):
                    uses = DOWN_USES * e
                    for t in range(XT):
                        act.wait_ge(bank_done, uses + t + 1)
                        nc.scalar.activation(xT_hi[:, :, t * P:(t + 1) * P],
                                             ps[:, DOWN_BANK + t % 4, :].rearrange("p (k t) -> p k t", t=P),
                                             ACT.Copy).then_inc(x_hi_done, 1)

                    def group(g):
                        n = GROUPS * e + g
                        for j in range(GJ):
                            act.wait_ge(raw_loaded[j], 16 * (n + 1))
                            after(act, pair_done, XT * (n - 1) + GJ + j + 1)
                            nc.scalar.activation(gu_hi[:, j].rearrange("p m k i -> p (m k i)"), raw[:, j, 0:GU],
                                                 ACT.Copy).then_inc(gu_hi_done, 1)
                        for b in range(BATCH):
                            after(act, bank_done, uses + XT * (g + 1) - XT + SLOT_TILES * (b + 1)
                                  if not (isinstance(g, int)) else uses - XT + SLOT_TILES * (b + 1))
                            for j in range(GJ):
                                pair = XT * n + GJ * b + j
                                act.wait_ge(pair_done, pair + 1)
                                after(act, h_lo_done, pair - 1)
                                nc.scalar.activation(act_out[:, j % 2, :], ps[:, 2 * (j % 2), :],
                                                     ACT.Silu).then_inc(silu_done, 1)
                                act.wait_ge(h_done, pair + 1)
                                nc.scalar.activation(h_hi[:, b, j, :], act_out[:, j % 2, :],
                                                     ACT.Copy).then_inc(h_hi_done, 1)
                                if b == 0:
                                    if j == 0:
                                        after(act, bank_done, down_uses_before(uses, g))
                                    nc.scalar.activation(down_hi[:, j, :], raw[:, j, GU:WCOLS],
                                                         ACT.Copy).then_inc(down_hi_done, 1)
                    groups(act, group)
                plan(act, body)

            @block.vector
            def _(dve):
                def list_tokens(i, g):
                    nc.vector.tensor_scalar(flags[:], prefix[:, i, :], keep["slot_number"][:, bass.ds(g, 1)],
                                            0.0, ALU.is_le, ALU.add,
                                            accum_out=found[:, bass.ds(SLOT_TILES * i + g, 1)])
                    dve.drain()

                def list_group(e, g):
                    if isinstance(g, int):
                        dve.wait_ge(prefix_loaded, 16 * (e + 1))
                    for i in range(BATCH):
                        list_tokens(i, g)
                    for i in range(BATCH):
                        col = bass.ds(SLOT_TILES * i + g, 1)
                        a = nc.vector.tensor_scalar(take[:, col], found[:, col], float(SEQ * i), None, ALU.add)
                    a.then_inc(listed, 1)

                def body(e, first, last):
                    uses = DOWN_USES * e
                    for t in range(XT):
                        cols = slice(t * P, (t + 1) * P)
                        dve.wait_ge(x_hi_done, XT * e + t + 1)
                        nc.vector.tensor_tensor(xT_lo[:, :, cols],
                                                ps[:, DOWN_BANK + t % 4, :].rearrange("p (k t) -> p k t", t=P),
                                                xT_hi[:, :, cols].bitcast(F32),
                                                ALU.subtract).then_inc(bank_free, 1)
                    for t in range(XT):
                        dve.wait_ge(tokens_gathered[t], 16 * (e + 1))
                    nc.vector.tensor_copy(gates[:], gathered[:, :, bass.ds(e + DIM, 1)].rearrange(
                        "p t c -> p (t c)")).then_inc(gates_read, 1)

                    def group(g):
                        n = GROUPS * e + g
                        for b in range(BATCH):
                            for j in range(GJ):
                                pair = XT * n + GJ * b + j
                                dve.wait_ge(silu_done, pair + 1)
                                nc.vector.tensor_tensor(act_out[:, j % 2, :], act_out[:, j % 2, :],
                                                        ps[:, 2 * (j % 2) + 1, :], ALU.mult).then_inc(h_done, 1)
                                dve.wait_ge(h_hi_done, pair + 1)
                                nc.vector.tensor_tensor(h_lo[:, b, j, :], act_out[:, j % 2, :],
                                                        h_hi[:, b, j, :].bitcast(F32),
                                                        ALU.subtract).then_inc(h_lo_done, 1)
                        if isinstance(g, int):
                            if not first:
                                dve.wait_ge(added_all, e)
                            nc.vector.tensor_copy(put[:], take[:]).then_inc(put_ready, 1)
                            dve.drain()
                        if not last:
                            list_group(e + 1, g)
                        for t in range(XT):
                            dve.wait_ge(bank_done, uses + XT + XT * g + t + 1)
                            bank = ps[:, DOWN_BANK + t % 4, :]
                            if isinstance(g, int):
                                a = nc.vector.tensor_copy(y[:, t, :], bank)
                            else:
                                a = nc.vector.tensor_tensor(y[:, t, :], y[:, t, :], bank, ALU.add)
                            a.then_inc(bank_free, 1)
                    groups(dve, group)
                    dve.drain()
                    for t in range(XT):
                        nc.vector.tensor_scalar(y[:, t, :], y[:, t, :], gates[:, t:t + 1], None,
                                                ALU.mult).then_inc(y_ready, 1)

                list_group(0, 0)
                for g in range(1, GROUPS):
                    for i in range(BATCH):
                        list_tokens(i, g)
                    for i in range(BATCH):
                        col = bass.ds(SLOT_TILES * i + g, 1)
                        a = nc.vector.tensor_scalar(take[:, col], found[:, col], float(SEQ * i), None, ALU.add)
                    a.then_inc(listed, 1)
                plan(dve, body)

            @block.gpsimd
            def _(pool):
                def gather(e):
                    hold(pool, listed, GROUPS * (e + 1), pool_passed)
                    for t in range(XT):
                        pool.indirect_dma_start(gathered[:, t, :], None, rows,
                                                bass.IndirectOffsetOnAxis(take[:, t:t + 1], 0)).then_inc(
                            tokens_gathered[t], 16)

                def body(e, first, last):
                    def group(g):
                        n = GROUPS * e + g
                        for j in range(GJ):
                            pool.wait_ge(gu_hi_done, GJ * n + j + 1)
                            nc.gpsimd.tensor_tensor(gu_lo[:, j].rearrange("p m k i -> p (m k i)"), raw[:, j, 0:GU],
                                                    gu_hi[:, j].rearrange("p m k i -> p (m k i)").bitcast(F32),
                                                    ALU.subtract).then_inc(gu_lo_done, 1)
                        if isinstance(g, int) and not first:
                            for t in range(XT):
                                pool.wait_ge(added[t], 16 * e)
                            pool.sem_inc(added_all, 1)
                        for j in range(GJ):
                            pool.wait_ge(down_hi_done, GJ * n + j + 1)
                            nc.gpsimd.tensor_tensor(down_lo[:, j, :], raw[:, j, GU:WCOLS],
                                                    down_hi[:, j, :].bitcast(F32),
                                                    ALU.subtract).then_inc(down_lo_done, 1)
                    groups(pool, group)
                    if not last:
                        pool.wait_ge(gates_read, e + 1)
                        pool.wait_ge(x_hi_done, XT * (e + 1))
                        gather(e + 1)
                    pool.wait_ge(put_ready, e + 1)
                    for t in range(XT):
                        hold(pool, y_ready, XT * e + t + 1, pool_passed)
                        pool.indirect_dma_start(out_rows, bass.IndirectOffsetOnAxis(put[:, t:t + 1], 0), y[:, t, :],
                                                None, compute_op=ALU.add).then_inc(added[t], 16)

                gather(0)
                plan(pool, body)
                for t in range(XT):
                    pool.wait_ge(added[t], 16 * EXPERTS)


def down_uses_before(uses, g):
    return uses if isinstance(g, int) else uses + XT * (g + 1)


def kernel(**inputs):
    import concourse.bacc as bacc
    from concourse.bass_utils import run_bass_kernel_spmd as run

    a = {name: np.asarray(value) for name, value in inputs.items()}

    def on_all(v):
        return np.ascontiguousarray(np.broadcast_to(v, (P,) + v.shape))

    ctx_t = a["ctx_1024"].transpose(2, 0, 1)
    lam = np.stack([a["L0_xattn_" + n] for n in ("lq1", "lk1", "lq2", "lk2")])
    gu = [a["L0_ffn_" + n].reshape(EXPERTS, INNER // P, P, KD, P).transpose(0, 1, 4, 3, 2).reshape(
        EXPERTS, INNER // P, P, DIM) for n in ("w_gate", "w_up")]
    down = a["L0_ffn_w_down"].transpose(0, 2, 1).reshape(EXPERTS, INNER // P, P, DIM)
    weights = np.concatenate(gu + [down], axis=-1).reshape(EXPERTS * GROUPS, GJ, P, WCOLS)
    arrays = {
        "x": a["x"].reshape(TOKENS, DIM),
        "ctxT": np.concatenate([ctx_t] * 3, axis=-1),
        "WqT": a["L0_xattn_Wq"].T, "WkT": a["L0_xattn_Wk"].T, "WvT": a["L0_xattn_Wv"].T,
        "WpT": a["L0_xattn_Wp"].T,
        "bias": on_all(a["L0_xattn_bp"]),
        "lam_in": on_all(lam),
        "subln": np.concatenate([a["L0_xattn_subln_w"]] * (P // V_DIM)).reshape(P, 1),
        "gate_wT": a["L0_ffn_gate_w"].T,
        "weights": weights,
        **shape_constants(),
    }
    arrays = {name: np.ascontiguousarray(v) for name, v in arrays.items()}
    feeds = {"in_" + name: v for name, v in arrays.items()}
    nc = bacc.Bacc("TRN2", target_bir_lowering=False, num_devices=1)
    io = {name: nc.dram_tensor("in_" + name, v.shape, mybir.dt.from_np(v.dtype), kind="ExternalInput").ap()
          for name, v in arrays.items()}
    io["out"] = nc.dram_tensor("out_x", (TOKENS, DIM), F32, kind="ExternalOutput").ap()
    io["rows"] = nc.dram_tensor("token_rows", (TOKENS, ROW), F32).ap()
    io["prefix"] = nc.dram_tensor("chosen_counts", (SETS * P, P), F16).ap()
    build(nc, io)
    got = run(nc, [feeds], core_ids=[0]).results[0]["out_x"]
    return got.reshape(BATCH, SEQ, DIM)
```

```python
from contextlib import ExitStack
import math

import numpy as np

import concourse.bass as bass
from concourse import mybir
from concourse.alu_op_type import AluOpType as ALU

F32 = mybir.dt.float32
F32R = mybir.dt.float32r
F16 = mybir.dt.float16
U32 = mybir.dt.uint32
ACT = mybir.ActivationFunctionType
X = mybir.AxisListType.X

P = 128
BATCH, SEQ, DIM = 2, 2048, 512
TOKENS = BATCH * SEQ
KEYS = 77
HEADS = 16
QK_HEADS = 2 * HEADS
QK_DIM = DIM // QK_HEADS
V_DIM = DIM // HEADS
KD = DIM // P
HEADS_PER_BLOCK = P // QK_DIM
BLOCKS = QK_HEADS // HEADS_PER_BLOCK
HALF = HEADS_PER_BLOCK // 2 * KEYS
CHUNKS = -(-HEADS * KEYS // P)
WINDOW = 3
WIN = WINDOW * V_DIM
CTX_COLS = 3 * KEYS
EPS = 1e-5
LAMBDA_INIT = 0.8 - 0.6 * math.exp(-0.3 * 4)
Q_SCALE = QK_DIM ** -0.5
TILES = TOKENS // P
SUB = 4
MACROS = TILES // SUB

EXPERTS, INNER = 8, 2048
CAP = SEQ // EXPERTS * 2
SLOT_TILES = CAP // P
XT = BATCH * SLOT_TILES
GJ = 4
GROUPS = INNER // P // GJ
GU = 2 * DIM
WCOLS = 3 * DIM
ROW = DIM + EXPERTS
SET_E = 4
SETS = EXPERTS // SET_E
GROUP_P = SEQ // P
TOP_BIT = 29

BLOCK_ORDER = [0, 2, 1, 3]


def after(eng, sem, count):
    if not isinstance(count, int) or count > 0:
        eng.wait_ge(sem, count)


def hold(eng, sem, count, passed):
    eng.wait_ge(sem, count)
    eng.sem_inc(passed, 1)


def first_head(c):
    return min(P * c // KEYS, HEADS - WINDOW)


def shape_constants():
    p = np.arange(P)
    flat = P * np.arange(CHUNKS)[None, :] + p[:, None]
    h0 = np.array([first_head(c) for c in range(CHUNKS)])
    vmask = (flat[:, :, None] // KEYS == h0[None, :, None] + np.arange(WINDOW)[None, None, :])
    same = p[:, None] // GROUP_P == p[None, :] // GROUP_P
    return {
        "ident": np.eye(P, dtype=np.float32),
        "headmask": (p[:, None] // QK_DIM == np.arange(HEADS_PER_BLOCK)[None, :]).astype(np.float32),
        "vmask": vmask.astype(np.float32),
        "same_group": same.astype(np.float32),
        "before_in_group": (same & (p[:, None] < p[None, :])).astype(np.float32),
        "slot_number": (p[:, None] + P * np.arange(SLOT_TILES)[None, :]).astype(np.float32),
        "top_bit": np.full((P, SETS), 1 << TOP_BIT, np.uint32),
    }


def build(nc, io):
    with ExitStack() as whole:
        ps = whole.enter_context(nc.psum_tensor("ps", [P, 8, 512], F32))
        keep = {}
        for name, shape, dt in [("ident", [P, P], F32), ("logits", [P, EXPERTS, TILES], F32),
                                ("slot_number", [P, SLOT_TILES], F32)]:
            keep[name] = whole.enter_context(nc.sbuf_tensor(name, shape, dt))
        with ExitStack() as ctx:
            att = {}
            for name, shape, dt in [
                ("wq_hi", [P, KD, DIM], F32R), ("wq_lo", [P, KD, DIM], F32R),
                ("wp_hi", [P, KD, DIM], F32R), ("wp_lo", [P, KD, DIM], F32R),
                ("k_hi", [P, BATCH, BLOCKS, HEADS_PER_BLOCK * KEYS], F32R),
                ("k_lo", [P, BATCH, BLOCKS, HEADS_PER_BLOCK * KEYS], F32R),
                ("v_hi", [P, BATCH, CHUNKS, WIN], F32R), ("v_lo", [P, BATCH, CHUNKS, WIN], F32R),
                ("gate_w", [P, KD, EXPERTS], F32), ("bias", [P, DIM], F32),
                ("neg_lambda", [P, 1], F32),
            ]:
                att[name] = ctx.enter_context(nc.sbuf_tensor(name, shape, dt))
            prepare(nc, io, ps, keep, att)
            attend(nc, io, ps, keep, att)
        route(nc, io, ps, keep)
        experts(nc, io, ps, keep)


def prepare(nc, io, ps, keep, att):
    with ExitStack() as ctx:
        def sb(name, shape, dt=F32):
            return ctx.enter_context(nc.sbuf_tensor(name, shape, dt))

        def sem(name):
            return ctx.enter_context(nc.semaphore(name))

        wq_raw, wp_raw = sb("wq_raw", [P, KD, DIM]), sb("wp_raw", [P, KD, DIM])
        wk, wv = sb("wk", [P, KD, DIM]), sb("wv", [P, KD, DIM])
        ctx_t = sb("ctx_t", [P, KD, BATCH, CTX_COLS])
        headmask = sb("headmask", [P, HEADS_PER_BLOCK])
        vmask = sb("vmask", [P, CHUNKS, WINDOW])
        k_f32 = sb("k_f32", [P, BATCH, BLOCKS, HEADS_PER_BLOCK, KEYS])
        v_f32 = sb("v_f32", [P, BATCH, CHUNKS, WIN])
        subln = sb("subln", [P, 1])
        lam_in = sb("lam_in", [P, 4, QK_DIM])
        lam_prod = sb("lam_prod", [P, 2, QK_DIM])
        lam_dot, lam_exp, lam_diff = sb("lam_dot", [P, 2]), sb("lam_exp", [P, 2]), sb("lam_diff", [P, 1])

        small_loaded, kv_loaded, q_loaded = sem("small_loaded"), sem("kv_loaded"), sem("q_loaded")
        wp_loaded = sem("wp_loaded")
        wp_scaled, hi_done, lam_dots, lam_exps = (sem("wp_scaled"), sem("hi_done"), sem("lam_dots"),
                                                  sem("lam_exps"))
        k_done, v_done, k_masked, v_masked = sem("k_done"), sem("v_done"), sem("k_masked"), sem("v_masked")

        def chunked(a):
            return a.rearrange("(k p) n -> p k n", p=P)

        small = [(keep["ident"], io["ident"]), (headmask, io["headmask"]), (vmask, io["vmask"]),
                 (keep["slot_number"], io["slot_number"]), (subln, io["subln"]), (lam_in, io["lam_in"]),
                 (att["gate_w"], chunked(io["gate_wT"])), (att["bias"], io["bias"])]

        with nc.Block() as block:
            @block.sync
            def _(sp):
                sp.dma_start(ctx_t[:], io["ctxT"].rearrange("(k p) b n -> p k b n", p=P)).then_inc(kv_loaded, 16)
                sp.dma_start(wk[:], chunked(io["WkT"])).then_inc(kv_loaded, 16)
                sp.dma_start(wv[:], chunked(io["WvT"])).then_inc(kv_loaded, 16)
                for dst, src in small:
                    sp.dma_start(dst[:], src).then_inc(small_loaded, 16)
                sp.dma_start(wq_raw[:], chunked(io["WqT"])).then_inc(q_loaded, 16)
                sp.dma_start(wp_raw[:], chunked(io["WpT"])).then_inc(wp_loaded, 16)

            @block.tensor
            def _(pe):
                pe.wait_ge(kv_loaded, 48)
                for b in range(BATCH):
                    for hb in range(BLOCKS):
                        for k in range(KD):
                            mm = nc.tensor.matmul(ps[:, b, hb * P:hb * P + KEYS], wk[:, k, hb * P:(hb + 1) * P],
                                                  ctx_t[:, k, b, 0:KEYS], start=(k == 0), stop=(k == KD - 1))
                        mm.then_inc(k_done, 1)
                for g in range(BATCH * CHUNKS):
                    b, c = divmod(g, CHUNKS)
                    key0, h0 = P * c % KEYS, first_head(c)
                    for k in range(KD):
                        mm = nc.tensor.matmul(ps[:, 2 + g // 5, g % 5 * WIN:(g % 5 + 1) * WIN],
                                              ctx_t[:, k, b, key0:key0 + P],
                                              wv[:, k, h0 * V_DIM:h0 * V_DIM + WIN],
                                              start=(k == 0), stop=(k == KD - 1))
                    if g % 5 == 4:
                        mm.then_inc(v_done, 1)

            @block.scalar
            def _(act):
                act.wait_ge(lam_dots, 1)
                nc.scalar.activation(lam_exp[:], lam_dot[:], ACT.Exp).then_inc(lam_exps, 1)
                for n in range(BATCH * BLOCKS):
                    b, hb = divmod(n, BLOCKS)
                    act.wait_ge(k_masked, n + 1)
                    nc.scalar.activation(att["k_hi"][:, b, hb, :],
                                         k_f32[:, b, hb].rearrange("p h k -> p (h k)"),
                                         ACT.Copy).then_inc(hi_done, 1)
                act.wait_ge(v_masked, 4)
                nc.scalar.activation(att["v_hi"][:], v_f32[:], ACT.Copy).then_inc(hi_done, 1)
                act.wait_ge(q_loaded, 16)
                nc.scalar.activation(att["wq_hi"][:], wq_raw[:], ACT.Copy).then_inc(hi_done, 1)
                act.wait_ge(wp_scaled, 1)
                nc.scalar.activation(att["wp_hi"][:], wp_raw[:], ACT.Copy).then_inc(hi_done, 1)

            @block.vector
            def _(dve):
                dve.wait_ge(small_loaded, 16 * len(small))
                lam_v = lam_in[:].rearrange("p (a b) d -> p a b d", b=2)
                nc.vector.tensor_tensor(lam_prod[:], lam_v[:, :, 0, :], lam_v[:, :, 1, :], ALU.mult)
                dve.drain()
                nc.vector.tensor_reduce(lam_dot[:], lam_prod[:], X, ALU.add).then_inc(lam_dots, 1)
                for n in range(BATCH * BLOCKS):
                    b, hb = divmod(n, BLOCKS)
                    dve.wait_ge(k_done, BLOCKS * (b + 1))
                    kt = ps[:, b, hb * P:hb * P + KEYS].unsqueeze(1).to_broadcast([P, HEADS_PER_BLOCK, KEYS])
                    mask = headmask[:].unsqueeze(2).to_broadcast([P, HEADS_PER_BLOCK, KEYS])
                    nc.vector.tensor_tensor(k_f32[:, b, hb], kt, mask, ALU.mult).then_inc(k_masked, 1)
                for g in range(4):
                    b, half = divmod(g, 2)
                    c0 = half * 5
                    dve.wait_ge(v_done, g + 1)
                    vv = ps[:, 2 + g, 0:5 * WIN].rearrange("p (a d) -> p a d", d=V_DIM)
                    mask = vmask[:, c0:c0 + 5, :].rearrange("p c w -> p (c w)").unsqueeze(2).to_broadcast(
                        [P, 5 * WINDOW, V_DIM])
                    nc.vector.tensor_tensor(v_f32[:, b, c0:c0 + 5, :].rearrange("p c (w d) -> p (c w) d", d=V_DIM),
                                            vv, mask, ALU.mult).then_inc(v_masked, 1)
                dve.wait_ge(wp_loaded, 16)
                nc.vector.tensor_scalar(wp_raw[:], wp_raw[:], subln[:, 0:1], 1.0 - LAMBDA_INIT,
                                        ALU.mult, ALU.mult).then_inc(wp_scaled, 1)
                for n in range(BATCH * BLOCKS):
                    b, hb = divmod(n, BLOCKS)
                    dve.wait_ge(hi_done, n + 1)
                    nc.vector.tensor_tensor(att["k_lo"][:, b, hb, :],
                                            k_f32[:, b, hb].rearrange("p h k -> p (h k)"),
                                            att["k_hi"][:, b, hb, :].bitcast(F32), ALU.subtract)
                for n, (lo, raw, hi) in enumerate([("v_lo", v_f32, "v_hi"), ("wq_lo", wq_raw, "wq_hi"),
                                                   ("wp_lo", wp_raw, "wp_hi")]):
                    dve.wait_ge(hi_done, BATCH * BLOCKS + n + 1)
                    nc.vector.tensor_tensor(att[lo][:], raw[:], att[hi][:].bitcast(F32), ALU.subtract)
                dve.wait_ge(lam_exps, 1)
                nc.vector.tensor_tensor(lam_diff[:], lam_exp[:, 1:2], lam_exp[:, 0:1], ALU.subtract)
                dve.drain()
                nc.vector.tensor_scalar(att["neg_lambda"][:], lam_diff[:], LAMBDA_INIT, None, ALU.subtract)
                dve.drain()


TURN_BANK, PROJECT_BANK, VALUE_BANK = 4, 6, 7

FIRST, MIDDLE, LAST, TAIL = "first", "middle", "last", "tail"


def has(kind, u, lag):
    if kind == FIRST:
        return u >= lag
    if kind == TAIL:
        return lag > u
    return True


def turns(kind):
    uses = []
    for u in range(SUB):
        if has(kind, u, 2):
            uses.append(("mix", u, 2))
        if u == 0 and kind != TAIL:
            uses.append(("query", 3))
        if has(kind, u, 3):
            uses.append(("attn", u))
        if kind in (FIRST, MIDDLE):
            uses += {2: [("tokens", s) for s in range(SUB)], 3: [("query", 0), ("query", 1)]}.get(u, [])
        if has(kind, u, 1):
            uses += [("mix", u, 0), ("mix", u, 1)]
        if u == SUB - 1 and kind in (FIRST, MIDDLE):
            uses.append(("query", 2))
    return uses


TURNS_AHEAD = SUB + 3


def turns_before(n, kind):
    if kind == FIRST:
        return TURNS_AHEAD
    if kind == TAIL:
        return TURNS_AHEAD + len(turns(FIRST)) + (MACROS - 2) * len(turns(MIDDLE)) + len(turns(LAST))
    return TURNS_AHEAD + len(turns(FIRST)) + (n - 1) * len(turns(MIDDLE))


class Turn:

    def __init__(self, n, kind):
        self.start, self.order = turns_before(n, kind), turns(kind)
        assert len(turns(MIDDLE)) % 2 == 0
        self.parity = turns_before(1, MIDDLE) % 2 if kind in (MIDDLE, LAST) else self.start % 2

    def at(self, *label):
        k = self.order.index(label)
        return self.start + k, TURN_BANK + (self.parity + k) % 2

    def query(self, kind, i):
        if i == BLOCKS - 1:
            return self.at("query", i)[0]
        return self.start - ((3, 2, 1) if kind == FIRST else (5, 4, 1))[i]


def attend(nc, io, ps, keep, att):
    with ExitStack() as ctx:
        def sb(name, shape, dt=F32):
            return ctx.enter_context(nc.sbuf_tensor(name, shape, dt))

        def sem(name):
            return ctx.enter_context(nc.semaphore(name))

        x_in = sb("x_in", [P, SUB, DIM])
        xn = sb("xn", [P, SUB, DIM])
        stats, mean_var = sb("stats", [P, SUB, 6]), sb("mean_var", [P, SUB, 2])
        var_eps, rstd, minus_half = sb("var_eps", [P, SUB]), sb("rstd", [P, SUB]), sb("minus_half", [P, HEADS])
        xnT_hi, xnT_lo = sb("xnT_hi", [P, KD, SUB * P], F32R), sb("xnT_lo", [P, KD, SUB * P], F32R)
        q_hi, q_lo = sb("q_hi", [P, BLOCKS, SUB * P], F32R), sb("q_lo", [P, BLOCKS, SUB * P], F32R)
        neg_max, sums = sb("neg_max", [P, 2, QK_HEADS]), sb("sums", [P, 2, QK_HEADS])
        recips = sb("recips", [P, 2, QK_HEADS])
        probs = sb("probs", [P, 2, QK_HEADS, KEYS])
        mix = sb("mix", [P, CHUNKS * P])
        mixT_hi, mixT_lo = sb("mixT_hi", [P, CHUNKS, P], F32R), sb("mixT_lo", [P, CHUNKS, P], F32R)
        squares, head_ms = sb("squares", [P, DIM]), sb("head_ms", [P, HEADS])
        ms_eps, head_rms = sb("ms_eps", [P, HEADS]), sb("head_rms", [P, HEADS])
        attn = sb("attn", [P, DIM])
        attnT_hi, attnT_lo = sb("attnT_hi", [P, KD, P], F32R), sb("attnT_lo", [P, KD, P], F32R)
        x_res, x1 = sb("x_res", [P, 2, DIM]), sb("x1", [P, 2, DIM])
        stats2, mean_var2 = sb("stats2", [P, 6]), sb("mean_var2", [P, 2])
        var_eps2, rstd2 = sb("var_eps2", [P, 1]), sb("rstd2", [P, 1])
        xn2, xn2T = sb("xn2", [P, 2, DIM]), sb("xn2T", [P, KD, P])

        x_loaded, res_loaded = sem("x_loaded"), [sem("res_loaded0"), sem("res_loaded1")]
        x1_stored = [sem("x1_stored0"), sem("x1_stored1")]
        xn2_stored = [sem("xn2_stored0"), sem("xn2_stored1")]
        out_free = sem("out_free")
        ln1_stats, ln1_rstd, xn_done = sem("ln1_stats"), sem("ln1_rstd"), sem("xn_done")
        turn_done, turn_hi, turn_lo = sem("turn_done"), sem("turn_hi"), sem("turn_lo")
        scores_done, max_done, exp_done = sem("scores_done"), sem("max_done"), sem("exp_done")
        recip_done, scaled, mix_done = sem("recip_done"), sem("scaled"), sem("mix_done")
        values_done, squared, ms_done, rms_done = sem("values_done"), sem("squared"), sem("ms_done"), sem("rms_done")
        attn_done, projected, res_ready, x1_done = (sem("attn_done"), sem("projected"), sem("res_ready"),
                                                    sem("x1_done"))
        ln2_stats, ln2_rstd, xn2_done = sem("ln2_stats"), sem("ln2_rstd"), sem("xn2_done")
        xn2T_psum, xn2T_done = sem("xn2T_psum"), sem("xn2T_done")
        logits_psum, logits_done = sem("logits_psum"), sem("logits_done")
        pool_passed = sem("pool_passed")

        x_rows = io["x"].rearrange("(n s p) d -> n p s d", s=SUB, p=P)
        x_tiles = io["x"].rearrange("(t p) d -> t p d", p=P)
        out_tiles = io["out"].rearrange("(t p) d -> t p d", p=P)
        row_tiles = io["rows"].rearrange("(t p) d -> t p d", p=P)

        def plan(eng, body):
            body(0, FIRST)
            with eng.Fori(1, MACROS - 1) as n:
                body(n, MIDDLE)
            body(MACROS - 1, LAST)
            body(MACROS, TAIL)

        def split_view(bank, w=DIM):
            return ps[:, bank, 0:w].rearrange("p (k t) -> p k t", t=P)

        with nc.Block() as block:
            @block.sync
            def _(sp):
                sp.sem_inc(out_free, 2)
                sp.dma_start(x_in[:], x_rows[0]).then_inc(x_loaded, 16)

                def body(n, kind):
                    for u in range(SUB):
                        s = 4 * n + u
                        if u == 0 and kind in (FIRST, MIDDLE):
                            sp.wait_ge(xn_done, n + 1)
                            sp.dma_start(x_in[:], x_rows[n + 1]).then_inc(x_loaded, 16)
                        if has(kind, u, 2):
                            after(sp, x1_done, s - 3)
                            sp.dma_start(x_res[:, u % 2], x_tiles[s - 2]).then_inc(res_loaded[u % 2], 16)
                        if has(kind, u, 4):
                            t, c = s - 4, u % 2
                            sp.wait_ge(x1_done, t + 1)
                            sp.dma_start(out_tiles[t], x1[:, c]).then_inc(x1_stored[c], 16)
                            sp.wait_ge(xn2_done, t + 1)
                            sp.dma_start(row_tiles[t, :, 0:DIM], xn2[:, c]).then_inc(xn2_stored[c], 16)
                            landed = 16 * (2 * (n - 1) + u // 2 + 1)
                            sp.wait_ge(x1_stored[c], landed)
                            sp.wait_ge(xn2_stored[c], landed)
                            sp.sem_inc(out_free, 1)
                plan(sp, body)

            @block.tensor
            def _(pe):
                def three(out, a_hi, a_lo, b_hi, b_lo, start=True, stop=True, **kw):
                    nc.tensor.matmul(out, a_hi, b_hi, start=start, stop=False, **kw)
                    nc.tensor.matmul(out, a_hi, b_lo, start=False, stop=False, **kw)
                    return nc.tensor.matmul(out, a_lo, b_hi, start=False, stop=stop, **kw)

                def turn(use, src, chunks=KD):
                    index, bank = use
                    after(pe, turn_lo, index - 1)
                    for k in range(chunks):
                        mm = nc.tensor.transpose(ps[:, bank, k * P:(k + 1) * P], src[:, k * P:(k + 1) * P],
                                                 keep["ident"][:])
                    mm.then_inc(turn_done, 1)

                def turn_tokens(n, uses, first):
                    pe.wait_ge(xn_done, n + 1)
                    for s, use in enumerate(uses, first):
                        turn(use, xn[:, s, :])

                def query(i, use, tokens=None):
                    index, bank = use
                    if tokens is not None:
                        pe.wait_ge(turn_lo, tokens + 1)
                    pe.wait_ge(turn_lo, index - 1)
                    hb = BLOCK_ORDER[i]
                    cols = slice(hb * P, (hb + 1) * P)
                    for k in range(KD):
                        mm = three(ps[:, bank, :], att["wq_hi"][:, k, cols], att["wq_lo"][:, k, cols],
                                   xnT_hi[:, k, :], xnT_lo[:, k, :], start=(k == 0), stop=(k == KD - 1))
                    mm.then_inc(turn_done, 1)

                def score_products(n, b, u, i, query_use):
                    hb = BLOCK_ORDER[i]
                    if u == 0:
                        pe.wait_ge(turn_lo, query_use + 1)
                    after(pe, exp_done, 16 * n + 4 * u + i - 1)
                    q = slice(u * P, (u + 1) * P)
                    products = []
                    for half in range(2):
                        k = slice(half * HALF, (half + 1) * HALF)
                        products += parts(ps[:, 2 * (i % 2) + half, 0:HALF], q_hi[:, hb, q], q_lo[:, hb, q],
                                          att["k_hi"][:, b, hb, k], att["k_lo"][:, b, hb, k])
                    return products

                def value_products(t, b, mix_use):
                    pe.wait_ge(turn_lo, mix_use + 1)
                    after(pe, attn_done, t)
                    products = []
                    for c in range(CHUNKS):
                        h0 = first_head(c)
                        products += parts(ps[:, VALUE_BANK, h0 * V_DIM:h0 * V_DIM + WIN], mixT_hi[:, c, :],
                                          mixT_lo[:, c, :], att["v_hi"][:, b, c, :], att["v_lo"][:, b, c, :],
                                          c == 0, c == CHUNKS - 1)
                    return products

                def parts(out, a_hi, a_lo, b_hi, b_lo, start=True, stop=True):
                    return [(out, a_hi, b_hi, start, False), (out, a_hi, b_lo, False, False),
                            (out, a_lo, b_hi, False, stop)]

                def beside(wide, narrow):
                    last = [None, None]
                    for w in range(max(len(wide), 1)):
                        if wide:
                            out, a, b, start, stop = wide[w]
                            last[0] = nc.tensor.matmul(out, a, b, start=start, stop=stop)
                        n = max(len(wide), 1)
                        for out, a, b, start, stop in narrow[w * len(narrow) // n:(w + 1) * len(narrow) // n]:
                            last[1] = nc.tensor.matmul(out, a, b, start=start, stop=stop, skip_group_check=True)
                    return last

                def turn_mix(t, uses):
                    pe.wait_ge(mix_done, 2 * t + 2)
                    for g in range(3):
                        turn(uses[g], mix[:, 4 * g * P:], min(4, CHUNKS - 4 * g))

                def projection(t, attn_use):
                    pe.wait_ge(turn_lo, attn_use + 1)
                    after(pe, xn2T_done, t)
                    products = []
                    for k in range(KD):
                        products += parts(ps[:, PROJECT_BANK, :], attnT_hi[:, k, :], attnT_lo[:, k, :],
                                          att["wp_hi"][:, k, :], att["wp_lo"][:, k, :], k == 0, k == KD - 1)
                    return products

                def turn_mix(uses, first):
                    for g, use in enumerate(uses, first):
                        turn(use, mix[:, 4 * g * P:], min(4, CHUNKS - 4 * g))

                def turn_router(t, c):
                    pe.wait_ge(xn2_done, t + 1)
                    for k in range(KD):
                        mm = nc.tensor.transpose(ps[:, PROJECT_BANK, k * P:(k + 1) * P],
                                                 xn2[:, c, k * P:(k + 1) * P], keep["ident"][:])
                    mm.then_inc(xn2T_psum, 1)

                def router(t, n):
                    pe.wait_ge(xn2T_done, t + 1)
                    pe.wait_ge(exp_done, 16 * n - 1)
                    after(pe, logits_done, t)
                    for k in range(KD):
                        mm = nc.tensor.matmul(ps[:, 0, HALF:HALF + EXPERTS], xn2T[:, k, :], att["gate_w"][:, k, :],
                                              start=(k == 0), stop=(k == KD - 1), skip_group_check=True)
                    mm.then_inc(logits_psum, 1)

                def body(n, kind, b, b_two):
                    use = Turn(n, kind)
                    own = kind != TAIL
                    ahead = kind in (FIRST, MIDDLE)

                    def score(u, i, between=None):
                        if own:
                            wide = score_products(n, b, u, i, use.query(kind, i) if u == 0 else None)
                        if between:
                            between()
                        if own:
                            beside(wide, [])[0].then_inc(scores_done, 1)

                    for u in range(SUB):
                        s = 4 * n + u
                        score(u, 0)
                        if has(kind, u, 2):
                            turn_mix([use.at("mix", u, 2)], 2)
                        if own and u == 0:
                            query(3, use.at("query", 3))
                        if has(kind, u, 4):
                            turn_router(s - 4, u % 2)
                        score(u, 1)
                        if has(kind, u, 3):
                            pe.wait_ge(attn_done, s - 3 + 1)
                            turn(use.at("attn", u), attn[:])
                        if ahead and u == 2:
                            turn_tokens(n + 1, [use.at("tokens", k) for k in range(2)], 0)
                        if ahead and u == 3:
                            query(0, use.at("query", 0), use.at("tokens", SUB - 1)[0])
                        score(u, 2, (lambda: router(s - 4, n)) if has(kind, u, 4) else None)
                        wide, narrow = [], []
                        if has(kind, u, 3):
                            wide = projection(s - 3, use.at("attn", u)[0])
                        if has(kind, u, 2):
                            narrow = value_products(s - 2, b if u >= 2 else b_two, use.at("mix", u, 2)[0])
                        last = beside(wide, narrow)
                        if has(kind, u, 3):
                            last[0].then_inc(projected, 1)
                        if has(kind, u, 2):
                            last[1].then_inc(values_done, 1)
                        if ahead and u == 2:
                            turn_tokens(n + 1, [use.at("tokens", k) for k in range(2, SUB)], 2)
                        if ahead and u == 3:
                            query(1, use.at("query", 1))
                        score(u, 3)
                        if has(kind, u, 1):
                            pe.wait_ge(mix_done, 2 * (s - 1) + 2)
                            turn_mix([use.at("mix", u, g) for g in range(2)], 0)
                        if ahead and u == 3:
                            query(2, use.at("query", 2))

                mid = MACROS // BATCH
                turn_tokens(0, [(k, TURN_BANK + k % 2) for k in range(SUB)], 0)
                for i in range(BLOCKS - 1):
                    query(i, (SUB + i, TURN_BANK + (SUB + i) % 2), SUB - 1)
                body(0, FIRST, 0, 0)
                with pe.Fori(1, mid) as n:
                    body(n, MIDDLE, 0, 0)
                body(mid, MIDDLE, 1, 0)
                with pe.Fori(mid + 1, MACROS - 1) as n:
                    body(n, MIDDLE, 1, 1)
                body(MACROS - 1, LAST, 1, 1)
                body(MACROS, TAIL, 1, 1)

            @block.scalar
            def _(act):
                def hi_part(dst, src, use, scale=1.0):
                    act.wait_ge(turn_done, use[0] + 1)
                    nc.scalar.activation(dst, src, ACT.Copy, scale=scale).then_inc(turn_hi, 1)

                def tokens_hi(uses, first):
                    for s, use in enumerate(uses, first):
                        hi_part(xnT_hi[:, :, s * P:(s + 1) * P], split_view(use[1]), use)

                def query_hi(i, use):
                    hi_part(q_hi[:, BLOCK_ORDER[i], :], ps[:, use[1], :], use, Q_SCALE)

                def exponentials(s, c, i):
                    hb = BLOCK_ORDER[i]
                    act.wait_ge(max_done, 4 * s + i + 1)
                    after(act, mix_done, 2 * (s - 2) + i // 2 + 1)
                    for h in range(HEADS_PER_BLOCK):
                        head = hb * HEADS_PER_BLOCK + h
                        e = nc.scalar.activation(probs[:, c, head, :],
                                                 ps[:, 2 * (i % 2) + h // 4, h % 4 * KEYS:(h % 4 + 1) * KEYS],
                                                 ACT.Exp, bias=neg_max[:, c, head:head + 1],
                                                 accum_out=sums[:, c, head:head + 1])
                    e.then_inc(exp_done, 1)

                def mix_hi(uses, first):
                    for g, use in enumerate(uses, first):
                        c = slice(4 * g, min(4 * g + 4, CHUNKS))
                        hi_part(mixT_hi[:, c, :], split_view(use[1], (c.stop - c.start) * P), use)

                def body(n, kind):
                    use = Turn(n, kind)
                    own = kind != TAIL
                    ahead = kind in (FIRST, MIDDLE)
                    for u in range(SUB):
                        s = 4 * n + u
                        if has(kind, u, 1):
                            exponentials(s - 1, (u - 1) % 2, 3)
                        if has(kind, u, 2):
                            mix_hi([use.at("mix", u, 2)], 2)
                        if own and u == 0:
                            query_hi(3, use.at("query", 3))
                        if own:
                            exponentials(s, u % 2, 0)
                        if has(kind, u, 4):
                            act.wait_ge(xn2T_psum, s - 4 + 1)
                            nc.scalar.activation(xn2T[:], split_view(PROJECT_BANK), ACT.Copy).then_inc(xn2T_done, 1)
                        if has(kind, u, 3):
                            hi_part(attnT_hi[:], split_view(use.at("attn", u)[1]), use.at("attn", u))
                        if ahead and u == 2:
                            tokens_hi([use.at("tokens", k) for k in range(2)], 0)
                        if ahead and u == 3:
                            query_hi(0, use.at("query", 0))
                        if own:
                            exponentials(s, u % 2, 1)
                        if ahead and u == 2:
                            tokens_hi([use.at("tokens", k) for k in range(2, SUB)], 2)
                        if ahead and u == 3:
                            query_hi(1, use.at("query", 1))
                        if has(kind, u, 4):
                            if own:
                                act.wait_ge(max_done, 4 * s + 2 + 1)
                            act.wait_ge(logits_psum, s - 4 + 1)
                            nc.scalar.activation(keep["logits"][:, :, bass.ds(s - 4, 1)].rearrange("p e t -> p (e t)"),
                                                 ps[:, 0, HALF:HALF + EXPERTS], ACT.Copy).then_inc(logits_done, 1)
                        if own:
                            exponentials(s, u % 2, 2)
                        if has(kind, u, 2):
                            act.wait_ge(values_done, s - 2 + 1)
                            nc.scalar.activation(squares[:], ps[:, VALUE_BANK, :], ACT.Square).then_inc(squared, 1)
                        if has(kind, u, 1):
                            mix_hi([use.at("mix", u, g) for g in range(2)], 0)
                        if ahead and u == 3:
                            query_hi(2, use.at("query", 2))

                tokens_hi([(k, TURN_BANK + k % 2) for k in range(SUB)], 0)
                for i in range(BLOCKS - 1):
                    query_hi(i, (SUB + i, TURN_BANK + (SUB + i) % 2))
                plan(act, body)

            @block.vector
            def _(dve):
                def lo_part(dst, src, hi, use):
                    dve.wait_ge(turn_hi, use[0] + 1)
                    nc.vector.tensor_tensor(dst, src, hi.bitcast(F32), ALU.subtract).then_inc(turn_lo, 1)

                def layer_norm(n, first):
                    if first == 0:
                        dve.wait_ge(x_loaded, 16 * (n + 1))
                    for s in range(first, first + 2):
                        nc.vector.bn_stats(stats[:, s, :], x_in[:, s, :])
                    if first:
                        dve.drain()
                        for s in range(SUB):
                            a = nc.vector.bn_aggr(mean_var[:, s, :], stats[:, s, :])
                        a.then_inc(ln1_stats, 1)

                def normalise(n, first):
                    if first == 0:
                        dve.wait_ge(ln1_rstd, n + 1)
                    for s in range(first, first + 2):
                        a = nc.vector.tensor_scalar(xn[:, s, :], x_in[:, s, :], mean_var[:, s, 0:1],
                                                    rstd[:, s:s + 1], ALU.subtract, ALU.mult)
                    if first:
                        a.then_inc(xn_done, 1)

                def tokens_lo(uses, first):
                    for s, use in enumerate(uses, first):
                        cols = slice(s * P, (s + 1) * P)
                        lo_part(xnT_lo[:, :, cols], split_view(use[1]), xnT_hi[:, :, cols], use)

                def query_lo(i, use):
                    hb = BLOCK_ORDER[i]
                    dve.wait_ge(turn_hi, use[0] + 1)
                    nc.vector.scalar_tensor_tensor(q_lo[:, hb, :], ps[:, use[1], :], Q_SCALE,
                                                   q_hi[:, hb, :].bitcast(F32), ALU.mult,
                                                   ALU.subtract).then_inc(turn_lo, 1)

                def maxima(s, c, i):
                    hb = BLOCK_ORDER[i]
                    dve.wait_ge(scores_done, 4 * s + i + 1)
                    heads = slice(hb * HEADS_PER_BLOCK, (hb + 1) * HEADS_PER_BLOCK)
                    nc.vector.tensor_reduce(
                        neg_max[:, c, heads].rearrange("p (a h) -> p a h", a=2),
                        ps[:, 2 * (i % 2):2 * (i % 2) + 2, 0:HALF].rearrange("p a (h k) -> p a h k", k=KEYS),
                        X, ALU.max, negate=True).then_inc(max_done, 1)

                def recip_half(s, c, half):
                    dve.wait_ge(exp_done, 4 * s + 2 * half + 2)
                    second = slice(HEADS + half * 8, HEADS + half * 8 + 8)
                    heads = [ap[:, c, :].rearrange("p (a h) -> p a h", a=2)[:, :, half * 8:half * 8 + 8]
                             for ap in (recips, sums)]
                    nc.vector.reciprocal(*heads)
                    dve.drain()
                    nc.vector.tensor_scalar(recips[:, c, second], recips[:, c, second],
                                            att["neg_lambda"][:, 0:1], None, ALU.mult).then_inc(recip_done, 1)

                def mix_half(s, c, half, turned):
                    first = slice(half * 8, half * 8 + 8)
                    second = slice(HEADS + half * 8, HEADS + half * 8 + 8)
                    dve.wait_ge(scaled, 2 * s + half + 1)
                    after(dve, turn_done, turned)
                    nc.vector.tensor_tensor(
                        mix[:, half * 8 * KEYS:(half + 1) * 8 * KEYS].rearrange("p (h k) -> p h k", k=KEYS),
                        probs[:, c, first, :], probs[:, c, second, :], ALU.add).then_inc(mix_done, 1)

                def mix_lo(uses, first):
                    for g, use in enumerate(uses, first):
                        c = slice(4 * g, min(4 * g + 4, CHUNKS))
                        lo_part(mixT_lo[:, c, :], split_view(use[1], (c.stop - c.start) * P),
                                mixT_hi[:, c, :], use)

                def mean_square(t):
                    dve.wait_ge(squared, t + 1)
                    nc.vector.tensor_reduce(head_ms[:], squares[:].rearrange("p (h d) -> p h d", d=V_DIM),
                                            X, ALU.add).then_inc(ms_done, 1)

                def head_norm(t):
                    dve.wait_ge(rms_done, t + 1)
                    nc.vector.tensor_tensor(attn[:].rearrange("p (h d) -> p h d", d=V_DIM),
                                            ps[:, VALUE_BANK, :].rearrange("p (h d) -> p h d", d=V_DIM),
                                            head_rms[:].unsqueeze(2).to_broadcast([P, HEADS, V_DIM]),
                                            ALU.mult).then_inc(attn_done, 1)

                def residual(t, c):
                    dve.wait_ge(projected, t + 1)
                    dve.wait_ge(res_ready, t + 1)
                    dve.wait_ge(out_free, t + 1)
                    nc.vector.tensor_tensor(x1[:, c], ps[:, PROJECT_BANK, :], x_res[:, c], ALU.add)
                    dve.drain()
                    nc.vector.bn_stats(stats2[:], x1[:, c]).then_inc(x1_done, 1)
                    dve.drain()
                    nc.vector.bn_aggr(mean_var2[:], stats2[:]).then_inc(ln2_stats, 1)

                def normalise2(t, c):
                    dve.wait_ge(ln2_rstd, t + 1)
                    nc.vector.tensor_scalar(xn2[:, c], x1[:, c], mean_var2[:, 0:1], rstd2[:, 0:1],
                                            ALU.subtract, ALU.mult).then_inc(xn2_done, 1)

                def body(n, kind):
                    use = Turn(n, kind)
                    own = kind != TAIL
                    ahead = kind in (FIRST, MIDDLE)
                    for u in range(SUB):
                        s = 4 * n + u
                        turned = use.at("mix", u, 2)[0] if has(kind, u, 2) else -1
                        if own:
                            maxima(s, u % 2, 0)
                        if has(kind, u, 1):
                            mix_half(s - 1, (u - 1) % 2, 0, turned)
                        if has(kind, u, 4):
                            normalise2(s - 4, u % 2)
                        if has(kind, u, 2):
                            mix_lo([use.at("mix", u, 2)], 2)
                        if own and u == 0:
                            query_lo(3, use.at("query", 3))
                        if has(kind, u, 3):
                            head_norm(s - 3)
                        if ahead and u == 1:
                            layer_norm(n + 1, 2)
                        if own:
                            maxima(s, u % 2, 1)
                        if has(kind, u, 1):
                            recip_half(s - 1, (u - 1) % 2, 1)
                        if has(kind, u, 3):
                            lo_part(attnT_lo[:], split_view(use.at("attn", u)[1]), attnT_hi[:], use.at("attn", u))
                        if ahead and u == 2:
                            tokens_lo([use.at("tokens", k) for k in range(2)], 0)
                        if ahead and u == 3:
                            query_lo(0, use.at("query", 0))
                        if own:
                            maxima(s, u % 2, 2)
                        if has(kind, u, 1):
                            mix_half(s - 1, (u - 1) % 2, 1, turned + 1)
                        if ahead and u == 1:
                            normalise(n + 1, 0)
                        if ahead and u == 2:
                            tokens_lo([use.at("tokens", k) for k in range(2, SUB)], 2)
                        if ahead and u == 3:
                            query_lo(1, use.at("query", 1))
                        if own:
                            maxima(s, u % 2, 3)
                            recip_half(s, u % 2, 0)
                        if has(kind, u, 3):
                            residual(s - 3, (u - 3) % 2)
                        if has(kind, u, 1):
                            mix_lo([use.at("mix", u, g) for g in range(2)], 0)
                        if has(kind, u, 2):
                            mean_square(s - 2)
                        if ahead and u == 0:
                            layer_norm(n + 1, 0)
                        if ahead and u == 1:
                            normalise(n + 1, 2)
                        if ahead and u == 3:
                            query_lo(2, use.at("query", 2))

                nc.vector.memset(mix[:, HEADS * KEYS:], 0.0)
                for first in (0, 2):
                    layer_norm(0, first)
                for first in (0, 2):
                    normalise(0, first)
                tokens_lo([(k, TURN_BANK + k % 2) for k in range(SUB)], 0)
                for i in range(BLOCKS - 1):
                    query_lo(i, (SUB + i, TURN_BANK + (SUB + i) % 2))
                plan(dve, body)

            @block.gpsimd
            def _(pool):
                def power(dst, src, w):
                    pool.drain()
                    return nc.gpsimd.tensor_tensor(dst, src, minus_half[:, 0:w], ALU.pow)

                def ln1(n):
                    hold(pool, ln1_stats, n + 1, pool_passed)
                    nc.gpsimd.tensor_scalar(var_eps[:], mean_var[:, :, 1], EPS, None, ALU.add)
                    power(rstd[:], var_eps[:], SUB).then_inc(ln1_rstd, 1)

                def scale(s, c, half):
                    h = slice(half * 8, half * 8 + 8)
                    soft = probs[:, c].rearrange("p (a h) k -> p a h k", a=2)[:, :, h, :]
                    factors = recips[:, c].rearrange("p (a h) -> p a h", a=2)[:, :, h]
                    pool.wait_ge(recip_done, 2 * s + half + 1)
                    nc.gpsimd.tensor_tensor(soft, soft, factors.unsqueeze(3).to_broadcast([P, 2, 8, KEYS]),
                                            ALU.mult).then_inc(scaled, 1)

                def add_bias(n, u):
                    c = (u - 3) % 2
                    pool.wait_ge(res_loaded[c], 16 * (2 * n + (u - 3) // 2 + 1))
                    nc.gpsimd.tensor_tensor(x_res[:, c], x_res[:, c], att["bias"][:], ALU.add).then_inc(res_ready, 1)

                def body(n, kind):
                    for u in range(SUB):
                        s = 4 * n + u
                        if has(kind, u, 1):
                            scale(s - 1, (u - 1) % 2, 1)
                        if has(kind, u, 3):
                            add_bias(n, u)
                        if kind in (FIRST, MIDDLE) and u == 1:
                            ln1(n + 1)
                        if kind != TAIL:
                            scale(s, u % 2, 0)
                        if has(kind, u, 3):
                            hold(pool, ln2_stats, s - 3 + 1, pool_passed)
                            nc.gpsimd.tensor_scalar(var_eps2[:], mean_var2[:, 1:2], EPS, None, ALU.add)
                            power(rstd2[:], var_eps2[:], 1).then_inc(ln2_rstd, 1)
                        if has(kind, u, 2):
                            hold(pool, ms_done, s - 2 + 1, pool_passed)
                            nc.gpsimd.tensor_scalar(ms_eps[:], head_ms[:], 1.0 / V_DIM, EPS, ALU.mult, ALU.add)
                            power(head_rms[:], ms_eps[:], HEADS).then_inc(rms_done, 1)

                nc.gpsimd.memset(minus_half[:], -0.5)
                ln1(0)
                plan(pool, body)


def route(nc, io, ps, keep):
    with ExitStack() as ctx:
        def sb(name, shape, dt=F32):
            return ctx.enter_context(nc.sbuf_tensor(name, shape, dt))

        def sem(name):
            return ctx.enter_context(nc.semaphore(name))

        same_group, before_in_group = sb("same_group", [P, P]), sb("before_in_group", [P, P])
        top = sb("top", [P, TILES])
        shifted = sb("shifted", [P, EXPERTS, TILES])
        expo = sb("expo", [P, EXPERTS, TILES])
        total, inverse = sb("total", [P, TILES]), sb("inverse", [P, TILES])
        affinity = sb("affinity", [P, EXPERTS, TILES])
        by_token = sb("by_token", [P, TILES, EXPERTS])
        aff = sb("aff", [P, SETS, P])
        bit, cut, trial = sb("bit", [P, SETS], U32), sb("cut", [P, SETS], U32), sb("trial", [P, SETS], U32)
        enough = sb("enough", [P, SETS], U32)
        flags = sb("flags", [P, SETS, P])
        count = sb("count", [P, SETS])
        above, equal = sb("above", [P, SETS, P]), sb("equal", [P, SETS, P])
        counts = sb("counts", [P, 2, SETS])
        wanted, equal_before = sb("wanted", [P, SETS]), sb("equal_before", [P, SETS])
        ones = sb("ones", [P, P])
        rank, kept, chosen = sb("rank", [P, SETS, P]), sb("kept", [P, SETS, P]), sb("chosen", [P, SETS, P])
        running = sb("running", [P, SETS, P])
        chosen_before = sb("chosen_before", [P, SETS])
        prefix = sb("prefix", [P, SETS, P], F16)

        loaded, exp_ready, exp_done = sem("consts_loaded"), sem("exp_ready"), sem("expo_done")
        aff_done, aff_turned = sem("aff_done"), sem("aff_turned")
        counted, summed, totals_ready, totals_done = (sem("counted"), sem("summed"), sem("totals_ready"),
                                                      sem("totals_done"))
        by_token_done, chosen_counted, chosen_summed = (sem("by_token_done"), sem("chosen_counted"),
                                                        sem("chosen_summed"))
        prefix_done, stored = sem("prefix_done"), sem("stored")

        with nc.Block() as block:
            @block.sync
            def _(sp):
                sp.dma_start(same_group[:], io["same_group"]).then_inc(loaded, 16)
                sp.dma_start(before_in_group[:], io["before_in_group"]).then_inc(loaded, 16)
                sp.dma_start(bit[:], io["top_bit"]).then_inc(loaded, 16)
                sp.wait_ge(by_token_done, 1)
                sp.dma_start(io["rows"].rearrange("(t p) c -> p t c", p=P)[:, :, DIM:ROW],
                             by_token[:]).then_inc(stored, 16)
                sp.wait_ge(prefix_done, 1)
                sp.dma_start(io["prefix"].rearrange("(s q) t -> q s t", s=SETS), prefix[:]).then_inc(stored, 16)
                sp.wait_ge(stored, 32)

            @block.scalar
            def _(act):
                act.wait_ge(exp_ready, 1)
                nc.scalar.activation(expo[:], shifted[:], ACT.Exp).then_inc(exp_done, 1)

            @block.tensor
            def _(pe):
                pe.wait_ge(aff_done, 1)
                for s in range(SETS):
                    mm = nc.tensor.transpose(ps[:, 0, s * P:(s + 1) * P],
                                             affinity[:, s * SET_E:(s + 1) * SET_E, :].rearrange("p e t -> p (e t)"),
                                             keep["ident"][:])
                mm.then_inc(aff_turned, 1)
                pe.wait_ge(loaded, 48)
                with pe.Fori(0, TOP_BIT + 1) as i:
                    pe.wait_ge(counted, i + 1)
                    nc.tensor.matmul(ps[:, 1, 0:SETS], same_group[:], count[:]).then_inc(summed, 1)
                pe.wait_ge(totals_ready, 1)
                nc.tensor.matmul(ps[:, 2, 0:SETS], same_group[:], counts[:, 0, :])
                nc.tensor.matmul(ps[:, 3, 0:SETS], before_in_group[:], counts[:, 1, :]).then_inc(totals_done, 1)
                pe.wait_ge(chosen_counted, 1)
                nc.tensor.matmul(ps[:, 4, 0:SETS], before_in_group[:], running[:, :, P - 1]).then_inc(
                    chosen_summed, 1)

            @block.vector
            def _(dve):
                nc.vector.memset(ones[:], 1.0)
                nc.vector.memset(cut[:], 0)
                wide = [P, EXPERTS, TILES]
                nc.vector.tensor_reduce(top[:], keep["logits"][:].rearrange("p e t -> p t e"), X, ALU.max)
                dve.drain()
                nc.vector.tensor_tensor(shifted[:], keep["logits"][:], top[:].unsqueeze(1).to_broadcast(wide),
                                        ALU.subtract).then_inc(exp_ready, 1)
                dve.wait_ge(exp_done, 1)
                nc.vector.tensor_reduce(total[:], expo[:].rearrange("p e t -> p t e"), X, ALU.add)
                dve.drain()
                nc.vector.reciprocal(inverse[:], total[:])
                dve.drain()
                nc.vector.tensor_tensor(affinity[:], expo[:], inverse[:].unsqueeze(1).to_broadcast(wide),
                                        ALU.mult).then_inc(aff_done, 1)
                dve.drain()
                nc.vector.tensor_copy(by_token[:], affinity[:].rearrange("p e t -> p t e")).then_inc(by_token_done, 1)
                dve.wait_ge(aff_turned, 1)
                nc.vector.tensor_copy(aff[:].rearrange("p s t -> p (s t)"), ps[:, 0, 0:SETS * P])
                dve.wait_ge(loaded, 48)
                dve.drain()
                with dve.Fori(0, TOP_BIT + 1) as i:
                    nc.vector.tensor_tensor(trial[:], cut[:], bit[:], ALU.bitwise_or)
                    dve.drain()
                    for s in range(SETS):
                        c = nc.vector.tensor_scalar(flags[:, s, :], aff[:, s, :], trial[:, s:s + 1].bitcast(F32),
                                                    0.0, ALU.is_ge, ALU.add, accum_out=count[:, s:s + 1])
                    c.then_inc(counted, 1)
                    nc.vector.tensor_single_scalar(bit[:], bit[:], 1, ALU.logical_shift_right)
                    dve.wait_ge(summed, i + 1)
                    nc.vector.tensor_scalar(enough[:], ps[:, 1, 0:SETS], float(CAP), None, ALU.is_ge)
                    dve.drain()
                    nc.vector.copy_predicated(cut[:], enough[:], trial[:])
                    dve.drain()
                for s in range(SETS):
                    level = cut[:, s:s + 1].bitcast(F32)
                    nc.vector.tensor_scalar(above[:, s, :], aff[:, s, :], level, 0.0, ALU.is_gt, ALU.add,
                                            accum_out=counts[:, 0, s:s + 1])
                    c = nc.vector.tensor_scalar(equal[:, s, :], aff[:, s, :], level, 0.0, ALU.is_equal, ALU.add,
                                                accum_out=counts[:, 1, s:s + 1])
                c.then_inc(totals_ready, 1)
                dve.wait_ge(totals_done, 1)
                nc.vector.tensor_scalar(wanted[:], ps[:, 2, 0:SETS], -1.0, float(CAP), ALU.mult, ALU.add)
                nc.vector.tensor_copy(equal_before[:], ps[:, 3, 0:SETS])
                dve.drain()
                for s in range(SETS):
                    nc.vector.tensor_tensor_scan(rank[:, s, :], ones[:], equal[:, s, :], equal_before[:, s:s + 1],
                                                 ALU.mult, ALU.add)
                dve.drain()
                for s in range(SETS):
                    nc.vector.scalar_tensor_tensor(kept[:, s, :], rank[:, s, :], wanted[:, s:s + 1],
                                                   equal[:, s, :], ALU.is_le, ALU.mult)
                dve.drain()
                nc.vector.tensor_tensor(chosen[:], kept[:], above[:], ALU.add)
                dve.drain()
                for s in range(SETS):
                    c = nc.vector.tensor_tensor_scan(running[:, s, :], ones[:], chosen[:, s, :], 0.0,
                                                     ALU.mult, ALU.add)
                c.then_inc(chosen_counted, 1)
                dve.wait_ge(chosen_summed, 1)
                nc.vector.tensor_copy(chosen_before[:], ps[:, 4, 0:SETS])
                dve.drain()
                for s in range(SETS):
                    c = nc.vector.tensor_scalar(prefix[:, s, :], running[:, s, :], chosen_before[:, s:s + 1],
                                                None, ALU.add)
                c.then_inc(prefix_done, 1)


DOWN_BANK = 4
DOWN_USES = XT + GROUPS * XT


def experts(nc, io, ps, keep):
    with ExitStack() as ctx:
        def sb(name, shape, dt=F32):
            return ctx.enter_context(nc.sbuf_tensor(name, shape, dt))

        def sem(name):
            return ctx.enter_context(nc.semaphore(name))

        raw = sb("raw", [P, GJ, WCOLS])
        gu_hi, gu_lo = sb("gu_hi", [P, GJ, 2, KD, P], F32R), sb("gu_lo", [P, GJ, 2, KD, P], F32R)
        down_hi, down_lo = sb("down_hi", [P, GJ, DIM], F32R), sb("down_lo", [P, GJ, DIM], F32R)
        act_out = sb("act_out", [P, 2, CAP])
        h_hi, h_lo = sb("h_hi", [P, BATCH, GJ, CAP], F32R), sb("h_lo", [P, BATCH, GJ, CAP], F32R)
        gathered = sb("gathered", [P, XT, ROW])
        xT_hi, xT_lo = sb("xT_hi", [P, KD, BATCH * CAP], F32R), sb("xT_lo", [P, KD, BATCH * CAP], F32R)
        y = sb("y", [P, XT, DIM])
        gates = sb("gates", [P, XT])
        prefix = sb("prefix_rows", [P, BATCH, SEQ], F16)
        flags = sb("slot_flags", [P, SEQ], F16)
        found = sb("found", [P, XT])
        take, put = sb("take", [P, XT], U32), sb("put", [P, XT], U32)

        raw_loaded = [sem(f"raw_loaded{j}") for j in range(GJ)]
        gu_hi_done, gu_lo_done, gu_used = sem("gu_hi_done"), sem("gu_lo_done"), sem("gu_used")
        down_hi_done, down_lo_done, down_used = sem("down_hi_done"), sem("down_lo_done"), sem("down_used")
        pair_done, silu_done, h_done, h_hi_done, h_lo_done = (sem("pair_done"), sem("silu_done"), sem("h_done"),
                                                              sem("h_hi_done"), sem("h_lo_done"))
        h_used = sem("h_used")
        bank_done, x_hi_done, bank_free = sem("bank_done"), sem("x_hi_done"), sem("bank_free")
        prefix_loaded, listed, gates_read = sem("prefix_loaded"), sem("listed"), sem("gates_read")
        tokens_gathered = [sem(f"tokens_gathered{t}") for t in range(XT)]
        y_ready, put_ready = sem("y_ready"), sem("put_ready")
        added = [sem(f"added{t}") for t in range(XT)]
        added_all = sem("added_all")
        pool_passed = sem("pool_passed")

        w = io["weights"]
        out_rows, rows = io["out"], io["rows"]

        def prefix_rows(e):
            return io["prefix"].rearrange("(e q) t -> e (q t)", e=EXPERTS)[bass.ds(e, 1), :]

        def plan(eng, body):
            body(0, True, False)
            with eng.Fori(1, EXPERTS - 1) as e:
                body(e, False, False)
            body(EXPERTS - 1, False, True)

        def groups(eng, group):
            group(0)
            with eng.Fori(1, GROUPS) as g:
                group(g)

        with nc.Block() as block:
            @block.sync
            def _(sp):
                def body(e, first, last):
                    if not last:
                        sp.wait_ge(listed, GROUPS * (e + 1))
                        sp.dma_start(prefix[:].rearrange("p b t -> p (b t)"),
                                     prefix_rows(e + 1).to_broadcast([P, BATCH * SEQ])).then_inc(prefix_loaded, 16)

                    def group(g):
                        n = GROUPS * e + g
                        for j in range(GJ):
                            after(sp, down_lo_done, GJ * (n - 1) + j + 1)
                            sp.dma_start(raw[:, j, :], w[n, j]).then_inc(raw_loaded[j], 16)
                    groups(sp, group)

                sp.dma_start(prefix[:].rearrange("p b t -> p (b t)"),
                             prefix_rows(0).to_broadcast([P, BATCH * SEQ])).then_inc(prefix_loaded, 16)
                plan(sp, body)

            @block.tensor
            def _(pe):
                def three(out, a_hi, a_lo, b_hi, b_lo, start, stop):
                    nc.tensor.matmul(out, a_hi, b_hi, start=start, stop=False)
                    nc.tensor.matmul(out, a_hi, b_lo, start=False, stop=False)
                    return nc.tensor.matmul(out, a_lo, b_hi, start=False, stop=stop)

                def body(e, first, last):
                    uses = DOWN_USES * e
                    for t in range(XT):
                        pe.wait_ge(tokens_gathered[t], 16 * (e + 1))
                        after(pe, bank_free, uses + t - 3)
                        for k in range(KD):
                            mm = nc.tensor.transpose(ps[:, DOWN_BANK + t % 4, k * P:(k + 1) * P],
                                                     gathered[:, t, k * P:(k + 1) * P], keep["ident"][:])
                        mm.then_inc(bank_done, 1)

                    def group(g):
                        n = GROUPS * e + g
                        for b in range(BATCH):
                            after_x = uses + SLOT_TILES * (b + 1)
                            if isinstance(g, int):
                                pe.wait_ge(bank_free, after_x)
                            for j in range(GJ):
                                pair = XT * n + GJ * b + j
                                if b == 0:
                                    pe.wait_ge(gu_lo_done, GJ * n + j + 1)
                                after(pe, silu_free, pair - 1)
                                for m in range(2):
                                    for k in range(KD):
                                        cols = slice(b * CAP, (b + 1) * CAP)
                                        mm = three(ps[:, 2 * (j % 2) + m, :], gu_hi[:, j, m, k, :],
                                                   gu_lo[:, j, m, k, :], xT_hi[:, k, cols], xT_lo[:, k, cols],
                                                   k == 0, k == KD - 1)
                                mm.then_inc(pair_done, 1)
                        for b in range(BATCH):
                            pe.wait_ge(h_lo_done, XT * n + GJ * (b + 1))
                            if b == 0:
                                pe.wait_ge(down_lo_done, GJ * (n + 1))
                            for t in range(SLOT_TILES):
                                use = uses + XT + XT * g + SLOT_TILES * b + t
                                pe.wait_ge(bank_free, use - 3)
                                cols = slice(t * P, (t + 1) * P)
                                for j in range(GJ):
                                    mm = three(ps[:, DOWN_BANK + t, :], h_hi[:, b, j, cols], h_lo[:, b, j, cols],
                                               down_hi[:, j, :], down_lo[:, j, :], j == 0, j == GJ - 1)
                                mm.then_inc(bank_done, 1)
                    groups(pe, group)

                silu_free = h_done
                plan(pe, body)

            @block.scalar
            def _(act):
                def body(e, first, last):
                    uses = DOWN_USES * e
                    for t in range(XT):
                        act.wait_ge(bank_done, uses + t + 1)
                        nc.scalar.activation(xT_hi[:, :, t * P:(t + 1) * P],
                                             ps[:, DOWN_BANK + t % 4, :].rearrange("p (k t) -> p k t", t=P),
                                             ACT.Copy).then_inc(x_hi_done, 1)

                    def group(g):
                        n = GROUPS * e + g
                        for j in range(GJ):
                            act.wait_ge(raw_loaded[j], 16 * (n + 1))
                            after(act, pair_done, XT * (n - 1) + GJ + j + 1)
                            nc.scalar.activation(gu_hi[:, j].rearrange("p m k i -> p (m k i)"), raw[:, j, 0:GU],
                                                 ACT.Copy).then_inc(gu_hi_done, 1)
                        for b in range(BATCH):
                            after(act, bank_done, uses + XT * (g + 1) - XT + SLOT_TILES * (b + 1)
                                  if not (isinstance(g, int)) else uses - XT + SLOT_TILES * (b + 1))
                            for j in range(GJ):
                                pair = XT * n + GJ * b + j
                                act.wait_ge(pair_done, pair + 1)
                                after(act, h_lo_done, pair - 1)
                                nc.scalar.activation(act_out[:, j % 2, :], ps[:, 2 * (j % 2), :],
                                                     ACT.Silu).then_inc(silu_done, 1)
                                act.wait_ge(h_done, pair + 1)
                                nc.scalar.activation(h_hi[:, b, j, :], act_out[:, j % 2, :],
                                                     ACT.Copy).then_inc(h_hi_done, 1)
                                if b == 0:
                                    if j == 0:
                                        after(act, bank_done, down_uses_before(uses, g))
                                    nc.scalar.activation(down_hi[:, j, :], raw[:, j, GU:WCOLS],
                                                         ACT.Copy).then_inc(down_hi_done, 1)
                    groups(act, group)
                plan(act, body)

            @block.vector
            def _(dve):
                def list_tokens(i, g):
                    nc.vector.tensor_scalar(flags[:], prefix[:, i, :], keep["slot_number"][:, bass.ds(g, 1)],
                                            0.0, ALU.is_le, ALU.add,
                                            accum_out=found[:, bass.ds(SLOT_TILES * i + g, 1)])
                    dve.drain()

                def list_group(e, g):
                    if isinstance(g, int):
                        dve.wait_ge(prefix_loaded, 16 * (e + 1))
                    for i in range(BATCH):
                        list_tokens(i, g)
                    for i in range(BATCH):
                        col = bass.ds(SLOT_TILES * i + g, 1)
                        a = nc.vector.tensor_scalar(take[:, col], found[:, col], float(SEQ * i), None, ALU.add)
                    a.then_inc(listed, 1)

                def body(e, first, last):
                    uses = DOWN_USES * e
                    for t in range(XT):
                        cols = slice(t * P, (t + 1) * P)
                        dve.wait_ge(x_hi_done, XT * e + t + 1)
                        nc.vector.tensor_tensor(xT_lo[:, :, cols],
                                                ps[:, DOWN_BANK + t % 4, :].rearrange("p (k t) -> p k t", t=P),
                                                xT_hi[:, :, cols].bitcast(F32),
                                                ALU.subtract).then_inc(bank_free, 1)
                    for t in range(XT):
                        dve.wait_ge(tokens_gathered[t], 16 * (e + 1))
                    nc.vector.tensor_copy(gates[:], gathered[:, :, bass.ds(e + DIM, 1)].rearrange(
                        "p t c -> p (t c)")).then_inc(gates_read, 1)

                    def group(g):
                        n = GROUPS * e + g
                        for b in range(BATCH):
                            for j in range(GJ):
                                pair = XT * n + GJ * b + j
                                dve.wait_ge(silu_done, pair + 1)
                                nc.vector.tensor_tensor(act_out[:, j % 2, :], act_out[:, j % 2, :],
                                                        ps[:, 2 * (j % 2) + 1, :], ALU.mult).then_inc(h_done, 1)
                                dve.wait_ge(h_hi_done, pair + 1)
                                nc.vector.tensor_tensor(h_lo[:, b, j, :], act_out[:, j % 2, :],
                                                        h_hi[:, b, j, :].bitcast(F32),
                                                        ALU.subtract).then_inc(h_lo_done, 1)
                        if isinstance(g, int):
                            if not first:
                                dve.wait_ge(added_all, e)
                            nc.vector.tensor_copy(put[:], take[:]).then_inc(put_ready, 1)
                            dve.drain()
                        if not last:
                            list_group(e + 1, g)
                        for t in range(XT):
                            dve.wait_ge(bank_done, uses + XT + XT * g + t + 1)
                            bank = ps[:, DOWN_BANK + t % 4, :]
                            if isinstance(g, int):
                                a = nc.vector.tensor_copy(y[:, t, :], bank)
                            else:
                                a = nc.vector.tensor_tensor(y[:, t, :], y[:, t, :], bank, ALU.add)
                            a.then_inc(bank_free, 1)
                    groups(dve, group)
                    dve.drain()
                    for t in range(XT):
                        nc.vector.tensor_scalar(y[:, t, :], y[:, t, :], gates[:, t:t + 1], None,
                                                ALU.mult).then_inc(y_ready, 1)

                list_group(0, 0)
                for g in range(1, GROUPS):
                    for i in range(BATCH):
                        list_tokens(i, g)
                    for i in range(BATCH):
                        col = bass.ds(SLOT_TILES * i + g, 1)
                        a = nc.vector.tensor_scalar(take[:, col], found[:, col], float(SEQ * i), None, ALU.add)
                    a.then_inc(listed, 1)
                plan(dve, body)

            @block.gpsimd
            def _(pool):
                def gather(e):
                    hold(pool, listed, GROUPS * (e + 1), pool_passed)
                    for t in range(XT):
                        pool.indirect_dma_start(gathered[:, t, :], None, rows,
                                                bass.IndirectOffsetOnAxis(take[:, t:t + 1], 0)).then_inc(
                            tokens_gathered[t], 16)

                def body(e, first, last):
                    def group(g):
                        n = GROUPS * e + g
                        for j in range(GJ):
                            pool.wait_ge(gu_hi_done, GJ * n + j + 1)
                            nc.gpsimd.tensor_tensor(gu_lo[:, j].rearrange("p m k i -> p (m k i)"), raw[:, j, 0:GU],
                                                    gu_hi[:, j].rearrange("p m k i -> p (m k i)").bitcast(F32),
                                                    ALU.subtract).then_inc(gu_lo_done, 1)
                        if isinstance(g, int) and not first:
                            for t in range(XT):
                                pool.wait_ge(added[t], 16 * e)
                            pool.sem_inc(added_all, 1)
                        for j in range(GJ):
                            pool.wait_ge(down_hi_done, GJ * n + j + 1)
                            nc.gpsimd.tensor_tensor(down_lo[:, j, :], raw[:, j, GU:WCOLS],
                                                    down_hi[:, j, :].bitcast(F32),
                                                    ALU.subtract).then_inc(down_lo_done, 1)
                    groups(pool, group)
                    if not last:
                        pool.wait_ge(gates_read, e + 1)
                        pool.wait_ge(x_hi_done, XT * (e + 1))
                        gather(e + 1)
                    pool.wait_ge(put_ready, e + 1)
                    for t in range(XT):
                        hold(pool, y_ready, XT * e + t + 1, pool_passed)
                        pool.indirect_dma_start(out_rows, bass.IndirectOffsetOnAxis(put[:, t:t + 1], 0), y[:, t, :],
                                                None, compute_op=ALU.add).then_inc(added[t], 16)

                gather(0)
                plan(pool, body)
                for t in range(XT):
                    pool.wait_ge(added[t], 16 * EXPERTS)


def down_uses_before(uses, g):
    return uses if isinstance(g, int) else uses + XT * (g + 1)


def kernel(**inputs):
    import concourse.bacc as bacc
    from concourse.bass_utils import run_bass_kernel_spmd as run

    a = {name: np.asarray(value) for name, value in inputs.items()}

    def on_all(v):
        return np.ascontiguousarray(np.broadcast_to(v, (P,) + v.shape))

    ctx_t = a["ctx_1024"].transpose(2, 0, 1)
    lam = np.stack([a["L0_xattn_" + n] for n in ("lq1", "lk1", "lq2", "lk2")])
    gu = [a["L0_ffn_" + n].reshape(EXPERTS, INNER // P, P, KD, P).transpose(0, 1, 4, 3, 2).reshape(
        EXPERTS, INNER // P, P, DIM) for n in ("w_gate", "w_up")]
    down = a["L0_ffn_w_down"].transpose(0, 2, 1).reshape(EXPERTS, INNER // P, P, DIM)
    weights = np.concatenate(gu + [down], axis=-1).reshape(EXPERTS * GROUPS, GJ, P, WCOLS)
    arrays = {
        "x": a["x"].reshape(TOKENS, DIM),
        "ctxT": np.concatenate([ctx_t] * 3, axis=-1),
        "WqT": a["L0_xattn_Wq"].T, "WkT": a["L0_xattn_Wk"].T, "WvT": a["L0_xattn_Wv"].T,
        "WpT": a["L0_xattn_Wp"].T,
        "bias": on_all(a["L0_xattn_bp"]),
        "lam_in": on_all(lam),
        "subln": np.concatenate([a["L0_xattn_subln_w"]] * (P // V_DIM)).reshape(P, 1),
        "gate_wT": a["L0_ffn_gate_w"].T,
        "weights": weights,
        **shape_constants(),
    }
    arrays = {name: np.ascontiguousarray(v) for name, v in arrays.items()}
    feeds = {"in_" + name: v for name, v in arrays.items()}
    nc = bacc.Bacc("TRN2", target_bir_lowering=False, num_devices=1)
    io = {name: nc.dram_tensor("in_" + name, v.shape, mybir.dt.from_np(v.dtype), kind="ExternalInput").ap()
          for name, v in arrays.items()}
    io["out"] = nc.dram_tensor("out_x", (TOKENS, DIM), F32, kind="ExternalOutput").ap()
    io["rows"] = nc.dram_tensor("token_rows", (TOKENS, ROW), F32).ap()
    io["prefix"] = nc.dram_tensor("chosen_counts", (SETS * P, P), F16).ap()
    build(nc, io)
    got = run(nc, [feeds], core_ids=[0]).results[0]["out_x"]
    return got.reshape(BATCH, SEQ, DIM)
```

```python
from contextlib import ExitStack
import math

import numpy as np

import concourse.bass as bass
from concourse import mybir
from concourse.alu_op_type import AluOpType as ALU

F32 = mybir.dt.float32
F32R = mybir.dt.float32r
F16 = mybir.dt.float16
U32 = mybir.dt.uint32
ACT = mybir.ActivationFunctionType
X = mybir.AxisListType.X

P = 128
BATCH, SEQ, DIM = 2, 2048, 512
TOKENS = BATCH * SEQ
KEYS = 77
HEADS = 16
QK_HEADS = 2 * HEADS
QK_DIM = DIM // QK_HEADS
V_DIM = DIM // HEADS
KD = DIM // P
HEADS_PER_BLOCK = P // QK_DIM
BLOCKS = QK_HEADS // HEADS_PER_BLOCK
HALF = HEADS_PER_BLOCK // 2 * KEYS
CHUNKS = -(-HEADS * KEYS // P)
WINDOW = 3
WIN = WINDOW * V_DIM
WIDE = 5
WIDE_WIN = WIDE * V_DIM
CTX_COLS = 3 * KEYS
EPS = 1e-5
LAMBDA_INIT = 0.8 - 0.6 * math.exp(-0.3 * 4)
Q_SCALE = QK_DIM ** -0.5
TILES = TOKENS // P
SUB = 4
MACROS = TILES // SUB

EXPERTS, INNER = 8, 2048
CAP = SEQ // EXPERTS * 2
SLOT_TILES = CAP // P
XT = BATCH * SLOT_TILES
GJ = 4
GROUPS = INNER // P // GJ
GU = 2 * DIM
WCOLS = 3 * DIM
ROW = DIM + EXPERTS
SET_E = 4
SETS = EXPERTS // SET_E
GROUP_P = SEQ // P
DIGITS = 15
DIGITS_PER_STEP = 3

BLOCK_ORDER = [0, 2, 1, 3]


def after(eng, sem, count):
    if not isinstance(count, int) or count > 0:
        eng.wait_ge(sem, count)


def hold(eng, sem, count, passed):
    eng.wait_ge(sem, count)
    eng.sem_inc(passed, 1)


def first_head(c):
    return min(P * c // KEYS, HEADS - WINDOW)


def wide_first(c):
    return min(first_head(c), HEADS - WIDE)


def shape_constants():
    p = np.arange(P)
    flat = P * np.arange(CHUNKS)[None, :] + p[:, None]
    h0 = np.array([first_head(c) for c in range(CHUNKS)])
    vmask = (flat[:, :, None] // KEYS == h0[None, :, None] + np.arange(WINDOW)[None, None, :])
    same = p[:, None] // GROUP_P == p[None, :] // GROUP_P
    return {
        "ident": np.eye(P, dtype=np.float32),
        "headmask": (p[:, None] // QK_DIM == np.arange(HEADS_PER_BLOCK)[None, :]).astype(np.float32),
        "vmask": vmask.astype(np.float32),
        "same_group": same.astype(np.float32),
        "before_in_group": (same & (p[:, None] < p[None, :])).astype(np.float32),
        "slot_number": (p[:, None] + P * np.arange(SLOT_TILES)[None, :]).astype(np.float32),
        "top_digits": np.tile((np.arange(1, 4, dtype=np.uint32) << (2 * DIGITS - 2))[None, :, None], (P, 1, SETS)),
    }


def build(nc, io):
    with ExitStack() as whole:
        ps = whole.enter_context(nc.psum_tensor("ps", [P, 8, 512], F32))
        keep = {}
        for name, shape, dt in [("ident", [P, P], F32), ("logits", [P, EXPERTS, TILES], F32),
                                ("slot_number", [P, SLOT_TILES], F32)]:
            keep[name] = whole.enter_context(nc.sbuf_tensor(name, shape, dt))
        with ExitStack() as ctx:
            att = {}
            for name, shape, dt in [
                ("wq_hi", [P, KD, DIM], F32R), ("wq_lo", [P, KD, DIM], F32R),
                ("wp_hi", [P, KD, DIM], F32R), ("wp_lo", [P, KD, DIM], F32R),
                ("k_hi", [P, BATCH, BLOCKS, HEADS_PER_BLOCK * KEYS], F32R),
                ("k_lo", [P, BATCH, BLOCKS, HEADS_PER_BLOCK * KEYS], F32R),
                ("v_hi", [P, BATCH, CHUNKS, WIDE_WIN], F32R),
                ("v_lo", [P, BATCH, CHUNKS, WIDE_WIN], F32R),
                ("gate_w", [P, KD, EXPERTS], F32), ("bias", [P, DIM], F32),
                ("neg_lambda", [P, 1], F32),
            ]:
                att[name] = ctx.enter_context(nc.sbuf_tensor(name, shape, dt))
            att["x_in"] = ctx.enter_context(nc.sbuf_tensor("x_in", [P, SUB, DIM], F32))
            x_loaded = [ctx.enter_context(nc.semaphore(f"x_loaded{k}")) for k in range(SUB)]
            prepare(nc, io, ps, keep, att, x_loaded)
            attend(nc, io, ps, keep, att, x_loaded)
        keep["raw"] = whole.enter_context(nc.sbuf_tensor("raw", [P, GJ, WCOLS], F32))
        raw_loaded = [whole.enter_context(nc.semaphore(f"raw_loaded{j}")) for j in range(GJ)]
        route(nc, io, ps, keep, raw_loaded)
        experts(nc, io, ps, keep, raw_loaded)


def prepare(nc, io, ps, keep, att, x_loaded):
    with ExitStack() as ctx:
        def sb(name, shape, dt=F32):
            return ctx.enter_context(nc.sbuf_tensor(name, shape, dt))

        def sem(name):
            return ctx.enter_context(nc.semaphore(name))

        wq_raw, wp_raw = sb("wq_raw", [P, KD, DIM]), sb("wp_raw", [P, KD, DIM])
        wk, wv = sb("wk", [P, KD, DIM]), sb("wv", [P, KD, DIM])
        ctx_t = sb("ctx_t", [P, KD, BATCH, CTX_COLS])
        headmask = sb("headmask", [P, HEADS_PER_BLOCK])
        vmask = sb("vmask", [P, CHUNKS, WINDOW])
        k_f32 = sb("k_f32", [P, BATCH, BLOCKS, HEADS_PER_BLOCK, KEYS])
        v_f32 = sb("v_f32", [P, BATCH, CHUNKS, WIDE_WIN])
        subln = sb("subln", [P, 1])
        lam_in = sb("lam_in", [P, 4, QK_DIM])
        lam_prod = sb("lam_prod", [P, 2, QK_DIM])
        lam_dot, lam_exp, lam_diff = sb("lam_dot", [P, 2]), sb("lam_exp", [P, 2]), sb("lam_diff", [P, 1])

        small_loaded, kv_loaded, q_loaded = sem("small_loaded"), sem("kv_loaded"), sem("q_loaded")
        wp_loaded = sem("wp_loaded")
        wp_scaled, lam_dots, lam_exps = sem("wp_scaled"), sem("lam_dots"), sem("lam_exps")
        k_hi_done, w_hi_done, v_hi_done = sem("k_hi_done"), sem("w_hi_done"), sem("v_hi_done")
        k_done, v_done, k_masked, v_masked = sem("k_done"), sem("v_done"), sem("k_masked"), sem("v_masked")

        def chunked(a):
            return a.rearrange("(k p) n -> p k n", p=P)

        def v_part(v, g):
            return v[:, g // 2, g % 2 * CHUNKS // 2:(g % 2 + 1) * CHUNKS // 2, :]

        small = [(keep["ident"], io["ident"]), (headmask, io["headmask"]), (vmask, io["vmask"]),
                 (keep["slot_number"], io["slot_number"]), (subln, io["subln"]), (lam_in, io["lam_in"]),
                 (att["gate_w"], chunked(io["gate_wT"])), (att["bias"], io["bias"])]

        with nc.Block() as block:
            @block.sync
            def _(sp):
                sp.dma_start(ctx_t[:], io["ctxT"].rearrange("(k p) b n -> p k b n", p=P)).then_inc(kv_loaded, 16)
                sp.dma_start(wk[:], chunked(io["WkT"])).then_inc(kv_loaded, 16)
                sp.dma_start(wv[:], chunked(io["WvT"])).then_inc(kv_loaded, 16)
                for dst, src in small:
                    sp.dma_start(dst[:], src).then_inc(small_loaded, 16)
                sp.dma_start(wq_raw[:], chunked(io["WqT"])).then_inc(q_loaded, 16)
                sp.dma_start(wp_raw[:], chunked(io["WpT"])).then_inc(wp_loaded, 16)
                for k in range(SUB):
                    sp.dma_start(att["x_in"][:, k], io["x"][k * P:(k + 1) * P, :]).then_inc(x_loaded[k], 16)

            @block.tensor
            def _(pe):
                pe.wait_ge(kv_loaded, 48)
                for b in range(BATCH):
                    for hb in range(BLOCKS):
                        for k in range(KD):
                            mm = nc.tensor.matmul(ps[:, b, hb * P:hb * P + KEYS], wk[:, k, hb * P:(hb + 1) * P],
                                                  ctx_t[:, k, b, 0:KEYS], start=(k == 0), stop=(k == KD - 1))
                        mm.then_inc(k_done, 1)
                for g in range(BATCH * CHUNKS):
                    b, c = divmod(g, CHUNKS)
                    key0, h0 = P * c % KEYS, first_head(c)
                    for k in range(KD):
                        mm = nc.tensor.matmul(ps[:, 2 + g // 5, g % 5 * WIN:(g % 5 + 1) * WIN],
                                              ctx_t[:, k, b, key0:key0 + P],
                                              wv[:, k, h0 * V_DIM:h0 * V_DIM + WIN],
                                              start=(k == 0), stop=(k == KD - 1))
                    if g % 5 == 4:
                        mm.then_inc(v_done, 1)

            @block.scalar
            def _(act):
                act.wait_ge(lam_dots, 1)
                nc.scalar.activation(lam_exp[:], lam_dot[:], ACT.Exp).then_inc(lam_exps, 1)
                for n in range(BATCH * BLOCKS):
                    b, hb = divmod(n, BLOCKS)
                    act.wait_ge(k_masked, n + 1)
                    nc.scalar.activation(att["k_hi"][:, b, hb, :],
                                         k_f32[:, b, hb].rearrange("p h k -> p (h k)"),
                                         ACT.Copy).then_inc(k_hi_done, 1)
                act.wait_ge(q_loaded, 16)
                nc.scalar.activation(att["wq_hi"][:], wq_raw[:], ACT.Copy).then_inc(w_hi_done, 1)
                act.wait_ge(wp_scaled, 1)
                nc.scalar.activation(att["wp_hi"][:], wp_raw[:], ACT.Copy).then_inc(w_hi_done, 1)
                for g in range(4):
                    act.wait_ge(v_masked, g + 1)
                    nc.scalar.activation(v_part(att["v_hi"], g), v_part(v_f32, g), ACT.Copy).then_inc(v_hi_done, 1)

            @block.vector
            def _(dve):
                def v_low_part(g):
                    dve.wait_ge(v_hi_done, g + 1)
                    nc.vector.tensor_tensor(v_part(att["v_lo"], g), v_part(v_f32, g),
                                            v_part(att["v_hi"], g).bitcast(F32), ALU.subtract)

                nc.vector.memset(v_f32[:], 0.0)
                dve.wait_ge(small_loaded, 16 * len(small))
                lam_v = lam_in[:].rearrange("p (a b) d -> p a b d", b=2)
                nc.vector.tensor_tensor(lam_prod[:], lam_v[:, :, 0, :], lam_v[:, :, 1, :], ALU.mult)
                dve.drain()
                nc.vector.tensor_reduce(lam_dot[:], lam_prod[:], X, ALU.add).then_inc(lam_dots, 1)
                for n in range(BATCH * BLOCKS):
                    b, hb = divmod(n, BLOCKS)
                    dve.wait_ge(k_done, BLOCKS * (b + 1))
                    kt = ps[:, b, hb * P:hb * P + KEYS].unsqueeze(1).to_broadcast([P, HEADS_PER_BLOCK, KEYS])
                    mask = headmask[:].unsqueeze(2).to_broadcast([P, HEADS_PER_BLOCK, KEYS])
                    nc.vector.tensor_tensor(k_f32[:, b, hb], kt, mask, ALU.mult).then_inc(k_masked, 1)
                dve.wait_ge(wp_loaded, 16)
                nc.vector.tensor_scalar(wp_raw[:], wp_raw[:], subln[:, 0:1], 1.0 - LAMBDA_INIT,
                                        ALU.mult, ALU.mult).then_inc(wp_scaled, 1)
                for n in range(BATCH * BLOCKS):
                    b, hb = divmod(n, BLOCKS)
                    dve.wait_ge(k_hi_done, n + 1)
                    nc.vector.tensor_tensor(att["k_lo"][:, b, hb, :],
                                            k_f32[:, b, hb].rearrange("p h k -> p (h k)"),
                                            att["k_hi"][:, b, hb, :].bitcast(F32), ALU.subtract)
                for g in range(4):
                    b, half = divmod(g, 2)
                    c0 = half * 5
                    dve.wait_ge(v_done, g + 1)
                    for c in range(c0, c0 + 5):
                        vv = ps[:, 2 + g, (c - c0) * WIN:(c - c0 + 1) * WIN].rearrange("p (w d) -> p w d", d=V_DIM)
                        mask = vmask[:, c, :].unsqueeze(2).to_broadcast([P, WINDOW, V_DIM])
                        left = (first_head(c) - wide_first(c)) * V_DIM
                        v = nc.vector.tensor_tensor(
                            v_f32[:, b, c, left:left + WIN].rearrange("p (w d) -> p w d", d=V_DIM),
                            vv, mask, ALU.mult)
                    v.then_inc(v_masked, 1)
                    if g:
                        v_low_part(g - 1)
                v_low_part(3)
                dve.wait_ge(lam_exps, 1)
                nc.vector.tensor_tensor(lam_diff[:], lam_exp[:, 1:2], lam_exp[:, 0:1], ALU.subtract)
                dve.drain()
                nc.vector.tensor_scalar(att["neg_lambda"][:], lam_diff[:], LAMBDA_INIT, None, ALU.subtract)
                dve.drain()

            @block.gpsimd
            def _(pool):
                for n, (lo, raw, hi) in enumerate([("wq_lo", wq_raw, "wq_hi"), ("wp_lo", wp_raw, "wp_hi")]):
                    pool.wait_ge(w_hi_done, n + 1)
                    nc.gpsimd.tensor_tensor(att[lo][:], raw[:], att[hi][:].bitcast(F32), ALU.subtract)



TURN_BANK, PROJECT_BANK, VALUE_BANK = 4, 6, 7
PAIRS = [slice(0, 2 * P), slice(2 * P, 4 * P)]
CHUNKS_FIRST = 5

FIRST, MIDDLE, LAST, TAIL = "first", "middle", "last", "tail"


def has(kind, u, lag):
    if kind == FIRST:
        return u >= lag
    if kind == TAIL:
        return lag > u
    return True


def turns(kind):
    uses = []
    for u in range(SUB):
        if has_queries(kind, u):
            uses.append(("query", u, 0))
        if has(kind, u, 2):
            uses += [("mix", u, 0), ("mix", u, 1)]
        if has_queries(kind, u):
            uses.append(("query", u, 1))
        if has(kind, u, 2):
            uses.append(("mix", u, 2))
        if has(kind, u, 3):
            uses.append(("attn", u))
        if kind in (FIRST, MIDDLE):
            uses.append(("tokens", u))
    return uses


def has_queries(kind, u):
    return kind in (FIRST, MIDDLE) or kind == LAST and u < 2


TURNS_AHEAD = SUB + BLOCKS


def turns_before(n, kind):
    if kind == FIRST:
        return TURNS_AHEAD
    if kind == TAIL:
        return TURNS_AHEAD + len(turns(FIRST)) + (MACROS - 2) * len(turns(MIDDLE)) + len(turns(LAST))
    return TURNS_AHEAD + len(turns(FIRST)) + (n - 1) * len(turns(MIDDLE))


class Turn:

    def __init__(self, n, kind):
        self.start, self.order = turns_before(n, kind), turns(kind)
        assert len(turns(MIDDLE)) % 2 == 0
        self.parity = turns_before(1, MIDDLE) % 2 if kind in (MIDDLE, LAST) else self.start % 2

    def at(self, *label):
        k = self.order.index(label)
        return self.start + k, TURN_BANK + (self.parity + k) % 2

    def query(self, kind, u, i):
        if u:
            return self.at("query", i // 2, i % 2)[0]
        if kind == FIRST:
            return self.start - BLOCKS + i
        return self.start - (9, 9, 7, 4)[i]


def attend(nc, io, ps, keep, att, x_loaded):
    with ExitStack() as ctx:
        def sb(name, shape, dt=F32):
            return ctx.enter_context(nc.sbuf_tensor(name, shape, dt))

        def sem(name):
            return ctx.enter_context(nc.semaphore(name))

        x_in = att["x_in"]
        xn = sb("xn", [P, SUB, DIM])
        stats, mean_var = sb("stats", [P, SUB, 6]), sb("mean_var", [P, SUB, 2])
        var_eps, rstd, minus_half = sb("var_eps", [P, SUB]), sb("rstd", [P, SUB]), sb("minus_half", [P, HEADS])
        xnT_hi, xnT_lo = sb("xnT_hi", [P, KD, SUB * P], F32R), sb("xnT_lo", [P, KD, SUB * P], F32R)
        q_hi, q_lo = sb("q_hi", [P, BLOCKS, SUB * P], F32R), sb("q_lo", [P, BLOCKS, SUB * P], F32R)
        neg_max, sums = sb("neg_max", [P, 2, QK_HEADS]), sb("sums", [P, 2, QK_HEADS])
        recips = sb("recips", [P, 2, QK_HEADS])
        probs = sb("probs", [P, 2, QK_HEADS, KEYS])
        mix = sb("mix", [P, CHUNKS * P])
        mixT_hi, mixT_lo = sb("mixT_hi", [P, CHUNKS, P], F32R), sb("mixT_lo", [P, CHUNKS, P], F32R)
        squares, head_ms = sb("squares", [P, DIM]), sb("head_ms", [P, HEADS])
        ms_eps, head_rms = sb("ms_eps", [P, HEADS]), sb("head_rms", [P, HEADS])
        attn = sb("attn", [P, DIM])
        attnT_hi, attnT_lo = sb("attnT_hi", [P, KD, P], F32R), sb("attnT_lo", [P, KD, P], F32R)
        x_res, x1 = sb("x_res", [P, 2, DIM]), sb("x1", [P, 2, DIM])
        stats2, mean_var2 = sb("stats2", [P, 6]), sb("mean_var2", [P, 2])
        var_eps2, rstd2 = sb("var_eps2", [P, 1]), sb("rstd2", [P, 1])
        xn2, xn2T = sb("xn2", [P, 2, DIM]), sb("xn2T", [P, KD, P])

        res_loaded = [sem("res_loaded0"), sem("res_loaded1")]
        x1_stored = [sem("x1_stored0"), sem("x1_stored1")]
        xn2_stored = [sem("xn2_stored0"), sem("xn2_stored1")]
        out_free = sem("out_free")
        ln1_stats, ln1_rstd, xn_done = sem("ln1_stats"), sem("ln1_rstd"), sem("xn_done")
        turn_done, turn_hi, turn_lo = sem("turn_done"), sem("turn_hi"), sem("turn_lo")
        scores_done, max_done, exp_done = sem("scores_done"), sem("max_done"), sem("exp_done")
        recip_done, scaled, mix_done = sem("recip_done"), sem("scaled"), sem("mix_done")
        values_done, squared, ms_done, rms_done = sem("values_done"), sem("squared"), sem("ms_done"), sem("rms_done")
        attn_done, projected, res_ready, x1_done = (sem("attn_done"), sem("projected"), sem("res_ready"),
                                                    sem("x1_done"))
        ln2_stats, ln2_rstd, xn2_done = sem("ln2_stats"), sem("ln2_rstd"), sem("xn2_done")
        xn2T_psum, xn2T_done = sem("xn2T_psum"), sem("xn2T_done")
        logits_psum, logits_done = sem("logits_psum"), sem("logits_done")
        pool_passed = sem("pool_passed")

        x_tiles = io["x"].rearrange("(t p) d -> t p d", p=P)
        out_tiles = io["out"].rearrange("(t p) d -> t p d", p=P)
        row_tiles = io["rows"].rearrange("(t p) d -> t p d", p=P)

        def plan(eng, body):
            body(0, FIRST)
            with eng.Fori(1, MACROS - 1) as n:
                body(n, MIDDLE)
            body(MACROS - 1, LAST)
            body(MACROS, TAIL)

        def split_view(bank, w=DIM):
            return ps[:, bank, 0:w].rearrange("p (k t) -> p k t", t=P)

        with nc.Block() as block:
            @block.sync
            def _(sp):
                sp.sem_inc(out_free, 2)

                def body(n, kind):
                    for u in range(SUB):
                        s = 4 * n + u
                        if kind in (FIRST, MIDDLE):
                            sp.wait_ge(xn_done, s + 1)
                            sp.dma_start(x_in[:, u], x_tiles[s + 4]).then_inc(x_loaded[u], 16)
                        if has(kind, u, 2):
                            after(sp, x1_done, s - 3)
                            sp.dma_start(x_res[:, u % 2], x_tiles[s - 2]).then_inc(res_loaded[u % 2], 16)
                        if has(kind, u, 4):
                            t, c = s - 4, u % 2
                            sp.wait_ge(x1_done, t + 1)
                            sp.dma_start(out_tiles[t], x1[:, c]).then_inc(x1_stored[c], 16)
                            sp.wait_ge(xn2_done, t + 1)
                            sp.dma_start(row_tiles[t, :, 0:DIM], xn2[:, c]).then_inc(xn2_stored[c], 16)
                            landed = 16 * (2 * (n - 1) + u // 2 + 1)
                            sp.wait_ge(x1_stored[c], landed)
                            sp.wait_ge(xn2_stored[c], landed)
                            sp.sem_inc(out_free, 1)
                plan(sp, body)

            @block.tensor
            def _(pe):
                def three(out, a_hi, a_lo, b_hi, b_lo, start=True, stop=True, **kw):
                    nc.tensor.matmul(out, a_hi, b_hi, start=start, stop=False, **kw)
                    nc.tensor.matmul(out, a_hi, b_lo, start=False, stop=False, **kw)
                    return nc.tensor.matmul(out, a_lo, b_hi, start=False, stop=stop, **kw)

                def turn(use, src, chunks=KD):
                    index, bank = use
                    after(pe, turn_lo, index - 1)
                    for k in range(chunks):
                        mm = nc.tensor.transpose(ps[:, bank, k * P:(k + 1) * P], src[:, k * P:(k + 1) * P],
                                                 keep["ident"][:])
                    mm.then_inc(turn_done, 1)

                def turn_tokens(t, u, use):
                    pe.wait_ge(xn_done, t + 1)
                    turn(use, xn[:, u, :])

                def query(i, pair, use, tokens):
                    index, bank = use
                    pe.wait_ge(turn_lo, tokens + 1)
                    pe.wait_ge(turn_lo, index - 1)
                    hb = BLOCK_ORDER[i]
                    cols = slice(hb * P, (hb + 1) * P)
                    for k in range(KD):
                        mm = three(ps[:, bank, 0:2 * P], att["wq_hi"][:, k, cols], att["wq_lo"][:, k, cols],
                                   xnT_hi[:, k, PAIRS[pair]], xnT_lo[:, k, PAIRS[pair]],
                                   start=(k == 0), stop=(k == KD - 1))
                    mm.then_inc(turn_done, 1)

                def score_products(n, b, u, i, query_use):
                    hb = BLOCK_ORDER[i]
                    if u % 2 == 0:
                        pe.wait_ge(turn_lo, query_use + 1)
                    after(pe, exp_done, 16 * n + 4 * u + i - 1)
                    q = slice(u * P, (u + 1) * P)
                    products = []
                    for half in range(2):
                        k = slice(half * HALF, (half + 1) * HALF)
                        products += parts(ps[:, 2 * (i % 2) + half, 0:HALF], q_hi[:, hb, q], q_lo[:, hb, q],
                                          att["k_hi"][:, b, hb, k], att["k_lo"][:, b, hb, k])
                    return products

                def value_products(b, chunks):
                    products = []
                    for c in chunks:
                        h0 = wide_first(c)
                        products += parts(ps[:, VALUE_BANK, h0 * V_DIM:h0 * V_DIM + WIDE_WIN], mixT_hi[:, c, :],
                                          mixT_lo[:, c, :], att["v_hi"][:, b, c, :], att["v_lo"][:, b, c, :],
                                          c == 0, c == CHUNKS - 1)
                    return products

                def parts(out, a_hi, a_lo, b_hi, b_lo, start=True, stop=True):
                    return [(out, a_hi, b_hi, start, False), (out, a_hi, b_lo, False, False),
                            (out, a_lo, b_hi, False, stop)]

                def beside(wide, narrow):
                    last = [None, None]
                    for w in range(max(len(wide), 1)):
                        if wide:
                            out, a, b, start, stop = wide[w]
                            last[0] = nc.tensor.matmul(out, a, b, start=start, stop=stop)
                        n = max(len(wide), 1)
                        for out, a, b, start, stop in narrow[w * len(narrow) // n:(w + 1) * len(narrow) // n]:
                            last[1] = nc.tensor.matmul(out, a, b, start=start, stop=stop, skip_group_check=True)
                    return last

                def turn_mix(t, uses):
                    pe.wait_ge(mix_done, 2 * t + 2)
                    for g in range(3):
                        turn(uses[g], mix[:, 4 * g * P:], min(4, CHUNKS - 4 * g))

                def projection(t, attn_use):
                    pe.wait_ge(turn_lo, attn_use + 1)
                    after(pe, xn2T_done, t)
                    products = []
                    for k in range(KD):
                        products += parts(ps[:, PROJECT_BANK, :], attnT_hi[:, k, :], attnT_lo[:, k, :],
                                          att["wp_hi"][:, k, :], att["wp_lo"][:, k, :], k == 0, k == KD - 1)
                    return products

                def turn_mix(uses, first):
                    for g, use in enumerate(uses, first):
                        turn(use, mix[:, 4 * g * P:], min(4, CHUNKS - 4 * g))

                def turn_router(t, c):
                    pe.wait_ge(xn2_done, t + 1)
                    for k in range(KD):
                        mm = nc.tensor.transpose(ps[:, PROJECT_BANK, k * P:(k + 1) * P],
                                                 xn2[:, c, k * P:(k + 1) * P], keep["ident"][:])
                    mm.then_inc(xn2T_psum, 1)

                def router(t, n):
                    pe.wait_ge(xn2T_done, t + 1)
                    pe.wait_ge(exp_done, 16 * n)
                    after(pe, logits_done, t)
                    for k in range(KD):
                        mm = nc.tensor.matmul(ps[:, 2, HALF:HALF + EXPERTS], xn2T[:, k, :], att["gate_w"][:, k, :],
                                              start=(k == 0), stop=(k == KD - 1), skip_group_check=True)
                    mm.then_inc(logits_psum, 1)

                def body(n, kind, b, b_two):
                    use = Turn(n, kind)
                    own = kind != TAIL
                    ahead = kind in (FIRST, MIDDLE)

                    def score(u, i, between=None, narrow=()):
                        wide = []
                        if own:
                            wide = score_products(n, b, u, i, use.query(kind, u, i) if u % 2 == 0 else None)
                        if between:
                            between()
                        last = beside(wide, narrow)
                        if own:
                            last[0].then_inc(scores_done, 1)
                        return last[1]

                    for u in range(SUB):
                        s = 4 * n + u
                        score(u, 0)
                        pair, blocks = 1 - u // 2, (u % 2 * 2, u % 2 * 2 + 1)
                        tokens = use.start - 1 if u < 2 else use.at("tokens", 1)[0] if ahead else None
                        if has_queries(kind, u):
                            query(blocks[0], pair, use.at("query", u, 0), tokens)
                        if has(kind, u, 2):
                            pe.wait_ge(mix_done, 2 * (s - 2) + 2)
                            turn_mix([use.at("mix", u, 0)], 0)
                        score(u, 1)
                        if has(kind, u, 2):
                            turn_mix([use.at("mix", u, 1)], 1)
                        if has_queries(kind, u):
                            query(blocks[1], pair, use.at("query", u, 1), tokens)
                        if has(kind, u, 2):
                            turn_mix([use.at("mix", u, 2)], 2)
                        if has(kind, u, 4):
                            turn_router(s - 4, u % 2)
                        b_values, values = (b if u >= 2 else b_two), []
                        if has(kind, u, 2):
                            pe.wait_ge(turn_lo, use.at("mix", u, 1)[0] + 1)
                            after(pe, attn_done, s - 2)
                            values = value_products(b_values, range(CHUNKS_FIRST))
                        score(u, 2, narrow=values)
                        if has(kind, u, 3):
                            pe.wait_ge(attn_done, s - 3 + 1)
                            turn(use.at("attn", u), attn[:])
                        score(u, 3, (lambda: router(s - 4, n)) if has(kind, u, 4) else None)
                        if ahead:
                            turn_tokens(s + 4, u, use.at("tokens", u))
                        wide = projection(s - 3, use.at("attn", u)[0]) if has(kind, u, 3) else []
                        if has(kind, u, 2):
                            pe.wait_ge(turn_lo, use.at("mix", u, 2)[0] + 1)
                            values = value_products(b_values, range(CHUNKS_FIRST, CHUNKS))
                        last = beside(wide, values)
                        if has(kind, u, 3):
                            last[0].then_inc(projected, 1)
                        if has(kind, u, 2):
                            last[1].then_inc(values_done, 1)

                mid = MACROS // BATCH
                for k in range(SUB):
                    turn_tokens(k, k, (k, TURN_BANK + k % 2))
                for i in range(BLOCKS):
                    query(i, 0, (SUB + i, TURN_BANK + (SUB + i) % 2), SUB - 1)
                body(0, FIRST, 0, 0)
                with pe.Fori(1, mid) as n:
                    body(n, MIDDLE, 0, 0)
                body(mid, MIDDLE, 1, 0)
                with pe.Fori(mid + 1, MACROS - 1) as n:
                    body(n, MIDDLE, 1, 1)
                body(MACROS - 1, LAST, 1, 1)
                body(MACROS, TAIL, 1, 1)

            @block.scalar
            def _(act):
                def hi_part(dst, src, use, scale=1.0):
                    act.wait_ge(turn_done, use[0] + 1)
                    nc.scalar.activation(dst, src, ACT.Copy, scale=scale).then_inc(turn_hi, 1)

                def tokens_hi(u, use):
                    hi_part(xnT_hi[:, :, u * P:(u + 1) * P], split_view(use[1]), use)

                def query_hi(i, pair, use):
                    hi_part(q_hi[:, BLOCK_ORDER[i], PAIRS[pair]], ps[:, use[1], 0:2 * P], use, Q_SCALE)

                def exponentials(s, c, i):
                    hb = BLOCK_ORDER[i]
                    act.wait_ge(max_done, 4 * s + i + 1)
                    after(act, mix_done, 2 * (s - 2) + i // 2 + 1)
                    for h in range(HEADS_PER_BLOCK):
                        head = hb * HEADS_PER_BLOCK + h
                        e = nc.scalar.activation(probs[:, c, head, :],
                                                 ps[:, 2 * (i % 2) + h // 4, h % 4 * KEYS:(h % 4 + 1) * KEYS],
                                                 ACT.Exp, bias=neg_max[:, c, head:head + 1],
                                                 accum_out=sums[:, c, head:head + 1])
                    e.then_inc(exp_done, 1)

                def mix_hi(uses, first):
                    for g, use in enumerate(uses, first):
                        c = slice(4 * g, min(4 * g + 4, CHUNKS))
                        hi_part(mixT_hi[:, c, :], split_view(use[1], (c.stop - c.start) * P), use)

                def body(n, kind):
                    use = Turn(n, kind)
                    own = kind != TAIL
                    ahead = kind in (FIRST, MIDDLE)
                    for u in range(SUB):
                        s = 4 * n + u
                        pair, blocks = 1 - u // 2, (u % 2 * 2, u % 2 * 2 + 1)
                        if has(kind, u, 1):
                            exponentials(s - 1, (u - 1) % 2, 3)
                        if has(kind, u, 3):
                            act.wait_ge(values_done, s - 3 + 1)
                            nc.scalar.activation(squares[:], ps[:, VALUE_BANK, :], ACT.Square).then_inc(squared, 1)
                        if has_queries(kind, u):
                            query_hi(blocks[0], pair, use.at("query", u, 0))
                        if has(kind, u, 2):
                            mix_hi([use.at("mix", u, g) for g in range(2)], 0)
                        if own:
                            exponentials(s, u % 2, 0)
                        if has_queries(kind, u):
                            query_hi(blocks[1], pair, use.at("query", u, 1))
                        if has(kind, u, 2):
                            mix_hi([use.at("mix", u, 2)], 2)
                        if has(kind, u, 4):
                            act.wait_ge(xn2T_psum, s - 4 + 1)
                            nc.scalar.activation(xn2T[:], split_view(PROJECT_BANK), ACT.Copy).then_inc(xn2T_done, 1)
                        if own:
                            exponentials(s, u % 2, 1)
                        if has(kind, u, 3):
                            hi_part(attnT_hi[:], split_view(use.at("attn", u)[1]), use.at("attn", u))
                        if own:
                            exponentials(s, u % 2, 2)
                        if ahead:
                            tokens_hi(u, use.at("tokens", u))

                for k in range(SUB):
                    tokens_hi(k, (k, TURN_BANK + k % 2))
                for i in range(BLOCKS):
                    query_hi(i, 0, (SUB + i, TURN_BANK + (SUB + i) % 2))
                plan(act, body)

            @block.vector
            def _(dve):
                def lo_part(dst, src, hi, use):
                    dve.wait_ge(turn_hi, use[0] + 1)
                    nc.vector.tensor_tensor(dst, src, hi.bitcast(F32), ALU.subtract).then_inc(turn_lo, 1)

                def layer_norm(n, u):
                    dve.wait_ge(x_loaded[u], 16 * (n + 1))
                    nc.vector.bn_stats(stats[:, u, :], x_in[:, u, :])
                    dve.drain()
                    nc.vector.bn_aggr(mean_var[:, u, :], stats[:, u, :]).then_inc(ln1_stats, 1)

                def normalise(t, u):
                    dve.wait_ge(ln1_rstd, t + 1)
                    nc.vector.tensor_scalar(xn[:, u, :], x_in[:, u, :], mean_var[:, u, 0:1],
                                            rstd[:, u:u + 1], ALU.subtract, ALU.mult).then_inc(xn_done, 1)

                def tokens_lo(u, use):
                    cols = slice(u * P, (u + 1) * P)
                    lo_part(xnT_lo[:, :, cols], split_view(use[1]), xnT_hi[:, :, cols], use)

                def query_lo(i, pair, use):
                    hb, cols = BLOCK_ORDER[i], PAIRS[pair]
                    dve.wait_ge(turn_hi, use[0] + 1)
                    nc.vector.scalar_tensor_tensor(q_lo[:, hb, cols], ps[:, use[1], 0:2 * P], Q_SCALE,
                                                   q_hi[:, hb, cols].bitcast(F32), ALU.mult,
                                                   ALU.subtract).then_inc(turn_lo, 1)

                def save_logits(t):
                    dve.wait_ge(logits_psum, t + 1)
                    nc.vector.tensor_copy(keep["logits"][:, :, bass.ds(t, 1)].rearrange("p e t -> p (e t)"),
                                          ps[:, 2, HALF:HALF + EXPERTS]).then_inc(logits_done, 1)

                def maxima(s, c, i, logits_of=None):
                    hb = BLOCK_ORDER[i]
                    dve.wait_ge(scores_done, 4 * s + i + 1)
                    if logits_of is not None:
                        save_logits(logits_of)
                    heads = slice(hb * HEADS_PER_BLOCK, (hb + 1) * HEADS_PER_BLOCK)
                    nc.vector.tensor_reduce(
                        neg_max[:, c, heads].rearrange("p (a h) -> p a h", a=2),
                        ps[:, 2 * (i % 2):2 * (i % 2) + 2, 0:HALF].rearrange("p a (h k) -> p a h k", k=KEYS),
                        X, ALU.max, negate=True).then_inc(max_done, 1)

                def recip_half(s, c, half):
                    dve.wait_ge(exp_done, 4 * s + 2 * half + 2)
                    second = slice(HEADS + half * 8, HEADS + half * 8 + 8)
                    heads = [ap[:, c, :].rearrange("p (a h) -> p a h", a=2)[:, :, half * 8:half * 8 + 8]
                             for ap in (recips, sums)]
                    nc.vector.reciprocal(*heads)
                    dve.drain()
                    nc.vector.tensor_scalar(recips[:, c, second], recips[:, c, second],
                                            att["neg_lambda"][:, 0:1], None, ALU.mult).then_inc(recip_done, 1)

                def mix_half(s, c, half, turned):
                    first = slice(half * 8, half * 8 + 8)
                    second = slice(HEADS + half * 8, HEADS + half * 8 + 8)
                    dve.wait_ge(scaled, 2 * s + half + 1)
                    after(dve, turn_done, turned)
                    nc.vector.tensor_tensor(
                        mix[:, half * 8 * KEYS:(half + 1) * 8 * KEYS].rearrange("p (h k) -> p h k", k=KEYS),
                        probs[:, c, first, :], probs[:, c, second, :], ALU.add).then_inc(mix_done, 1)

                def mix_lo(uses, first):
                    for g, use in enumerate(uses, first):
                        c = slice(4 * g, min(4 * g + 4, CHUNKS))
                        lo_part(mixT_lo[:, c, :], split_view(use[1], (c.stop - c.start) * P),
                                mixT_hi[:, c, :], use)

                def mean_square(t):
                    dve.wait_ge(squared, t + 1)
                    nc.vector.tensor_reduce(head_ms[:], squares[:].rearrange("p (h d) -> p h d", d=V_DIM),
                                            X, ALU.add).then_inc(ms_done, 1)

                def head_norm(t):
                    dve.wait_ge(rms_done, t + 1)
                    nc.vector.tensor_tensor(attn[:].rearrange("p (h d) -> p h d", d=V_DIM),
                                            ps[:, VALUE_BANK, :].rearrange("p (h d) -> p h d", d=V_DIM),
                                            head_rms[:].unsqueeze(2).to_broadcast([P, HEADS, V_DIM]),
                                            ALU.mult).then_inc(attn_done, 1)

                def residual(t, c):
                    dve.wait_ge(projected, t + 1)
                    dve.wait_ge(res_ready, t + 1)
                    dve.wait_ge(out_free, t + 1)
                    nc.vector.tensor_tensor(x1[:, c], ps[:, PROJECT_BANK, :], x_res[:, c], ALU.add)
                    dve.drain()
                    nc.vector.bn_stats(stats2[:], x1[:, c]).then_inc(x1_done, 1)
                    dve.drain()
                    nc.vector.bn_aggr(mean_var2[:], stats2[:]).then_inc(ln2_stats, 1)

                def normalise2(t, c):
                    dve.wait_ge(ln2_rstd, t + 1)
                    nc.vector.tensor_scalar(xn2[:, c], x1[:, c], mean_var2[:, 0:1], rstd2[:, 0:1],
                                            ALU.subtract, ALU.mult).then_inc(xn2_done, 1)

                def body(n, kind):
                    use = Turn(n, kind)
                    own = kind != TAIL
                    ahead = kind in (FIRST, MIDDLE)
                    for u in range(SUB):
                        s = 4 * n + u
                        pair, blocks = 1 - u // 2, (u % 2 * 2, u % 2 * 2 + 1)
                        turned = use.at("mix", u, 2)[0] + 1 if has(kind, u, 2) else 0
                        if own:
                            maxima(s, u % 2, 0)
                        if has(kind, u, 3):
                            mean_square(s - 3)
                        if has_queries(kind, u):
                            query_lo(blocks[0], pair, use.at("query", u, 0))
                        if has(kind, u, 2):
                            mix_lo([use.at("mix", u, 0)], 0)
                        if has(kind, u, 4):
                            residual(s - 4, u % 2)
                        if has(kind, u, 2):
                            mix_lo([use.at("mix", u, 1)], 1)
                        if own:
                            maxima(s, u % 2, 1)
                        if has(kind, u, 4):
                            normalise2(s - 4, u % 2)
                        if has(kind, u, 3):
                            head_norm(s - 3)
                        if has_queries(kind, u):
                            query_lo(blocks[1], pair, use.at("query", u, 1))
                        if has(kind, u, 2):
                            mix_lo([use.at("mix", u, 2)], 2)
                        if has(kind, u, 1):
                            recip_half(s - 1, (u - 1) % 2, 1)
                            mix_half(s - 1, (u - 1) % 2, 0, turned)
                        if ahead:
                            layer_norm(n + 1, u)
                        if own:
                            maxima(s, u % 2, 2)
                        if has(kind, u, 1):
                            mix_half(s - 1, (u - 1) % 2, 1, turned)
                        if ahead:
                            normalise(s + 4, u)
                        if has(kind, u, 3):
                            lo_part(attnT_lo[:], split_view(use.at("attn", u)[1]), attnT_hi[:], use.at("attn", u))
                        logits_of = s - 4 if has(kind, u, 4) else None
                        if own:
                            maxima(s, u % 2, 3, logits_of)
                            recip_half(s, u % 2, 0)
                        elif logits_of is not None:
                            save_logits(logits_of)
                        if ahead:
                            tokens_lo(u, use.at("tokens", u))

                nc.vector.memset(mix[:, HEADS * KEYS:], 0.0)
                for k in range(SUB):
                    layer_norm(0, k)
                for k in range(SUB):
                    normalise(k, k)
                for k in range(SUB):
                    tokens_lo(k, (k, TURN_BANK + k % 2))
                for i in range(BLOCKS):
                    query_lo(i, 0, (SUB + i, TURN_BANK + (SUB + i) % 2))
                plan(dve, body)

            @block.gpsimd
            def _(pool):
                def power(dst, src, w):
                    pool.drain()
                    return nc.gpsimd.tensor_tensor(dst, src, minus_half[:, 0:w], ALU.pow)

                def ln1(t, u):
                    hold(pool, ln1_stats, t + 1, pool_passed)
                    nc.gpsimd.tensor_scalar(var_eps[:, u:u + 1], mean_var[:, u, 1:2], EPS, None, ALU.add)
                    power(rstd[:, u:u + 1], var_eps[:, u:u + 1], 1).then_inc(ln1_rstd, 1)

                def scale(s, c, half):
                    h = slice(half * 8, half * 8 + 8)
                    soft = probs[:, c].rearrange("p (a h) k -> p a h k", a=2)[:, :, h, :]
                    factors = recips[:, c].rearrange("p (a h) -> p a h", a=2)[:, :, h]
                    pool.wait_ge(recip_done, 2 * s + half + 1)
                    nc.gpsimd.tensor_tensor(soft, soft, factors.unsqueeze(3).to_broadcast([P, 2, 8, KEYS]),
                                            ALU.mult).then_inc(scaled, 1)

                def add_bias(n, u):
                    c = (u - 3) % 2
                    pool.wait_ge(res_loaded[c], 16 * (2 * n + (u - 3) // 2 + 1))
                    nc.gpsimd.tensor_tensor(x_res[:, c], x_res[:, c], att["bias"][:], ALU.add).then_inc(res_ready, 1)

                def body(n, kind):
                    for u in range(SUB):
                        s = 4 * n + u
                        if has(kind, u, 3):
                            hold(pool, ms_done, s - 3 + 1, pool_passed)
                            nc.gpsimd.tensor_scalar(ms_eps[:], head_ms[:], 1.0 / V_DIM, EPS, ALU.mult, ALU.add)
                            power(head_rms[:], ms_eps[:], HEADS).then_inc(rms_done, 1)
                        if has(kind, u, 4):
                            hold(pool, ln2_stats, s - 4 + 1, pool_passed)
                            nc.gpsimd.tensor_scalar(var_eps2[:], mean_var2[:, 1:2], EPS, None, ALU.add)
                            power(rstd2[:], var_eps2[:], 1).then_inc(ln2_rstd, 1)
                        if has(kind, u, 1):
                            scale(s - 1, (u - 1) % 2, 1)
                        if kind in (FIRST, MIDDLE):
                            ln1(s + 4, u)
                        if has(kind, u, 3):
                            add_bias(n, u)
                        if kind != TAIL:
                            scale(s, u % 2, 0)

                nc.gpsimd.memset(minus_half[:], -0.5)
                for k in range(SUB):
                    ln1(k, k)
                plan(pool, body)


def route(nc, io, ps, keep, raw_loaded):
    with ExitStack() as ctx:
        def sb(name, shape, dt=F32):
            return ctx.enter_context(nc.sbuf_tensor(name, shape, dt))

        def sem(name):
            return ctx.enter_context(nc.semaphore(name))

        same_group, before_in_group = sb("same_group", [P, P]), sb("before_in_group", [P, P])
        top = sb("top", [P, TILES])
        shifted = sb("shifted", [P, EXPERTS, TILES])
        expo = sb("expo", [P, EXPERTS, TILES])
        total, inverse = sb("total", [P, TILES]), sb("inverse", [P, TILES])
        affinity = sb("affinity", [P, EXPERTS, TILES])
        by_token = sb("by_token", [P, TILES, EXPERTS])
        aff = sb("aff", [P, SETS, P])
        digits, trial, enough = (sb("digits", [P, 3, SETS], U32), sb("trial", [P, 3, SETS], U32),
                                 sb("enough", [P, 3, SETS], U32))
        cut = sb("cut", [P, SETS], U32)
        flags = sb("flags", [P, 3, SETS, P])
        count = sb("count", [P, 3, SETS])
        above, equal = sb("above", [P, SETS, P]), sb("equal", [P, SETS, P])
        counts = sb("counts", [P, 2, SETS])
        wanted, equal_before = sb("wanted", [P, SETS]), sb("equal_before", [P, SETS])
        ones = sb("ones", [P, P])
        rank, kept, chosen = sb("rank", [P, SETS, P]), sb("kept", [P, SETS, P]), sb("chosen", [P, SETS, P])
        running = sb("running", [P, SETS, P])
        chosen_before = sb("chosen_before", [P, SETS])
        prefix = sb("prefix", [P, SETS, P], F16)

        loaded, exp_ready, exp_done = sem("consts_loaded"), sem("exp_ready"), sem("expo_done")
        aff_done, aff_turned = sem("aff_done"), sem("aff_turned")
        counted, summed, totals_ready, totals_done = (sem("counted"), sem("summed"), sem("totals_ready"),
                                                      sem("totals_done"))
        by_token_done, chosen_counted, chosen_summed = (sem("by_token_done"), sem("chosen_counted"),
                                                        sem("chosen_summed"))
        prefix_done, stored = sem("prefix_done"), sem("stored")

        with nc.Block() as block:
            @block.sync
            def _(sp):
                sp.dma_start(same_group[:], io["same_group"]).then_inc(loaded, 16)
                sp.dma_start(before_in_group[:], io["before_in_group"]).then_inc(loaded, 16)
                sp.dma_start(digits[:], io["top_digits"]).then_inc(loaded, 16)
                for j in range(GJ):
                    sp.dma_start(keep["raw"][:, j, :], io["weights"][0, j]).then_inc(raw_loaded[j], 16)
                sp.wait_ge(by_token_done, 1)
                sp.dma_start(io["rows"].rearrange("(t p) c -> p t c", p=P)[:, :, DIM:ROW],
                             by_token[:]).then_inc(stored, 16)
                sp.wait_ge(prefix_done, 1)
                sp.dma_start(io["prefix"].rearrange("(s q) t -> q s t", s=SETS), prefix[:]).then_inc(stored, 16)
                sp.wait_ge(stored, 32)

            @block.scalar
            def _(act):
                act.wait_ge(exp_ready, 1)
                nc.scalar.activation(expo[:], shifted[:], ACT.Exp).then_inc(exp_done, 1)

            @block.tensor
            def _(pe):
                pe.wait_ge(aff_done, 1)
                for s in range(SETS):
                    mm = nc.tensor.transpose(ps[:, 0, s * P:(s + 1) * P],
                                             affinity[:, s * SET_E:(s + 1) * SET_E, :].rearrange("p e t -> p (e t)"),
                                             keep["ident"][:])
                mm.then_inc(aff_turned, 1)
                pe.wait_ge(loaded, 48)
                with pe.Fori(0, DIGITS // DIGITS_PER_STEP) as i:
                    for d in range(DIGITS_PER_STEP):
                        pe.wait_ge(counted, DIGITS_PER_STEP * i + d + 1)
                        nc.tensor.matmul(ps[:, 1, 0:3 * SETS], same_group[:],
                                         count[:].rearrange("p v s -> p (v s)")).then_inc(summed, 1)
                pe.wait_ge(totals_ready, 1)
                nc.tensor.matmul(ps[:, 2, 0:SETS], same_group[:], counts[:, 0, :])
                nc.tensor.matmul(ps[:, 3, 0:SETS], before_in_group[:], counts[:, 1, :]).then_inc(totals_done, 1)
                pe.wait_ge(chosen_counted, 1)
                nc.tensor.matmul(ps[:, 4, 0:SETS], before_in_group[:], running[:, :, P - 1]).then_inc(
                    chosen_summed, 1)

            @block.vector
            def _(dve):
                nc.vector.memset(ones[:], 1.0)
                nc.vector.memset(cut[:], 0)
                wide = [P, EXPERTS, TILES]
                nc.vector.tensor_reduce(top[:], keep["logits"][:].rearrange("p e t -> p t e"), X, ALU.max)
                dve.drain()
                nc.vector.tensor_tensor(shifted[:], keep["logits"][:], top[:].unsqueeze(1).to_broadcast(wide),
                                        ALU.subtract).then_inc(exp_ready, 1)
                dve.wait_ge(exp_done, 1)
                nc.vector.tensor_reduce(total[:], expo[:].rearrange("p e t -> p t e"), X, ALU.add)
                dve.drain()
                nc.vector.reciprocal(inverse[:], total[:])
                dve.drain()
                nc.vector.tensor_tensor(affinity[:], expo[:], inverse[:].unsqueeze(1).to_broadcast(wide),
                                        ALU.mult).then_inc(aff_done, 1)
                dve.drain()
                nc.vector.tensor_copy(by_token[:], affinity[:].rearrange("p e t -> p t e")).then_inc(by_token_done, 1)
                dve.wait_ge(aff_turned, 1)
                nc.vector.tensor_copy(aff[:].rearrange("p s t -> p (s t)"), ps[:, 0, 0:SETS * P])
                dve.wait_ge(loaded, 48)
                dve.drain()
                with dve.Fori(0, DIGITS // DIGITS_PER_STEP) as i:
                    for d in range(DIGITS_PER_STEP):
                        nc.vector.tensor_tensor(trial[:], cut[:].unsqueeze(1).to_broadcast([P, 3, SETS]), digits[:],
                                                ALU.bitwise_or)
                        dve.drain()
                        for v in range(3):
                            for s in range(SETS):
                                c = nc.vector.tensor_scalar(flags[:, v, s, :], aff[:, s, :],
                                                            trial[:, v, s:s + 1].bitcast(F32), 0.0, ALU.is_ge,
                                                            ALU.add, accum_out=count[:, v, s:s + 1])
                        c.then_inc(counted, 1)
                        nc.vector.tensor_single_scalar(digits[:], digits[:], 2, ALU.logical_shift_right)
                        dve.wait_ge(summed, DIGITS_PER_STEP * i + d + 1)
                        nc.vector.tensor_scalar(enough[:].rearrange("p v s -> p (v s)"), ps[:, 1, 0:3 * SETS],
                                                float(CAP), None, ALU.is_ge)
                        for v in range(3):
                            dve.drain()
                            nc.vector.copy_predicated(cut[:], enough[:, v], trial[:, v])
                        dve.drain()
                for s in range(SETS):
                    level = cut[:, s:s + 1].bitcast(F32)
                    nc.vector.tensor_scalar(above[:, s, :], aff[:, s, :], level, 0.0, ALU.is_gt, ALU.add,
                                            accum_out=counts[:, 0, s:s + 1])
                    c = nc.vector.tensor_scalar(equal[:, s, :], aff[:, s, :], level, 0.0, ALU.is_equal, ALU.add,
                                                accum_out=counts[:, 1, s:s + 1])
                c.then_inc(totals_ready, 1)
                dve.wait_ge(totals_done, 1)
                nc.vector.tensor_scalar(wanted[:], ps[:, 2, 0:SETS], -1.0, float(CAP), ALU.mult, ALU.add)
                nc.vector.tensor_copy(equal_before[:], ps[:, 3, 0:SETS])
                dve.drain()
                for s in range(SETS):
                    nc.vector.tensor_tensor_scan(rank[:, s, :], ones[:], equal[:, s, :], equal_before[:, s:s + 1],
                                                 ALU.mult, ALU.add)
                dve.drain()
                for s in range(SETS):
                    nc.vector.scalar_tensor_tensor(kept[:, s, :], rank[:, s, :], wanted[:, s:s + 1],
                                                   equal[:, s, :], ALU.is_le, ALU.mult)
                dve.drain()
                nc.vector.tensor_tensor(chosen[:], kept[:], above[:], ALU.add)
                dve.drain()
                for s in range(SETS):
                    c = nc.vector.tensor_tensor_scan(running[:, s, :], ones[:], chosen[:, s, :], 0.0,
                                                     ALU.mult, ALU.add)
                c.then_inc(chosen_counted, 1)
                dve.wait_ge(chosen_summed, 1)
                nc.vector.tensor_copy(chosen_before[:], ps[:, 4, 0:SETS])
                dve.drain()
                for s in range(SETS):
                    c = nc.vector.tensor_scalar(prefix[:, s, :], running[:, s, :], chosen_before[:, s:s + 1],
                                                None, ALU.add)
                c.then_inc(prefix_done, 1)


DOWN_BANK = 4
DOWN_USES = XT + GROUPS * XT


def experts(nc, io, ps, keep, raw_loaded):
    with ExitStack() as ctx:
        def sb(name, shape, dt=F32):
            return ctx.enter_context(nc.sbuf_tensor(name, shape, dt))

        def sem(name):
            return ctx.enter_context(nc.semaphore(name))

        raw = keep["raw"]
        gu_hi, gu_lo = sb("gu_hi", [P, GJ, 2, KD, P], F32R), sb("gu_lo", [P, GJ, 2, KD, P], F32R)
        down_hi, down_lo = sb("down_hi", [P, GJ, DIM], F32R), sb("down_lo", [P, GJ, DIM], F32R)
        act_out = sb("act_out", [P, 2, CAP])
        h_hi, h_lo = sb("h_hi", [P, BATCH, GJ, CAP], F32R), sb("h_lo", [P, BATCH, GJ, CAP], F32R)
        gathered = sb("gathered", [P, XT, ROW])
        xT_hi, xT_lo = sb("xT_hi", [P, KD, BATCH * CAP], F32R), sb("xT_lo", [P, KD, BATCH * CAP], F32R)
        y = sb("y", [P, XT, DIM])
        gates = sb("gates", [P, XT])
        prefix = sb("prefix_rows", [P, BATCH, SEQ], F16)
        flags = sb("slot_flags", [P, SEQ], F16)
        found = sb("found", [P, XT])
        take, put = sb("take", [P, XT], U32), sb("put", [P, XT], U32)

        gu_hi_done, gu_lo_done, gu_used = sem("gu_hi_done"), sem("gu_lo_done"), sem("gu_used")
        down_hi_done, down_lo_done, down_used = sem("down_hi_done"), sem("down_lo_done"), sem("down_used")
        pair_done, silu_done, h_done, h_hi_done, h_lo_done = (sem("pair_done"), sem("silu_done"), sem("h_done"),
                                                              sem("h_hi_done"), sem("h_lo_done"))
        h_used = sem("h_used")
        bank_done, x_hi_done, bank_free = sem("bank_done"), sem("x_hi_done"), sem("bank_free")
        prefix_loaded, listed, gates_read = sem("prefix_loaded"), sem("listed"), sem("gates_read")
        tokens_gathered = [sem(f"tokens_gathered{t}") for t in range(XT)]
        y_ready, put_ready = sem("y_ready"), sem("put_ready")
        added = [sem(f"added{t}") for t in range(XT)]
        added_all = sem("added_all")
        pool_passed = sem("pool_passed")

        w = io["weights"]
        out_rows, rows = io["out"], io["rows"]

        def prefix_rows(e):
            return io["prefix"].rearrange("(e q) t -> e (q t)", e=EXPERTS)[bass.ds(e, 1), :]

        def plan(eng, body):
            body(0, True, False)
            with eng.Fori(1, EXPERTS - 1) as e:
                body(e, False, False)
            body(EXPERTS - 1, False, True)

        def groups(eng, group):
            group(0)
            with eng.Fori(1, GROUPS) as g:
                group(g)

        with nc.Block() as block:
            @block.sync
            def _(sp):
                def body(e, first, last):
                    if not last:
                        sp.wait_ge(listed, GROUPS * (e + 1))
                        sp.dma_start(prefix[:].rearrange("p b t -> p (b t)"),
                                     prefix_rows(e + 1).to_broadcast([P, BATCH * SEQ])).then_inc(prefix_loaded, 16)

                    def group(g):
                        n = GROUPS * e + g
                        if isinstance(n, int) and n == 0:
                            return
                        for j in range(GJ):
                            after(sp, down_lo_done, GJ * (n - 1) + j + 1)
                            sp.dma_start(raw[:, j, :], w[n, j]).then_inc(raw_loaded[j], 16)
                    groups(sp, group)

                sp.dma_start(prefix[:].rearrange("p b t -> p (b t)"),
                             prefix_rows(0).to_broadcast([P, BATCH * SEQ])).then_inc(prefix_loaded, 16)
                plan(sp, body)

            @block.tensor
            def _(pe):
                def three(out, a_hi, a_lo, b_hi, b_lo, start, stop):
                    nc.tensor.matmul(out, a_hi, b_hi, start=start, stop=False)
                    nc.tensor.matmul(out, a_hi, b_lo, start=False, stop=False)
                    return nc.tensor.matmul(out, a_lo, b_hi, start=False, stop=stop)

                def body(e, first, last):
                    uses = DOWN_USES * e

                    def turn_tokens(tiles):
                        for t in tiles:
                            pe.wait_ge(tokens_gathered[t], 16 * (e + 1))
                            after(pe, bank_free, uses + t - 3)
                            for k in range(KD):
                                mm = nc.tensor.transpose(ps[:, DOWN_BANK + t % 4, k * P:(k + 1) * P],
                                                         gathered[:, t, k * P:(k + 1) * P], keep["ident"][:])
                            mm.then_inc(bank_done, 1)

                    turn_tokens(range(SLOT_TILES))

                    def group(g):
                        n = GROUPS * e + g
                        for b in range(BATCH):
                            after_x = uses + SLOT_TILES * (b + 1)
                            if isinstance(g, int):
                                pe.wait_ge(bank_free, after_x)
                            for j in range(GJ):
                                pair = XT * n + GJ * b + j
                                if b == 0:
                                    if j == GJ - 1 and isinstance(g, int):
                                        turn_tokens(range(SLOT_TILES, XT))
                                    pe.wait_ge(gu_lo_done, GJ * n + j + 1)
                                after(pe, silu_free, pair - 1)
                                for m in range(2):
                                    for k in range(KD):
                                        cols = slice(b * CAP, (b + 1) * CAP)
                                        mm = three(ps[:, 2 * (j % 2) + m, :], gu_hi[:, j, m, k, :],
                                                   gu_lo[:, j, m, k, :], xT_hi[:, k, cols], xT_lo[:, k, cols],
                                                   k == 0, k == KD - 1)
                                mm.then_inc(pair_done, 1)
                        for b in range(BATCH):
                            pe.wait_ge(h_lo_done, XT * n + GJ * (b + 1))
                            if b == 0:
                                pe.wait_ge(down_lo_done, GJ * (n + 1))
                            for t in range(SLOT_TILES):
                                use = uses + XT + XT * g + SLOT_TILES * b + t
                                pe.wait_ge(bank_free, use - 3)
                                cols = slice(t * P, (t + 1) * P)
                                for j in range(GJ):
                                    mm = three(ps[:, DOWN_BANK + t, :], h_hi[:, b, j, cols], h_lo[:, b, j, cols],
                                               down_hi[:, j, :], down_lo[:, j, :], j == 0, j == GJ - 1)
                                mm.then_inc(bank_done, 1)
                    groups(pe, group)

                silu_free = h_done
                plan(pe, body)

            @block.scalar
            def _(act):
                def body(e, first, last):
                    uses = DOWN_USES * e

                    def tokens_hi(tiles):
                        for t in tiles:
                            act.wait_ge(bank_done, uses + t + 1)
                            nc.scalar.activation(xT_hi[:, :, t * P:(t + 1) * P],
                                                 ps[:, DOWN_BANK + t % 4, :].rearrange("p (k t) -> p k t", t=P),
                                                 ACT.Copy).then_inc(x_hi_done, 1)

                    def group(g):
                        n = GROUPS * e + g
                        for j in range(GJ):
                            act.wait_ge(raw_loaded[j], 16 * (n + 1))
                            after(act, pair_done, XT * (n - 1) + GJ + j + 1)
                            nc.scalar.activation(gu_hi[:, j].rearrange("p m k i -> p (m k i)"), raw[:, j, 0:GU],
                                                 ACT.Copy).then_inc(gu_hi_done, 1)
                        if isinstance(g, int):
                            tokens_hi(range(SLOT_TILES))
                        for b in range(BATCH):
                            after(act, bank_done, uses + XT * (g + 1) - XT + SLOT_TILES * (b + 1)
                                  if not (isinstance(g, int)) else uses - XT + SLOT_TILES * (b + 1))
                            for j in range(GJ):
                                pair = XT * n + GJ * b + j
                                if b == 0 and j == GJ - 1 and isinstance(g, int):
                                    tokens_hi(range(SLOT_TILES, XT))
                                act.wait_ge(pair_done, pair + 1)
                                after(act, h_lo_done, pair - 1)
                                nc.scalar.activation(act_out[:, j % 2, :], ps[:, 2 * (j % 2), :],
                                                     ACT.Silu).then_inc(silu_done, 1)
                                act.wait_ge(h_done, pair + 1)
                                nc.scalar.activation(h_hi[:, b, j, :], act_out[:, j % 2, :],
                                                     ACT.Copy).then_inc(h_hi_done, 1)
                                if b == 0:
                                    if j == 0:
                                        after(act, bank_done, down_uses_before(uses, g))
                                    nc.scalar.activation(down_hi[:, j, :], raw[:, j, GU:WCOLS],
                                                         ACT.Copy).then_inc(down_hi_done, 1)
                    groups(act, group)
                plan(act, body)

            @block.vector
            def _(dve):
                def list_tokens(i, g):
                    nc.vector.tensor_scalar(flags[:], prefix[:, i, :], keep["slot_number"][:, bass.ds(g, 1)],
                                            0.0, ALU.is_le, ALU.add,
                                            accum_out=found[:, bass.ds(SLOT_TILES * i + g, 1)])
                    dve.drain()

                def list_group(e, g):
                    if isinstance(g, int):
                        dve.wait_ge(prefix_loaded, 16 * (e + 1))
                    for i in range(BATCH):
                        list_tokens(i, g)
                    for i in range(BATCH):
                        col = bass.ds(SLOT_TILES * i + g, 1)
                        a = nc.vector.tensor_scalar(take[:, col], found[:, col], float(SEQ * i), None, ALU.add)
                    a.then_inc(listed, 1)

                def scale_by_gates():
                    dve.drain()
                    for t in range(XT):
                        nc.vector.tensor_scalar(y[:, t, :], y[:, t, :], gates[:, t:t + 1], None,
                                                ALU.mult).then_inc(y_ready, 1)
                    dve.drain()

                def body(e, first, last):
                    uses = DOWN_USES * e

                    def tokens_lo(tiles):
                        for t in tiles:
                            cols = slice(t * P, (t + 1) * P)
                            dve.wait_ge(x_hi_done, XT * e + t + 1)
                            nc.vector.tensor_tensor(xT_lo[:, :, cols],
                                                    ps[:, DOWN_BANK + t % 4, :].rearrange("p (k t) -> p k t", t=P),
                                                    xT_hi[:, :, cols].bitcast(F32),
                                                    ALU.subtract).then_inc(bank_free, 1)

                    tokens_lo(range(SLOT_TILES))
                    if not first:
                        scale_by_gates()
                    for t in range(XT):
                        dve.wait_ge(tokens_gathered[t], 16 * (e + 1))
                    nc.vector.tensor_copy(gates[:], gathered[:, :, bass.ds(e + DIM, 1)].rearrange(
                        "p t c -> p (t c)")).then_inc(gates_read, 1)

                    def group(g):
                        n = GROUPS * e + g
                        for b in range(BATCH):
                            for j in range(GJ):
                                pair = XT * n + GJ * b + j
                                if b == 0 and j == GJ - 1 and isinstance(g, int):
                                    tokens_lo(range(SLOT_TILES, XT))
                                dve.wait_ge(silu_done, pair + 1)
                                nc.vector.tensor_tensor(act_out[:, j % 2, :], act_out[:, j % 2, :],
                                                        ps[:, 2 * (j % 2) + 1, :], ALU.mult).then_inc(h_done, 1)
                                dve.wait_ge(h_hi_done, pair + 1)
                                nc.vector.tensor_tensor(h_lo[:, b, j, :], act_out[:, j % 2, :],
                                                        h_hi[:, b, j, :].bitcast(F32),
                                                        ALU.subtract).then_inc(h_lo_done, 1)
                        if isinstance(g, int):
                            if not first:
                                dve.wait_ge(added_all, e)
                            nc.vector.tensor_copy(put[:], take[:]).then_inc(put_ready, 1)
                            dve.drain()
                        if not last:
                            list_group(e + 1, g)
                        for t in range(XT):
                            dve.wait_ge(bank_done, uses + XT + XT * g + t + 1)
                            bank = ps[:, DOWN_BANK + t % 4, :]
                            if isinstance(g, int):
                                a = nc.vector.tensor_copy(y[:, t, :], bank)
                            else:
                                a = nc.vector.tensor_tensor(y[:, t, :], y[:, t, :], bank, ALU.add)
                            a.then_inc(bank_free, 1)
                    groups(dve, group)

                list_group(0, 0)
                for g in range(1, GROUPS):
                    for i in range(BATCH):
                        list_tokens(i, g)
                    for i in range(BATCH):
                        col = bass.ds(SLOT_TILES * i + g, 1)
                        a = nc.vector.tensor_scalar(take[:, col], found[:, col], float(SEQ * i), None, ALU.add)
                    a.then_inc(listed, 1)
                plan(dve, body)
                scale_by_gates()

            @block.gpsimd
            def _(pool):
                def gather(tiles):
                    for t in tiles:
                        pool.indirect_dma_start(gathered[:, t, :], None, rows,
                                                bass.IndirectOffsetOnAxis(take[:, t:t + 1], 0)).then_inc(
                            tokens_gathered[t], 16)

                def scatter(e):
                    pool.wait_ge(put_ready, e + 1)
                    for t in range(XT):
                        hold(pool, y_ready, XT * e + t + 1, pool_passed)
                        pool.indirect_dma_start(out_rows, bass.IndirectOffsetOnAxis(put[:, t:t + 1], 0), y[:, t, :],
                                                None, compute_op=ALU.add).then_inc(added[t], 16)

                def body(e, first, last):
                    def group(g):
                        n = GROUPS * e + g
                        for j in range(GJ):
                            pool.wait_ge(gu_hi_done, GJ * n + j + 1)
                            nc.gpsimd.tensor_tensor(gu_lo[:, j].rearrange("p m k i -> p (m k i)"), raw[:, j, 0:GU],
                                                    gu_hi[:, j].rearrange("p m k i -> p (m k i)").bitcast(F32),
                                                    ALU.subtract).then_inc(gu_lo_done, 1)
                        if isinstance(g, int) and not first:
                            scatter(e - 1)
                        for j in range(GJ):
                            pool.wait_ge(down_hi_done, GJ * n + j + 1)
                            nc.gpsimd.tensor_tensor(down_lo[:, j, :], raw[:, j, GU:WCOLS],
                                                    down_hi[:, j, :].bitcast(F32),
                                                    ALU.subtract).then_inc(down_lo_done, 1)
                        if isinstance(g, int) and not first:
                            for t in range(XT):
                                pool.wait_ge(added[t], 16 * e)
                            pool.sem_inc(added_all, 1)
                    groups(pool, group)
                    if not last:
                        pool.wait_ge(gates_read, e + 1)
                        pool.wait_ge(x_hi_done, XT * (e + 1))
                        hold(pool, listed, GROUPS * (e + 2), pool_passed)
                        gather(range(XT))

                for g in range(GROUPS):
                    hold(pool, listed, g + 1, pool_passed)
                    gather([g, SLOT_TILES + g])
                plan(pool, body)
                scatter(EXPERTS - 1)
                for t in range(XT):
                    pool.wait_ge(added[t], 16 * EXPERTS)


def down_uses_before(uses, g):
    return uses if isinstance(g, int) else uses + XT * (g + 1)


def kernel(**inputs):
    import concourse.bacc as bacc
    from concourse.bass_utils import run_bass_kernel_spmd as run

    a = {name: np.asarray(value) for name, value in inputs.items()}

    def on_all(v):
        return np.ascontiguousarray(np.broadcast_to(v, (P,) + v.shape))

    ctx_t = a["ctx_1024"].transpose(2, 0, 1)
    lam = np.stack([a["L0_xattn_" + n] for n in ("lq1", "lk1", "lq2", "lk2")])
    gu = [a["L0_ffn_" + n].reshape(EXPERTS, INNER // P, P, KD, P).transpose(0, 1, 4, 3, 2).reshape(
        EXPERTS, INNER // P, P, DIM) for n in ("w_gate", "w_up")]
    down = a["L0_ffn_w_down"].transpose(0, 2, 1).reshape(EXPERTS, INNER // P, P, DIM)
    weights = np.concatenate(gu + [down], axis=-1).reshape(EXPERTS * GROUPS, GJ, P, WCOLS)
    arrays = {
        "x": a["x"].reshape(TOKENS, DIM),
        "ctxT": np.concatenate([ctx_t] * 3, axis=-1),
        "WqT": a["L0_xattn_Wq"].T, "WkT": a["L0_xattn_Wk"].T, "WvT": a["L0_xattn_Wv"].T,
        "WpT": a["L0_xattn_Wp"].T,
        "bias": on_all(a["L0_xattn_bp"]),
        "lam_in": on_all(lam),
        "subln": np.concatenate([a["L0_xattn_subln_w"]] * (P // V_DIM)).reshape(P, 1),
        "gate_wT": a["L0_ffn_gate_w"].T,
        "weights": weights,
        **shape_constants(),
    }
    arrays = {name: np.ascontiguousarray(v) for name, v in arrays.items()}
    feeds = {"in_" + name: v for name, v in arrays.items()}
    nc = bacc.Bacc("TRN2", target_bir_lowering=False, num_devices=1)
    io = {name: nc.dram_tensor("in_" + name, v.shape, mybir.dt.from_np(v.dtype), kind="ExternalInput").ap()
          for name, v in arrays.items()}
    io["out"] = nc.dram_tensor("out_x", (TOKENS, DIM), F32, kind="ExternalOutput").ap()
    io["rows"] = nc.dram_tensor("token_rows", (TOKENS, ROW), F32).ap()
    io["prefix"] = nc.dram_tensor("chosen_counts", (SETS * P, P), F16).ap()
    build(nc, io)
    got = run(nc, [feeds], core_ids=[0]).results[0]["out_x"]
    return got.reshape(BATCH, SEQ, DIM)
```
